# Optimizing a Trainium2 kernel written in Bass

```python
import numpy as np
import jax
import jax.numpy as jnp

def _softmax(x, axis=-1):
    return jax.nn.softmax(x, axis=axis)

def _gelu(x):
    return jax.nn.gelu(x, approximate=True)

def _silu(x):
    return jax.nn.silu(x)

def _sigmoid(x):
    return jax.nn.sigmoid(x)

def _layernorm(x, axis=-1, eps=1e-05):
    m = jnp.mean(x, axis=axis, keepdims=True)
    v = jnp.var(x, axis=axis, keepdims=True)
    return (x - m) / jnp.sqrt(v + eps)

def _scatter_add(tgt, idx, src, axis=0):
    return tgt.at[idx].add(src)

def _segment_sum(src, seg, n):
    return jax.ops.segment_sum(src, seg, n)
kernel_name = 'mk_gps_d1_gnn_r8_ab5e6f'

def setup_inputs(seed: int=0):
    np.random.seed(seed)
    _w = jnp.asarray

    def _rec_inputs():
        import jax
        import jax.numpy as jnp
        _gk = jax.random.key(seed)
        x = -7.329e-05 + 0.9999 * jax.random.normal(jax.random.fold_in(_gk, 1), (1250, 512), jnp.float32)
        src = jax.random.randint(jax.random.fold_in(_gk, 2), (40000,), 0, 1250, jnp.int32)
        dst = jax.random.randint(jax.random.fold_in(_gk, 3), (40000,), 0, 1250, jnp.int32)
        _o = jnp.argsort(dst, stable=True)
        src = src[_o]
        dst = dst[_o]
        return (x, src, dst)
    x, src, dst = _rec_inputs()

    def _L0_gnn_setup():
        import jax, jax.numpy as jnp
        import numpy as np
        N_NODES = 12500
        N_EDGES = 37500

        def _gcn_conv(x, W, b, src, dst, n):
            h = x @ W
            loop = jnp.arange(n, dtype=src.dtype)
            s = jnp.concatenate([src, loop])
            d = jnp.concatenate([dst, loop])
            deg = jax.ops.segment_sum(jnp.ones(s.shape[0], dtype=x.dtype), d, num_segments=n)
            dinv = jnp.where(deg > 0, jax.lax.rsqrt(deg), jnp.zeros_like(deg))
            norm = dinv[s] * dinv[d]
            out = jax.ops.segment_sum(h[s] * norm[:, None], d, num_segments=n)
            return out + b
        key = jax.random.key(seed)
        ks = jax.random.split(key, 10)
        x = jax.random.normal(ks[0], (N_NODES, 512), dtype=jnp.float32)
        edge_index = jax.random.randint(ks[1], (2, N_EDGES), 0, N_NODES, dtype=jnp.int32)

        def lin(k, fan_in, fan_out):
            s = 1.0 / np.sqrt(fan_in)
            return jax.random.uniform(k, (fan_in, fan_out), jnp.float32, -s, s)
        W1 = lin(ks[2], 512, 256)
        b1 = jnp.zeros((256,), jnp.float32)
        W2 = lin(ks[3], 256, 128)
        b2 = jnp.zeros((128,), jnp.float32)
        W3 = lin(ks[4], 128, 128)
        b3 = jnp.zeros((128,), jnp.float32)
        s4 = 1.0 / np.sqrt(512)
        W4 = jax.random.uniform(ks[5], (512, 512), jnp.float32, -s4, s4)
        b4 = jax.random.uniform(ks[6], (512,), jnp.float32, -s4, s4)
        return {'x': x, 'W1': W1, 'b1': b1, 'W2': W2, 'b2': b2, 'W3': W3, 'b3': b3, 'W4': W4, 'b4': b4, 'edge_index': edge_index}
    _L0_gnn_all = _L0_gnn_setup()
    _L0_gnn_in = {k: v for k, v in _L0_gnn_all.items() if k in ('W1', 'b1', 'W2', 'b2', 'W3', 'b3', 'W4', 'b4')}
    del _L0_gnn_all

    def _L0_mix_setup():
        import jax, jax.numpy as jnp
        import numpy as np
        B, T, D = (4, 1024, 512)
        H, S = (8, 16)
        HD = D // H
        PRUNE_THRESH = 0.02
        key = jax.random.key(seed)
        ks = jax.random.split(key, 8)
        base_centers = jax.random.normal(ks[0], (H, S, HD), jnp.float32) * 0.3
        center_deltas = jax.random.normal(ks[1], (H, S, HD), jnp.float32) * 0.1
        log_scales = jnp.full((H, S), -0.5, jnp.float32) + 0.1 * jax.random.normal(ks[2], (H, S), jnp.float32)
        log_amps = jnp.full((H, S), -1.0, jnp.float32) + 0.1 * jax.random.normal(ks[3], (H, S), jnp.float32)
        movement_scale_param = jnp.array([0.05], jnp.float32)
        temperature = jnp.ones((1,), jnp.float32)
        qkv_w = jax.random.normal(ks[4], (3 * D, D), jnp.float32) * (1.0 / np.sqrt(D))
        out_w = jax.random.normal(ks[5], (D, D), jnp.float32) * (1.0 / np.sqrt(D))
        x = jax.random.normal(ks[6], (B, T, D), jnp.float32)
        return {'x': x, 'base_centers': base_centers, 'center_deltas': center_deltas, 'log_scales': log_scales, 'log_amps': log_amps, 'movement_scale_param': movement_scale_param, 'temperature': temperature, 'qkv_w': qkv_w, 'out_w': out_w}
    _L0_mix_all = _L0_mix_setup()
    _L0_mix_in = {k: v for k, v in _L0_mix_all.items() if k in ('base_centers', 'center_deltas', 'log_scales', 'log_amps', 'movement_scale_param', 'temperature', 'qkv_w', 'out_w')}
    del _L0_mix_all

    def _L0_ffn_setup():
        import jax, jax.numpy as jnp
        import numpy as np
        EPS = 1e-05
        TOP_K = 2

        def layer_norm(x, g, b):
            m = x.mean(-1, keepdims=True)
            v = ((x - m) ** 2).mean(-1, keepdims=True)
            return (x - m) / jnp.sqrt(v + EPS) * g + b
        key = jax.random.key(seed)
        ks = jax.random.split(key, 8)
        B, S, D, E, H = (8, 512, 512, 8, 256)
        x = jax.random.normal(ks[0], (B, S, D), dtype=jnp.float32)
        Wg = jax.random.normal(ks[1], (D, E), dtype=jnp.float32) * 0.02
        W1 = jax.random.normal(ks[2], (E, D, H), dtype=jnp.float32) * 0.02
        b1 = jnp.zeros((E, H), dtype=jnp.float32)
        W2 = jax.random.normal(ks[3], (E, H, D), dtype=jnp.float32) * 0.02
        b2 = jnp.zeros((E, D), dtype=jnp.float32)
        ln_g = jnp.ones((D,), dtype=jnp.float32)
        ln_b = jnp.zeros((D,), dtype=jnp.float32)
        out_g = jnp.ones((D,), dtype=jnp.float32)
        out_b = jnp.zeros((D,), dtype=jnp.float32)
        return {'x': x, 'Wg': Wg, 'W1': W1, 'b1': b1, 'W2': W2, 'b2': b2, 'ln_g': ln_g, 'ln_b': ln_b, 'out_g': out_g, 'out_b': out_b}
    _L0_ffn_all = _L0_ffn_setup()
    _L0_ffn_in = {k: v for k, v in _L0_ffn_all.items() if k in ('Wg', 'W1', 'b1', 'W2', 'b2', 'ln_g', 'ln_b', 'out_g', 'out_b')}
    del _L0_ffn_all
    return {'x': x, 'src': src, 'dst': dst, 'L0_gnn_W1': _L0_gnn_in['W1'], 'L0_gnn_b1': _L0_gnn_in['b1'], 'L0_gnn_W2': _L0_gnn_in['W2'], 'L0_gnn_b2': _L0_gnn_in['b2'], 'L0_gnn_W3': _L0_gnn_in['W3'], 'L0_gnn_b3': _L0_gnn_in['b3'], 'L0_gnn_W4': _L0_gnn_in['W4'], 'L0_gnn_b4': _L0_gnn_in['b4'], 'L0_mix_base_centers': _L0_mix_in['base_centers'], 'L0_mix_center_deltas': _L0_mix_in['center_deltas'], 'L0_mix_log_scales': _L0_mix_in['log_scales'], 'L0_mix_log_amps': _L0_mix_in['log_amps'], 'L0_mix_movement_scale_param': _L0_mix_in['movement_scale_param'], 'L0_mix_temperature': _L0_mix_in['temperature'], 'L0_mix_qkv_w': _L0_mix_in['qkv_w'], 'L0_mix_out_w': _L0_mix_in['out_w'], 'L0_ffn_Wg': _L0_ffn_in['Wg'], 'L0_ffn_W1': _L0_ffn_in['W1'], 'L0_ffn_b1': _L0_ffn_in['b1'], 'L0_ffn_W2': _L0_ffn_in['W2'], 'L0_ffn_b2': _L0_ffn_in['b2'], 'L0_ffn_ln_g': _L0_ffn_in['ln_g'], 'L0_ffn_ln_b': _L0_ffn_in['ln_b'], 'L0_ffn_out_g': _L0_ffn_in['out_g'], 'L0_ffn_out_b': _L0_ffn_in['out_b']}

def reference(x, src, dst, L0_gnn_W1, L0_gnn_b1, L0_gnn_W2, L0_gnn_b2, L0_gnn_W3, L0_gnn_b3, L0_gnn_W4, L0_gnn_b4, L0_mix_base_centers, L0_mix_center_deltas, L0_mix_log_scales, L0_mix_log_amps, L0_mix_movement_scale_param, L0_mix_temperature, L0_mix_qkv_w, L0_mix_out_w, L0_ffn_Wg, L0_ffn_W1, L0_ffn_b1, L0_ffn_W2, L0_ffn_b2, L0_ffn_ln_g, L0_ffn_ln_b, L0_ffn_out_g, L0_ffn_out_b):
    import jax
    import jax.numpy as jnp

    def _L0_gnn_ref(x, W1, b1, W2, b2, W3, b3, W4, b4, edge_index):
        import jax, jax.numpy as jnp
        import numpy as np
        N_NODES = 12500
        N_EDGES = 37500

        def _gcn_conv(x, W, b, src, dst, n):
            h = x @ W
            loop = jnp.arange(n, dtype=src.dtype)
            s = jnp.concatenate([src, loop])
            d = jnp.concatenate([dst, loop])
            deg = jax.ops.segment_sum(jnp.ones(s.shape[0], dtype=x.dtype), d, num_segments=n)
            dinv = jnp.where(deg > 0, jax.lax.rsqrt(deg), jnp.zeros_like(deg))
            norm = dinv[s] * dinv[d]
            out = jax.ops.segment_sum(h[s] * norm[:, None], d, num_segments=n)
            return out + b
        n = x.shape[0]
        src, dst = (edge_index[0], edge_index[1])
        x1 = jax.nn.relu(_gcn_conv(x, W1, b1, src, dst, n))
        x2 = jax.nn.relu(_gcn_conv(x1, W2, b2, src, dst, n))
        x3 = jax.nn.relu(_gcn_conv(x2, W3, b3, src, dst, n))
        xc = jnp.concatenate([x1, x2, x3], axis=1)
        return xc @ W4.T + b4

    def _L0_mix_ref(x, base_centers, center_deltas, log_scales, log_amps, movement_scale_param, temperature, qkv_w, out_w):
        import jax, jax.numpy as jnp
        import numpy as np
        B, T, D = (4, 1024, 512)
        H, S = (8, 16)
        HD = D // H
        PRUNE_THRESH = 0.02
        b, t, d = x.shape
        h, s, hd = base_centers.shape
        qkv = (x @ qkv_w.T).reshape(b, t, 3, h, hd)
        q, k, v = (qkv[:, :, 0], qkv[:, :, 1], qkv[:, :, 2])
        ms = jax.nn.sigmoid(movement_scale_param[0]) * 0.1
        centers = base_centers + center_deltas * ms
        scales = jnp.clip(jnp.exp(log_scales), 0.0001, 2.0)
        amps = jnp.exp(log_amps)
        eff_amps = amps * (amps > PRUNE_THRESH).astype(amps.dtype)
        inv_var = 0.5 / (scales ** 2 + 1e-08)
        c_sq = jnp.sum(centers ** 2, -1)

        def splat_weights(tok):
            d2 = jnp.sum(tok ** 2, -1)[..., None] + c_sq[None, None] - 2.0 * jnp.einsum('bthd,hsd->bths', tok, centers)
            return jnp.exp(-d2 * inv_var[None, None]) * eff_amps[None, None]
        qw = splat_weights(q)
        kw = splat_weights(k)
        temp = jnp.maximum(temperature[0], 0.1)
        logits = jnp.einsum('bihs,bjhs->bijh', qw, kw) / temp
        attn = jax.nn.softmax(logits, axis=2)
        out = jnp.einsum('bijh,bjhd->bihd', attn, v).reshape(b, t, d)
        return out @ out_w.T

    def _L0_ffn_ref(x, Wg, W1, b1, W2, b2, ln_g, ln_b, out_g, out_b):
        import jax, jax.numpy as jnp
        import numpy as np
        EPS = 1e-05
        TOP_K = 2

        def layer_norm(x, g, b):
            m = x.mean(-1, keepdims=True)
            v = ((x - m) ** 2).mean(-1, keepdims=True)
            return (x - m) / jnp.sqrt(v + EPS) * g + b
        xn = layer_norm(x, ln_g, ln_b)
        logits = jnp.einsum('bsd,de->bse', xn, Wg)
        probs = jax.nn.softmax(logits, axis=-1)
        top_p, top_i = jax.lax.top_k(probs, TOP_K)
        conf = top_p / top_p.sum(-1, keepdims=True)
        h = jax.nn.gelu(jnp.einsum('bsd,edh->bseh', xn, W1) + b1)
        o = jnp.einsum('bseh,ehd->bsed', h, W2) + b2
        sel = jnp.take_along_axis(o, top_i[..., None], axis=2)
        combined = jnp.einsum('bskd,bsk->bsd', sel, conf)
        return layer_norm(x + combined, out_g, out_b)
    edge_index = jnp.stack([src, dst])
    xn = _layernorm(x, axis=-1)
    x = x + _L0_gnn_ref(xn, L0_gnn_W1, L0_gnn_b1, L0_gnn_W2, L0_gnn_b2, L0_gnn_W3, L0_gnn_b3, L0_gnn_W4, L0_gnn_b4, edge_index) + _L0_mix_ref(xn[None], L0_mix_base_centers, L0_mix_center_deltas, L0_mix_log_scales, L0_mix_log_amps, L0_mix_movement_scale_param, L0_mix_temperature, L0_mix_qkv_w, L0_mix_out_w)[0]
    x = x + _L0_ffn_ref(_layernorm(x, axis=-1)[None], L0_ffn_Wg, L0_ffn_W1, L0_ffn_b1, L0_ffn_W2, L0_ffn_b2, L0_ffn_ln_g, L0_ffn_ln_b, L0_ffn_out_g, L0_ffn_out_b)[0]
    return x

_drawn_inputs = setup_inputs


def setup_inputs(seed=0):
    import zlib

    import numpy as np

    out = dict(_drawn_inputs(seed))
    spreads = {'L0_gnn_b1': (0.0, 0.297),
     'L0_gnn_b2': (0.0, 0.346),
     'L0_gnn_b3': (0.0, 0.368),
     'L0_ffn_b1': (0.0, 0.8),
     'L0_ffn_b2': (0.0, 0.1),
     'L0_ffn_ln_g': (1.0, 0.6),
     'L0_ffn_ln_b': (0.0, 0.501),
     'L0_ffn_out_g': (1.0, 0.2),
     'L0_ffn_out_b': (0.0, 0.1)}
    factors = {'L0_gnn_W2': 5.609, 'L0_gnn_W3': 5.787}
    for name, (base, spread) in spreads.items():
        noise = np.random.default_rng([zlib.crc32(name.encode()), seed]).standard_normal(out[name].shape)
        drawn = base * np.exp(spread * noise) if base else spread * noise
        out[name] = jnp.asarray(drawn.astype(out[name].dtype))
    for name, factor in factors.items():
        out[name] = (out[name] * factor).astype(out[name].dtype)
    return out
```

```python
from contextlib import ExitStack
import concourse.bass as bass
from concourse import mybir
ALU = mybir.AluOpType
ACT = mybir.ActivationFunctionType
AX = mybir.AxisListType
F32 = mybir.dt.float32
F32R = mybir.dt.float32r
F16 = mybir.dt.float16
I32 = mybir.dt.int32

R = 125
QUAD = 4


def tools(nc, ctx, phase):
    def sb(name, shape, dtype=F32):
        return ctx.enter_context(nc.sbuf_tensor(f"{phase}_{name}", shape, dtype))

    def banks(name, count):
        return ctx.enter_context(nc.psum_tensor(f"{phase}_{name}", [128, count, 512], F32))

    def sem(name):
        return ctx.enter_context(nc.semaphore(f"{phase}_{name}"))
    return sb, banks, sem


def adjacency(nc, src, dst, ident, zero_hot, adj, dinv):
    n_nodes = adj.shape[2]
    tiles = n_nodes // R
    groups = src.shape[0] // (QUAD * R)
    half_nodes = 250
    with ExitStack() as ctx:
        sb, banks, sem = tools(nc, ctx, "adjacency")
        src_i = sb("src_i", [groups, QUAD * R], I32)
        dst_i = sb("dst_i", [groups, QUAD * R], I32)
        src_f = sb("src_f", [groups, QUAD * R])
        dst_f = sb("dst_f", [groups, QUAD * R])
        src_col = sb("src_col", [R, (QUAD + 1) * groups])
        dst_col = sb("dst_col", [R, (QUAD + 1) * groups])
        node_row = sb("node_row", [R, n_nodes], F16)
        block_row = sb("block_row", [groups, tiles])
        group_col = sb("group_col", [groups, 1])
        low = sb("low", [groups, 1])
        low_end = sb("low_end", [groups, 1])
        high = sb("high", [groups, 1])
        begins = sb("begins", [groups, tiles])
        touches = sb("touches", [groups, tiles])
        first_less = sb("first_less", [groups, 1])
        last_less = sb("last_less", [groups, 1])
        candidates = sb("candidates", [groups, 2 * tiles])
        extreme = sb("extreme", [2 * tiles, 1])
        bounds_f = sb("bounds_f", [1, 2 * tiles])
        span_f = sb("span_f", [1, 2 * tiles])
        span_end = sb("span_end", [1, tiles])
        bounds = sb("bounds", [1, 2 * tiles], I32)
        src_hot = sb("src_hot", [R, QUAD, n_nodes], F16)
        dst_hot = sb("dst_hot", [R, QUAD, R], F16)
        rows = sb("rows", [R, 3, n_nodes])
        degree = sb("degree", [R, tiles])
        root = sb("root", [R, tiles])
        ps = banks("ps", 8)

        def count_rows(b):
            first = 3 * (b % 2)
            return ps[0:R, first:first + 3, :].rearrange("p a (c n) -> p (a c) n", n=256)[:, 0:5, 0:half_nodes]

        edges_in = sem("edges_in")
        iotas = sem("iotas")
        edge_f = sem("edge_f")
        edge_turned = sem("edge_turned")
        edge_cols = sem("edge_cols")
        range_step = sem("range_step")
        cand_ready = sem("cand_ready")
        cand_turned = sem("cand_turned")
        extreme_ready = sem("extreme_ready")
        extreme_turned = sem("extreme_turned")
        bounds_ready = sem("bounds_ready")
        hot_ready = sem("hot_ready")
        hot_free = sem("hot_free")
        counted = sem("counted")
        counts_out = sem("counts_out")
        loops_in = sem("loops_in")
        root_ready = sem("root_ready")
        dinv_ready = sem("dinv_ready")
        rows_scaled = sem("rows_scaled")
        block_turned = sem("block_turned")
        block_out = sem("block_out")
        block = ctx.enter_context(nc.Block())
        turn_groups = [(0, 4), (4, 8), (8, tiles)]

        @block.sync
        def _(sp):
            sp.dma_start(src_i[:, :], src.rearrange("(g e) -> g e", e=QUAD * R)).then_inc(edges_in, 16)
            sp.dma_start(dst_i[:, :], dst.rearrange("(g e) -> g e", e=QUAD * R)).then_inc(edges_in, 16)

        @block.gpsimd
        def _(pool):
            nc.gpsimd.iota(node_row[:, :], [[1, n_nodes]], base=0, channel_multiplier=0,
                           allow_small_or_imprecise_dtypes=True).then_inc(iotas, 1)
            nc.gpsimd.iota(block_row[:, :], [[R, tiles]], base=0, channel_multiplier=0,
                           allow_small_or_imprecise_dtypes=True).then_inc(iotas, 1)
            nc.gpsimd.iota(group_col[:, :], [[1, 1]], base=0, channel_multiplier=1,
                           allow_small_or_imprecise_dtypes=True).then_inc(iotas, 1)
            for b in range(tiles):
                own = rows[:, b % 3, b * R:(b + 1) * R]
                pool.wait_ge(counts_out, b + 1)
                nc.gpsimd.tensor_tensor(own, own, ident[0:R, 0:R], ALU.add).then_inc(loops_in, 1)
                pool.wait_ge(loops_in, b + 1)
                pool.wait_ge(dinv_ready, b + 1)
                nc.gpsimd.tensor_scalar(rows[:, b % 3, :], rows[:, b % 3, :], dinv[:, b:b + 1], None,
                                        ALU.mult).then_inc(rows_scaled, 1)

        @block.vector
        def _(dve):
            dve.wait_ge(edges_in, 32)
            nc.vector.tensor_copy(src_f[:, :], src_i[:, :]).then_inc(edge_f, 1)
            nc.vector.tensor_copy(dst_f[:, :], dst_i[:, :]).then_inc(edge_f, 1)
            dve.wait_ge(edge_f, 2)
            nc.vector.tensor_reduce(low[:, :], dst_f[:, :], AX.X, ALU.min).then_inc(range_step, 1)
            nc.vector.tensor_reduce(high[:, :], dst_f[:, :], AX.X, ALU.max).then_inc(range_step, 1)
            dve.wait_ge(iotas, 3)
            nc.vector.tensor_scalar(first_less[:, :], group_col[:, :], -float(groups), None, ALU.add).then_inc(range_step, 1)
            nc.vector.tensor_scalar(last_less[:, :], group_col[:, :], -1.0, -1.0, ALU.mult, ALU.add).then_inc(range_step, 1)
            dve.wait_ge(range_step, 4)
            nc.vector.tensor_scalar(low_end[:, :], low[:, :], -float(R - 1), None, ALU.add).then_inc(range_step, 1)
            dve.wait_ge(range_step, 5)
            nc.vector.tensor_scalar(begins[:, :], block_row[:, :], low_end[:, 0:1], None, ALU.is_ge).then_inc(range_step, 1)
            nc.vector.tensor_scalar(touches[:, :], block_row[:, :], high[:, 0:1], None, ALU.is_le).then_inc(range_step, 1)
            dve.wait_ge(range_step, 7)
            nc.vector.scalar_tensor_tensor(out=candidates[:, 0:tiles], in0=begins[:, :], scalar=first_less[:, 0:1],
                                           in1=touches[:, :], op0=ALU.mult, op1=ALU.mult).then_inc(cand_ready, 1)
            nc.vector.scalar_tensor_tensor(out=candidates[:, tiles:2 * tiles], in0=begins[:, :], scalar=last_less[:, 0:1],
                                           in1=touches[:, :], op0=ALU.mult, op1=ALU.mult).then_inc(cand_ready, 1)
            dve.wait_ge(cand_turned, 1)
            nc.vector.tensor_reduce(extreme[:, :], ps[0:2 * tiles, 0, 0:groups], AX.X, ALU.min).then_inc(extreme_ready, 1)
            dve.wait_ge(extreme_turned, 1)
            nc.vector.tensor_scalar(bounds_f[:, 0:tiles], ps[0:1, 1, 0:tiles], float(groups), float(groups - 1),
                                    ALU.add, ALU.min).then_inc(range_step, 1)
            nc.vector.tensor_scalar(span_end[:, :], ps[0:1, 1, tiles:2 * tiles], -1.0, None, ALU.mult).then_inc(range_step, 1)
            dve.wait_ge(range_step, 9)
            nc.vector.tensor_tensor(span_f[:, 0:tiles], span_end[:, :], bounds_f[:, 0:tiles], ALU.subtract).then_inc(range_step, 1)
            dve.wait_ge(range_step, 10)
            nc.vector.tensor_scalar(bounds_f[:, tiles:2 * tiles], span_f[:, 0:tiles], 1.0, None, ALU.max).then_inc(range_step, 1)
            dve.wait_ge(range_step, 11)
            nc.vector.tensor_copy(bounds[:, :], bounds_f[:, :]).then_inc(bounds_ready, 1)
            for n, col in enumerate((src_col, dst_col)):
                dve.wait_ge(edge_turned, n + 1)
                nc.vector.tensor_copy(col[:, 0:QUAD * groups], ps[0:R, 2 + n, 0:QUAD * groups]).then_inc(edge_cols, 1)
            dve.wait_ge(edge_cols, 2)
            dve.wait_ge(bounds_ready, 1)
            visits = 0
            for b in range(tiles):
                start = dve.value_load(bounds[0:1, b:b + 1], min_val=0, max_val=groups - 1)
                span = dve.value_load(bounds[0:1, tiles + b:tiles + b + 1], min_val=1, max_val=groups)
                with dve.Fori(0, span) as k:
                    group = dve.snap(start + k)
                    for half in range(2):
                        dve.wait_ge(hot_free, (k + visits) * 2 + half + 1)
                        for q in (2 * half, 2 * half + 1):
                            edge = group + q * groups
                            nc.vector.tensor_scalar(src_hot[:, q, :], node_row[:, :], src_col[:, bass.ds(edge, 1)],
                                                    None, ALU.is_equal)
                            last = nc.vector.tensor_scalar(dst_hot[:, q, :], node_row[:, b * R:(b + 1) * R],
                                                           dst_col[:, bass.ds(edge, 1)], None, ALU.is_equal)
                        last.then_inc(hot_ready, 1)
                visits = dve.snap(span + visits)
                if b >= 1:
                    dve.wait_ge(root_ready, b)
                    nc.vector.reciprocal(dinv[:, b - 1:b], root[:, b - 1:b]).then_inc(dinv_ready, 1)
            dve.wait_ge(root_ready, tiles)
            nc.vector.reciprocal(dinv[:, tiles - 1:tiles], root[:, tiles - 1:tiles]).then_inc(dinv_ready, 1)

        @block.scalar
        def _(act):
            def blocks_out(b):
                for n, (t0, t1) in enumerate(turn_groups):
                    act.wait_ge(block_turned, 3 * b + n + 1)
                    nc.scalar.copy(adj[:, t0:t1, b * R:(b + 1) * R],
                                   ps[0:R, 6 + (b + n) % 2, 0:(t1 - t0) * R].rearrange("p (t n) -> p t n", n=R)).then_inc(block_out, 1)

            for b in range(tiles):
                if b >= 2:
                    blocks_out(b - 2)
                act.wait_ge(counted, b + 1)
                if b >= 3:
                    act.wait_ge(block_turned, 3 * (b - 2))
                nc.scalar.activation(rows[:, b % 3, :].rearrange("p (c n) -> p c n", n=half_nodes), count_rows(b),
                                     ACT.Identity, accum_out=degree[:, b:b + 1]).then_inc(counts_out, 1)
                act.wait_ge(counts_out, b + 1)
                nc.scalar.activation(root[:, b:b + 1], degree[:, b:b + 1], ACT.Sqrt, bias=1.0).then_inc(root_ready, 1)
            blocks_out(tiles - 2)
            blocks_out(tiles - 1)

        @block.tensor
        def _(pe):
            pe.wait_ge(edge_f, 2)
            for n, edges in enumerate((src_f, dst_f)):
                for q in range(QUAD):
                    last = nc.tensor.transpose(ps[0:R, 2 + n, q * groups:(q + 1) * groups], edges[:, q * R:(q + 1) * R],
                                               ident[0:groups, 0:groups])
                last.then_inc(edge_turned, 1)
            pe.wait_ge(cand_ready, 2)
            nc.tensor.transpose(ps[0:2 * tiles, 0, 0:groups], candidates[:, :], ident[0:groups, 0:groups]).then_inc(cand_turned, 1)
            pe.wait_ge(extreme_ready, 1)
            nc.tensor.transpose(ps[0:1, 1, 0:2 * tiles], extreme[:, :], ident[0:2 * tiles, 0:2 * tiles]).then_inc(extreme_turned, 1)
            pe.wait_ge(bounds_ready, 1)
            pe.wait_ge(edge_cols, 2)
            pe.sem_inc(hot_free, 2)

            def turn(b):
                pe.wait_ge(rows_scaled, b + 1)
                for n, (t0, t1) in enumerate(turn_groups):
                    g = 3 * b + n
                    if g >= 2:
                        pe.wait_ge(block_out, g - 1)
                    for t in range(t0, t1):
                        last = nc.tensor.transpose(ps[0:R, 6 + (b + n) % 2, (t - t0) * R:(t - t0 + 1) * R],
                                                   rows[:, b % 3, t * R:(t + 1) * R], ident[0:R, 0:R])
                    last.then_inc(block_turned, 1)

            visits = 0
            for b in range(tiles):
                if b >= 2:
                    pe.wait_ge(counts_out, b - 1)
                    turn(b - 2)
                span = pe.value_load(bounds[0:1, tiles + b:tiles + b + 1], min_val=1, max_val=groups)
                first = 3 * (b % 2)
                for c in range(3):
                    nc.tensor.matmul(ps[0:R, first + c, 0:(512 if c < 2 else 256)], zero_hot[:, 0:R], zero_hot[:, 0:(512 if c < 2 else 256)], start=True, stop=False,
                                     skip_group_check=True)
                with pe.Fori(0, span) as k:
                    for half in range(2):
                        pe.wait_ge(hot_ready, (k + visits) * 2 + half + 1)
                        for q in (2 * half, 2 * half + 1):
                            for c in range(5):
                                last = nc.tensor.matmul(count_rows(b)[:, c, :], dst_hot[:, q, :],
                                                        src_hot[:, q, c * half_nodes:(c + 1) * half_nodes],
                                                        start=False, stop=False, skip_group_check=True)
                        last.then_inc(hot_free, 1)
                visits = pe.snap(span + visits)
                nc.tensor.matmul(ps[0:R, first, 0:256], zero_hot[:, 0:R], zero_hot[:, 0:256], start=False, stop=True,
                                 skip_group_check=True).then_inc(counted, 1)
            turn(tiles - 2)
            turn(tiles - 1)

def turn_normalised(nc, name, x_tiles, ident, turned_hi, turned_lo, eps, gain=None, offset=None):
    tiles = x_tiles.shape[1]
    width = x_tiles.shape[2]
    blocks = width // 128
    with ExitStack() as ctx:
        sb, banks, sem = tools(nc, ctx, name)
        stats = sb("stats", [R, 2, 6])
        moments = sb("moments", [R, tiles, 2])
        root = sb("root", [R, tiles])
        scale = sb("scale", [R, tiles])
        eps_col = sb("eps_col", [R, 1])
        unit = sb("unit", [R, 2, width])
        affine = sb("affine", [128, 2, blocks * R])
        gains = sb("gains", [128, 2, blocks])
        ps = banks("ps", 2)
        eps_in = sem("eps_in")
        stats_ready = sem("stats_ready")
        moments_ready = sem("moments_ready")
        root_ready = sem("root_ready")
        scale_ready = sem("scale_ready")
        unit_ready = sem("unit_ready")
        turned = sem("turned")
        hi_ready = sem("hi_ready")
        lo_ready = sem("lo_ready")
        gains_in = sem("gains_in")
        affine_ready = sem("affine_ready")
        block = ctx.enter_context(nc.Block())

        def turned_view(n):
            return ps[:, n % 2, 0:blocks * R].rearrange("p (k n) -> p k n", n=R)

        @block.sync
        def _(sp):
            for n, row in enumerate((gain, offset)):
                if row is not None:
                    sp.dma_start(gains[:, n, :], row.rearrange("(k p) -> p k", p=128),
                                 allow_slow_non_contiguous=True).then_inc(gains_in, 16)

        @block.gpsimd
        def _(pool):
            nc.gpsimd.memset(eps_col[:, :], eps).then_inc(eps_in, 1)

        @block.vector
        def _(dve):
            for t in range(tiles):
                if t >= 2:
                    dve.wait_ge(moments_ready, t - 1)
                nc.vector.bn_stats(stats[:, t % 2, :], x_tiles[:, t, :]).then_inc(stats_ready, 1)
                dve.wait_ge(stats_ready, t + 1)
                nc.vector.bn_aggr(moments[:, t, :], stats[:, t % 2, :]).then_inc(moments_ready, 1)
            dve.wait_ge(root_ready, 1)
            nc.vector.reciprocal(scale[:, :], root[:, :]).then_inc(scale_ready, 1)
            dve.wait_ge(scale_ready, 1)
            for t in range(tiles + 1):
                if t < tiles:
                    if t >= 2:
                        dve.wait_ge(turned, t - 1)
                    nc.vector.tensor_scalar(unit[:, t % 2, :], x_tiles[:, t, :], moments[:, t, 0:1], scale[:, t:t + 1],
                                            ALU.subtract, ALU.mult).then_inc(unit_ready, 1)
                if t >= 1:
                    n = t - 1
                    at = slice(n * R, (n + 1) * R)
                    dve.wait_ge(hi_ready, n + 1)
                    whole = turned_view(n) if gain is None else affine[:, n % 2, :].rearrange("p (k n) -> p k n", n=R)
                    nc.vector.tensor_tensor(turned_lo[:, :, at], whole, turned_hi[:, :, at].bitcast(F32),
                                            ALU.subtract).then_inc(lo_ready, 1)

        @block.scalar
        def _(act):
            act.wait_ge(moments_ready, tiles)
            act.wait_ge(eps_in, 1)
            nc.scalar.activation(root[:, :], moments[:, :, 1], ACT.Sqrt, bias=eps_col[:, 0:1]).then_inc(root_ready, 1)
            for t in range(tiles):
                act.wait_ge(turned, t + 1)
                whole = turned_view(t)
                if gain is not None:
                    act.wait_ge(gains_in, 32)
                    if t >= 2:
                        act.wait_ge(lo_ready, t - 1)
                    whole = affine[:, t % 2, :].rearrange("p (k n) -> p k n", n=R)
                    for k in range(blocks):
                        last = nc.scalar.activation(whole[:, k, :], turned_view(t)[:, k, :], ACT.Identity,
                                                    scale=gains[:, 0, k:k + 1], bias=gains[:, 1, k:k + 1])
                    last.then_inc(affine_ready, 1)
                    act.wait_ge(affine_ready, t + 1)
                nc.scalar.copy(turned_hi[:, :, t * R:(t + 1) * R], whole).then_inc(hi_ready, 1)

        @block.tensor
        def _(pe):
            for t in range(tiles):
                pe.wait_ge(unit_ready, t + 1)
                if t >= 2:
                    pe.wait_ge(lo_ready, t - 1)
                for k in range(blocks):
                    last = nc.tensor.transpose(turned_view(t)[:, k, :], unit[:, t % 2, k * 128:(k + 1) * 128],
                                               ident[0:R, 0:R])
                last.then_inc(turned, 1)


def spans(width, step):
    return [(a, min(a + step, width)) for a in range(0, width, step)]


def graph_layers(nc, turned_hi, turned_lo, adj, dinv, weights, biases, kept):
    n_nodes = adj.shape[2]
    tiles = n_nodes // R
    chunks = spans(n_nodes, 500)
    sizes = [tuple(w.shape) for w in weights]
    with ExitStack() as ctx:
        sb, banks, sem = tools(nc, ctx, "graph")
        w1 = sb("w1", [128, sizes[0][0] // 128, sizes[0][1]])
        w1_hi = sb("w1_hi", [128, sizes[0][0] // 128, sizes[0][1]], F32R)
        w1_lo = sb("w1_lo", [128, sizes[0][0] // 128, sizes[0][1]], F32R)
        w2 = sb("w2", [128, sizes[1][0] // 128, sizes[1][1]])
        w3 = sb("w3", [128, sizes[2][0] // 128, sizes[2][1]])
        bias = sb("bias", [128, 4])
        projected = sb("projected", [R, tiles, sizes[0][1]])
        ps = banks("ps", 8)
        w1_in = sem("w1_in")
        w_in = sem("w_in")
        w1_part = sem("w1_part")
        rows_done = sem("rows_done")
        rows_out = sem("rows_out")
        gathered = sem("gathered")
        kept_ready = sem("kept_ready")
        block = ctx.enter_context(nc.Block())
        layers = [(None, 4, None, 2, 0), (w2, 2, 0, 1, 2), (w3, 1, 2, 1, 3)]

        @block.sync
        def _(sp):
            sp.dma_start(w1[:, :, :], weights[0].rearrange("(k p) n -> p k n", p=128)).then_inc(w1_in, 16)
            sp.dma_start(w2[:, :, :], weights[1].rearrange("(k p) n -> p k n", p=128)).then_inc(w_in, 16)
            sp.dma_start(w3[:, :, :], weights[2].rearrange("(k p) n -> p k n", p=128)).then_inc(w_in, 16)
            at = 0
            for b in biases:
                m = b.shape[0] // 128
                sp.dma_start(bias[:, at:at + m], b.rearrange("(m p) -> p m", p=128),
                             allow_slow_non_contiguous=True).then_inc(w_in, 16)
                at += m

        @block.vector
        def _(dve):
            dve.wait_ge(w1_in, 16)
            nc.vector.tensor_copy(w1_hi[:, :, :], w1[:, :, :]).then_inc(w1_part, 1)
            dve.wait_ge(w1_part, 1)
            nc.vector.tensor_tensor(w1_lo[:, :, :], w1[:, :, :], w1_hi[:, :, :].bitcast(F32), ALU.subtract).then_inc(w1_part, 1)
            done = 0
            for n in range(3):
                wide = sizes[n][1]
                for t in range(tiles):
                    dve.wait_ge(rows_done, done + 1)
                    if n and t == 0:
                        dve.wait_ge(gathered, (2, 3)[n - 1])
                    nc.vector.tensor_scalar(projected[:, t, 0:wide], ps[0:R, 6 + t % 2, 0:wide], dinv[:, t:t + 1], None,
                                            ALU.mult).then_inc(rows_out, 1)
                    done += 1

        @block.scalar
        def _(act):
            act.wait_ge(w_in, 16 * 5)
            done = 0
            for n in range(3):
                _, _, _, out_blocks, first = layers[n]
                for m in range(out_blocks):
                    act.wait_ge(gathered, done + 1)
                    for c, (a, b) in enumerate(chunks):
                        nc.scalar.activation(kept[:, first + m, a:b], ps[:, 3 * (done % 2) + c, 0:b - a], ACT.Relu,
                                             bias=bias[:, first + m:first + m + 1]).then_inc(kept_ready, 1)
                    done += 1

        @block.tensor
        def _(pe):
            pe.wait_ge(w1_part, 2)
            pe.wait_ge(w_in, 16 * 5)
            rows = 0
            done = 0
            for n in range(3):
                w, depth, source, out_blocks, first = layers[n]
                wide = sizes[n][1]
                if n:
                    pe.wait_ge(kept_ready, len(chunks) * done)
                for t in range(tiles):
                    if rows >= 2:
                        pe.wait_ge(rows_out, rows - 1)
                    to = ps[0:R, 6 + t % 2, 0:wide]
                    at = slice(t * R, (t + 1) * R)
                    for k in range(depth):
                        if n:
                            last = nc.tensor.matmul(to, kept[:, source + k, at], w[:, k, :],
                                                    start=(k == 0), stop=(k == depth - 1))
                        else:
                            nc.tensor.matmul(to, turned_hi[:, k, at], w1_hi[:, k, :], start=(k == 0), stop=False)
                            nc.tensor.matmul(to, turned_hi[:, k, at], w1_lo[:, k, :], start=False, stop=False)
                            last = nc.tensor.matmul(to, turned_lo[:, k, at], w1_hi[:, k, :],
                                                    start=False, stop=(k == depth - 1))
                    last.then_inc(rows_done, 1)
                    rows += 1
                for m in range(out_blocks):
                    if done >= 2:
                        pe.wait_ge(kept_ready, len(chunks) * (done - 1))
                    for t in range(tiles):
                        if m == 0:
                            pe.wait_ge(rows_out, rows - tiles + t + 1)
                        for c, (a, b) in enumerate(chunks):
                            last = nc.tensor.matmul(ps[:, 3 * (done % 2) + c, 0:b - a], projected[:, t, m * 128:(m + 1) * 128],
                                                    adj[:, t, a:b], start=(t == 0), stop=(t == tiles - 1))
                    last.then_inc(gathered, 1)
                    done += 1

PAIR = 128
CODES = 64


def splat_constants(nc, a, ident, center_hi, center_lo, columns, part_mask, head_sum, inv_temp):
    heads, splats, depth = a["base_centers"].shape
    pairs = heads // 2
    with ExitStack() as ctx:
        sb, banks, sem = tools(nc, ctx, "splats")
        base = sb("base", [128, pairs, 128])
        delta = sb("delta", [128, pairs, 128])
        log_scale = sb("log_scale", [128, pairs])
        log_amp = sb("log_amp", [128, pairs])
        move = sb("move", [128, 1])
        move_exp = sb("move_exp", [128, 1])
        move_one = sb("move_one", [128, 1])
        move_rec = sb("move_rec", [128, 1])
        move_by = sb("move_by", [128, 1])
        temp = sb("temp", [R, 1])
        temp_max = sb("temp_max", [R, 1])
        centers = sb("centers", [128, pairs, 128])
        squares = sb("squares", [128, pairs, 128])
        center_sq = sb("center_sq", [128, pairs])
        scales = sb("scales", [128, pairs])
        clipped = sb("clipped", [128, pairs])
        scale_sq = sb("scale_sq", [128, pairs])
        var_eps = sb("var_eps", [128, pairs])
        inv_var = sb("inv_var", [128, pairs])
        amps = sb("amps", [128, pairs])
        kept_amp = sb("kept_amp", [128, pairs])
        mask_rows = sb("mask_rows", [1, 3, 128])
        keep_rows = sb("keep_rows", [128, 1])
        center_f = sb("center_f", [128, pairs, 128])
        ps = banks("ps", 2)
        cleared = sem("cleared")
        loaded = sem("loaded")
        exps = sem("exps")
        step = sem("step")
        centers_ready = sem("centers_ready")
        centers_turned = sem("centers_turned")
        masks_turned = sem("masks_turned")
        halved = sem("halved")
        block = ctx.enter_context(nc.Block())

        @block.gpsimd
        def _(pool):
            for tile in (base, delta):
                nc.gpsimd.memset(tile[:, :, :], 0.0)
            nc.gpsimd.memset(log_scale[:, :], 0.0)
            nc.gpsimd.memset(log_amp[:, :], 0.0)
            nc.gpsimd.memset(mask_rows[:, :, :], 0.0)
            nc.gpsimd.memset(head_sum[:, :].bitcast(F32), 0.0).then_inc(cleared, 1)
            pool.wait_ge(cleared, 1)
            for h in range(2):
                at = CODES * h
                nc.gpsimd.memset(mask_rows[:, 0, at + splats:at + 2 * splats], 1.0)
                nc.gpsimd.memset(mask_rows[:, 1, at + 2 * splats:at + 3 * splats], 1.0)
                nc.gpsimd.memset(mask_rows[:, 2, at:at + 3 * splats], 1.0)
                last = nc.gpsimd.memset(head_sum[depth * h:depth * (h + 1), at:at + 3 * splats].bitcast(F32), 1.0)
            last.then_inc(cleared, 1)

        @block.sync
        def _(sp):
            sp.wait_ge(cleared, 1)
            for h in range(2):
                for r in range(3):
                    rows = slice(CODES * h + splats * r, CODES * h + splats * (r + 1))
                    own = slice(depth * h, depth * (h + 1))
                    for to, name in ((base, "base_centers"), (delta, "center_deltas")):
                        sp.dma_start(to[rows, :, own], a[name].rearrange("(p h) s d -> h s p d", h=2)[h]).then_inc(loaded, 16)
                    for to, name in ((log_scale, "log_scales"), (log_amp, "log_amps")):
                        sp.dma_start(to[rows, :], a[name].rearrange("(p h) s -> h s p", h=2)[h],
                                     allow_slow_non_contiguous=True).then_inc(loaded, 16)
            sp.dma_start(move[:, :], a["movement_scale_param"].partition_broadcast(128)).then_inc(loaded, 16)
            sp.dma_start(temp[:, :], a["temperature"].partition_broadcast(R)).then_inc(loaded, 16)

        @block.scalar
        def _(act):
            act.wait_ge(loaded, 16 * 26)
            nc.scalar.activation(move_exp[:, :], move[:, :], ACT.Exp, scale=-1.0).then_inc(exps, 1)
            nc.scalar.activation(scales[:, :], log_scale[:, :], ACT.Exp).then_inc(exps, 1)
            nc.scalar.activation(amps[:, :], log_amp[:, :], ACT.Exp).then_inc(exps, 1)
            act.wait_ge(centers_turned, 1)
            nc.scalar.mul(center_hi[:, :, :], ps[:, 0, :].rearrange("p (n m) -> p n m", n=pairs), -2.0)
            nc.scalar.mul(center_f[:, :, :], ps[:, 0, :].rearrange("p (n m) -> p n m", n=pairs), -2.0).then_inc(halved, 1)

        @block.vector
        def _(dve):
            count = [0]

            def link(instruction):
                count[0] += 1
                instruction.then_inc(step, 1)
                dve.wait_ge(step, count[0])

            dve.wait_ge(loaded, 16 * 26)
            dve.wait_ge(exps, 3)
            link(nc.vector.tensor_scalar(move_one[:, :], move_exp[:, :], 1.0, None, ALU.add))
            link(nc.vector.reciprocal(move_rec[:, :], move_one[:, :]))
            link(nc.vector.tensor_scalar(move_by[:, :], move_rec[:, :], 0.1, None, ALU.mult))
            link(nc.vector.scalar_tensor_tensor(out=centers[:, :, :], in0=delta[:, :, :], scalar=move_by[:, 0:1],
                                                in1=base[:, :, :], op0=ALU.mult, op1=ALU.add))
            nc.vector.tensor_copy(center_f[:, :, :], centers[:, :, :]).then_inc(centers_ready, 1)
            link(nc.vector.tensor_tensor(squares[:, :, :], centers[:, :, :], centers[:, :, :], ALU.mult))
            link(nc.vector.tensor_reduce(center_sq[:, :], squares[:, :, :], AX.X, ALU.add))
            link(nc.vector.tensor_scalar(clipped[:, :], scales[:, :], 0.0001, 2.0, ALU.max, ALU.min))
            link(nc.vector.tensor_tensor(scale_sq[:, :], clipped[:, :], clipped[:, :], ALU.mult))
            link(nc.vector.tensor_scalar(var_eps[:, :], scale_sq[:, :], 1e-8, None, ALU.add))
            link(nc.vector.reciprocal(inv_var[:, :], var_eps[:, :]))
            link(nc.vector.tensor_scalar(columns[:, 0, :], inv_var[:, :], -0.5, None, ALU.mult))
            link(nc.vector.tensor_tensor(columns[:, 1, :], columns[:, 0, :], center_sq[:, :], ALU.mult))
            link(nc.vector.tensor_scalar(kept_amp[:, :], amps[:, :], 0.02, None, ALU.is_gt))
            link(nc.vector.tensor_tensor(columns[:, 3, :], kept_amp[:, :], amps[:, :], ALU.mult))
            dve.wait_ge(masks_turned, 1)
            link(nc.vector.tensor_scalar(part_mask[:, :], ps[:, 1, 0:2], -1.0, None, ALU.mult))
            link(nc.vector.tensor_copy(keep_rows[:, :], ps[:, 1, 2:3]))
            link(nc.vector.tensor_scalar(columns[:, 2, :], columns[:, 3, :], keep_rows[:, 0:1], None, ALU.mult))
            link(nc.vector.tensor_scalar(temp_max[:, :], temp[:, :], 0.1, None, ALU.max))
            link(nc.vector.reciprocal(inv_temp[:, :], temp_max[:, :]))
            dve.wait_ge(halved, 1)
            nc.vector.tensor_tensor(center_lo[:, :, :], center_f[:, :, :], center_hi[:, :, :].bitcast(F32), ALU.subtract)

        @block.tensor
        def _(pe):
            pe.wait_ge(cleared, 2)
            for n in range(3):
                last = nc.tensor.matmul(ps[:, 1, n:n + 1], mask_rows[:, n, :], ident[0:1, 0:1], start=True, stop=True)
            last.then_inc(masks_turned, 1)
            pe.wait_ge(centers_ready, 1)
            for p in range(pairs):
                last = nc.tensor.transpose(ps[:, 0, p * 128:(p + 1) * 128], center_f[:, p, :], ident[:, :])
            last.then_inc(centers_turned, 1)


def attention(nc, a, ident, x_hi, x_lo, attended):
    n_nodes = x_hi.shape[2]
    tiles = n_nodes // R
    pairs = a["base_centers"].shape[0] // 2
    splats = a["base_centers"].shape[1]
    depth = a["base_centers"].shape[2]
    features = x_hi.shape[1] * 128
    blocks = x_hi.shape[1]
    wide = attended.shape[2]
    quarter = wide // 4
    part = n_nodes // 5
    with ExitStack() as ctx:
        sb, banks, sem = tools(nc, ctx, "attention")
        center_hi = sb("center_hi", [128, pairs, 128], F32R)
        center_lo = sb("center_lo", [128, pairs, 128], F32R)
        columns = sb("columns", [128, 4, pairs])
        part_mask = sb("part_mask", [128, 2])
        head_sum = sb("head_sum", [128, 128], F32R)
        inv_temp = sb("inv_temp", [R, 1])
        splat_constants(nc, a, ident, center_hi, center_lo, columns, part_mask, head_sum, inv_temp)
        own_hi = sb("own_hi", [128, 128], F32R)
        own_lo = sb("own_lo", [128, 128], F32R)
        own_cols = sb("own_cols", [128, 4])
        raw = sb("raw", [128, 3, features])
        w_hi = sb("w_hi", [128, 3, blocks, 128], F32R)
        w_lo = sb("w_lo", [128, 3, blocks, 128], F32R)
        side_hi = sb("side_hi", [128, 2, n_nodes], F32R)
        side_lo = sb("side_lo", [128, 2, n_nodes], F32R)
        square = sb("square", [128, 2, n_nodes])
        square_hi = sb("square_hi", [128, 2, n_nodes], F32R)
        square_lo = sb("square_lo", [128, 2, n_nodes], F32R)
        weight = sb("weight", [128, n_nodes])
        weight_amp = sb("weight_amp", [128, n_nodes])
        weight_hi = sb("weight_hi", [128, n_nodes], F32R)
        stack = sb("stack", [128, 3, wide], F32R)
        v_turn = sb("v_turn", [128, n_nodes])
        v_hi = sb("v_hi", [R, tiles, 2, depth + 1], F32R)
        v_lo = sb("v_lo", [R, tiles, 2, depth + 1], F32R)
        part_max = sb("part_max", [R, tiles, 2])
        row_max = sb("row_max", [R, tiles])
        shift = sb("shift", [tiles, R])
        shift_hi = sb("shift_hi", [tiles, R], F32R)
        shift_lo = sb("shift_lo", [tiles, R], F32R)
        prob = sb("prob", [R, 2, 2 * quarter])
        prob_hi = sb("prob_hi", [R, 2, 2 * quarter], F32R)
        prob_lo = sb("prob_lo", [R, 2, 2 * quarter], F32R)
        mixed = sb("mixed", [depth + 1, 2, 2 * quarter])
        ps = banks("ps", 8)

        names = ("ready raw_in raw_free own_in w_turned w_hi_ready w_lo_ready projected squared side_lo_ready "
                 "square_hi_ready square_lo_ready dist_ready weighted amped weight_parted stacked v_copied v_turned v_hi_ready "
                 "v_lo_ready scored reduced max_ready max_turned shift_step shift_in logits_ready prob_ready prob_hi_ready "
                 "prob_lo_ready mixed_out mix_step")
        s = {name: sem(name) for name in names.split()}
        stored = [sem("stored_0"), sem("stored_1")]
        block = ctx.enter_context(nc.Block())

        def five(first_bank):
            return ps[:, first_bank:first_bank + 3, :].rearrange("p a (c n) -> p (a c) n", n=256)[:, 0:5, 0:part]

        def fives(tile):
            return tile.rearrange("p (c n) -> p c n", n=part)

        def pair_of_banks(first, rows):
            return ps[0:rows, first:first + 2, 0:quarter]

        v_groups = [(0, 4), (4, 8), (8, tiles)]

        def v_bank(n, t0, t1):
            return ps[0:R, 6 + n % 2, 0:(t1 - t0) * 128].rearrange("p (t h d) -> p t h d", h=2, d=depth)

        @block.sync
        def _(sp):
            with sp.Fori(0, pairs) as p:
                sp.wait_ge(s["raw_free"], p + 1)
                for n in range(3):
                    sp.dma_start(raw[:, n, :], a["qkv_w"][bass.ds(p * PAIR + n * features, PAIR), :]).then_inc(s["raw_in"], 16)
                for h in range(2):
                    row = CODES * h + 3 * splats
                    sp.wait_ge(s["shift_step"], p * 6 + 3 * h + 3)
                    sp.dma_start(stack[row:row + 1, h, 0:n_nodes].bitcast(F32), shift_hi[:, :].bitcast(F32)).then_inc(s["shift_in"], 16)
                    sp.dma_start(stack[row + 1:row + 2, h, 0:n_nodes].bitcast(F32), shift_lo[:, :].bitcast(F32)).then_inc(s["shift_in"], 16)
                    for half in range(2):
                        g = 2 * h + half
                        sp.wait_ge(s["mixed_out"], p * 4 + g + 2)
                        sp.dma_start(attended[bass.ds(p * 2 + h, 1), :, 2 * quarter * half:2 * quarter * (half + 1)].rearrange("a d n -> (a d) n"),
                                     mixed[:, half, :]).then_inc(stored[half], 16)
            for half in range(2):
                sp.wait_ge(stored[half], 16 * (2 * pairs + 1))

        @block.gpsimd
        def _(pool):
            nc.gpsimd.memset(stack[:, :, :].bitcast(F32), 0.0).then_inc(s["ready"], 1)
            nc.gpsimd.memset(v_hi[:, :, :, :].bitcast(F32), 1.0).then_inc(s["ready"], 1)
            nc.gpsimd.memset(v_lo[:, :, :, :].bitcast(F32), 0.0).then_inc(s["ready"], 1)
            for half in range(2):
                pool.sem_inc(stored[half], 16)
            with pool.Fori(0, pairs) as p:
                pool.wait_ge(s["stacked"], p * 3 + 1)
                nc.gpsimd.tensor_copy(own_hi[:, :], center_hi[:, bass.ds(p, 1), :].rearrange("p a n -> p (a n)").bitcast(F32))
                nc.gpsimd.tensor_copy(own_lo[:, :], center_lo[:, bass.ds(p, 1), :].rearrange("p a n -> p (a n)").bitcast(F32))
                nc.gpsimd.tensor_copy(own_cols[:, :], columns[:, :, bass.ds(p, 1)].rearrange("p c a -> p (c a)")).then_inc(s["own_in"], 1)

        @block.vector
        def _(dve):
            dve.sem_inc(s["stacked"], 1)
            dve.wait_ge(s["ready"], 3)
            with dve.Fori(0, pairs) as p:
                for n in range(3):
                    dve.wait_ge(s["w_hi_ready"], p * 3 + n + 1)
                    nc.vector.tensor_tensor(w_lo[:, n, :, :], ps[:, 6 + n % 2, :].rearrange("p (k n) -> p k n", n=128),
                                            w_hi[:, n, :, :].bitcast(F32), ALU.subtract).then_inc(s["w_lo_ready"], 1)

                def parts(n):
                    dve.wait_ge(s["squared"], p * 2 + n + 1)
                    nc.vector.tensor_tensor(fives(side_lo[:, n, :]), five(0), fives(side_hi[:, n, :]).bitcast(F32),
                                            ALU.subtract).then_inc(s["side_lo_ready"], 1)
                    nc.vector.tensor_copy(square_hi[:, n, :], square[:, n, :]).then_inc(s["square_hi_ready"], 1)
                    dve.wait_ge(s["square_hi_ready"], p * 2 + n + 1)
                    nc.vector.tensor_tensor(square_lo[:, n, :], square[:, n, :], square_hi[:, n, :].bitcast(F32),
                                            ALU.subtract).then_inc(s["square_lo_ready"], 1)

                def stacks(n):
                    dve.wait_ge(s["own_in"], p + 1)
                    dve.wait_ge(s["stacked"], p * 3 + 2 * n + 1)
                    dve.wait_ge(s["weighted"], p * 2 + n + 1)
                    nc.vector.tensor_scalar(weight_amp[:, :], weight[:, :], own_cols[:, 2 + n:3 + n], None, ALU.mult).then_inc(s["amped"], 1)
                    dve.wait_ge(s["amped"], p * 2 + n + 1)
                    nc.vector.tensor_copy(weight_hi[:, :], weight_amp[:, :]).then_inc(s["weight_parted"], 1)
                    dve.wait_ge(s["weight_parted"], p * 2 + n + 1)
                    for to, rows in (((0, slice(0, CODES)), (1, slice(CODES, 2 * CODES))), ((2, slice(0, 2 * CODES)),))[n]:
                        nc.vector.scalar_tensor_tensor(out=stack[rows, to, 0:n_nodes], in0=weight_hi[rows, :].bitcast(F32),
                                                       scalar=part_mask[rows, n:n + 1], in1=weight_amp[rows, :],
                                                       op0=ALU.mult, op1=ALU.add).then_inc(s["stacked"], 1)

                parts(0)
                parts(1)
                stacks(0)
                stacks(1)
                for n, (t0, t1) in enumerate(v_groups):
                    dve.wait_ge(s["v_hi_ready"], p * 3 + n + 1)
                    nc.vector.tensor_tensor(v_lo[:, t0:t1, :, 0:depth], v_bank(n, t0, t1), v_hi[:, t0:t1, :, 0:depth].bitcast(F32),
                                            ALU.subtract).then_inc(s["v_lo_ready"], 1)
                for h in range(2):
                    for t in range(tiles):
                        for half in range(2):
                            g = 2 * t + half
                            dve.wait_ge(s["scored"], p * 4 * tiles + 2 * tiles * h + g + 1)
                            nc.vector.tensor_reduce(part_max[:, t, half:half + 1], pair_of_banks(2 * (g % 2), R), AX.XY, ALU.max).then_inc(s["reduced"], 1)
                    dve.wait_ge(s["reduced"], (p * 4 + 2 * h + 2) * tiles)
                    nc.vector.tensor_reduce(row_max[:, :], part_max[:, :, :], AX.X, ALU.max).then_inc(s["max_ready"], 1)
                    dve.wait_ge(s["max_turned"], p * 2 + h + 1)
                    nc.vector.tensor_scalar(shift[:, :], ps[0:tiles, 0, 0:R], -1.0, None, ALU.mult).then_inc(s["shift_step"], 1)
                    dve.wait_ge(s["shift_step"], p * 6 + 3 * h + 1)
                    nc.vector.tensor_copy(shift_hi[:, :], shift[:, :]).then_inc(s["shift_step"], 1)
                    dve.wait_ge(s["shift_step"], p * 6 + 3 * h + 2)
                    nc.vector.tensor_tensor(shift_lo[:, :], shift[:, :], shift_hi[:, :].bitcast(F32), ALU.subtract).then_inc(s["shift_step"], 1)
                    for n in range(2 * tiles):
                        at = p * 4 * tiles + 2 * tiles * h + n
                        dve.wait_ge(s["prob_hi_ready"], at + 1)
                        if n >= 2:
                            dve.wait_ge(s["mix_step"], at - 1)
                        nc.vector.tensor_tensor(prob_lo[:, n % 2, :], prob[:, n % 2, :], prob_hi[:, n % 2, :].bitcast(F32),
                                                ALU.subtract).then_inc(s["prob_lo_ready"], 1)

        @block.scalar
        def _(act):
            act.sem_inc(s["mixed_out"], 1)
            act.wait_ge(s["ready"], 3)
            with act.Fori(0, pairs) as p:
                for n in range(3):
                    act.wait_ge(s["w_turned"], p * 3 + n + 1)
                    nc.scalar.copy(w_hi[:, n, :, :], ps[:, 6 + n % 2, :].rearrange("p (k n) -> p k n", n=128)).then_inc(s["w_hi_ready"], 1)

                def parts(n):
                    act.wait_ge(s["projected"], p * 3 + n + 1)
                    nc.scalar.copy(fives(side_hi[:, n, :]), five(0))
                    nc.scalar.activation(fives(square[:, n, :]), five(0), ACT.Square).then_inc(s["squared"], 1)

                def weights(n):
                    act.wait_ge(s["own_in"], p + 1)
                    act.wait_ge(s["dist_ready"], p * 2 + n + 1)
                    if n:
                        act.wait_ge(s["amped"], p * 2 + 1)
                    nc.scalar.activation(fives(weight[:, :]), five(3), ACT.Exp, scale=own_cols[:, 0:1],
                                         bias=own_cols[:, 1:2]).then_inc(s["weighted"], 1)

                parts(0)
                parts(1)
                weights(0)
                act.wait_ge(s["projected"], p * 3 + 3)
                nc.scalar.copy(fives(v_turn[:, :]), five(0)).then_inc(s["v_copied"], 1)
                weights(1)
                for n, (t0, t1) in enumerate(v_groups):
                    act.wait_ge(s["v_turned"], p * 3 + n + 1)
                    nc.scalar.copy(v_hi[:, t0:t1, :, 0:depth], v_bank(n, t0, t1)).then_inc(s["v_hi_ready"], 1)
                for h in range(2):
                    for n in range(2 * tiles):
                        at = p * 4 * tiles + 2 * tiles * h + n
                        act.wait_ge(s["logits_ready"], at + 1)
                        if n >= 2:
                            act.wait_ge(s["prob_lo_ready"], at - 1)
                        nc.scalar.activation(prob[:, n % 2, :].rearrange("p (a n) -> p a n", a=2), pair_of_banks(2 + 2 * (n % 2), R),
                                             ACT.Exp, scale=inv_temp[:, 0:1]).then_inc(s["prob_ready"], 1)
                        act.wait_ge(s["prob_ready"], at + 1)
                        if n >= 2:
                            act.wait_ge(s["mix_step"], at - 1)
                        nc.scalar.copy(prob_hi[:, n % 2, :], prob[:, n % 2, :]).then_inc(s["prob_hi_ready"], 1)
                        if n % tiles == tiles - 1:
                            g = 2 * h + n // tiles
                            act.wait_ge(s["mix_step"], at + 1)
                            act.wait_ge(stored[g % 2], (p * 2 + h + 1) * 16)
                            nc.scalar.copy(mixed[:, g % 2, :].rearrange("p (a n) -> p a n", a=2), pair_of_banks(6, depth + 1)).then_inc(s["mixed_out"], 1)

        @block.tensor
        def _(pe):
            pe.sem_inc(s["raw_free"], 1)
            with pe.Fori(0, pairs) as p:
                pe.wait_ge(s["mixed_out"], p * 4 + 1)
                for n in range(3):
                    pe.wait_ge(s["raw_in"], p * 48 + 48)
                    if n == 2:
                        pe.wait_ge(s["w_lo_ready"], p * 3 + 1)
                    for k in range(blocks):
                        last = nc.tensor.transpose(ps[:, 6 + n % 2, k * 128:(k + 1) * 128], raw[:, n, k * 128:(k + 1) * 128], ident[:, :])
                    last.then_inc(s["w_turned"], 1)
                pe.sem_inc(s["raw_free"], 1)

                def project(n):
                    pe.wait_ge(s["w_lo_ready"], p * 3 + n + 1)
                    if n:
                        pe.wait_ge(s["side_lo_ready"], p * 2 + n)
                    for k in range(blocks):
                        for m, (w, x) in enumerate(((w_hi, x_hi), (w_hi, x_lo), (w_lo, x_hi))):
                            for c in range(5):
                                last = nc.tensor.matmul(five(0)[:, c, :], w[:, n, k, :], x[:, k, c * part:(c + 1) * part],
                                                        start=(k == 0 and m == 0 and c % 2 == 0), stop=(k == blocks - 1 and m == 2),
                                                        skip_group_check=True)
                    last.then_inc(s["projected"], 1)

                def distances(n):
                    pe.wait_ge(s["own_in"], p + 1)
                    if n:
                        pe.wait_ge(s["weighted"], p * 2 + n)
                    pe.wait_ge(s["square_lo_ready"], p * 2 + n + 1)
                    products = ((own_hi, side_hi), (own_lo, side_hi), (own_hi, side_lo), (head_sum, square_hi), (head_sum, square_lo))
                    for m, (w, x) in enumerate(products):
                        for c in range(5):
                            last = nc.tensor.matmul(five(3)[:, c, :], w[:, :], x[:, n, c * part:(c + 1) * part],
                                                    start=(m == 0 and c % 2 == 0), stop=(m == 4), skip_group_check=True)
                    last.then_inc(s["dist_ready"], 1)

                project(0)
                project(1)
                distances(0)
                project(2)
                distances(1)
                pe.wait_ge(s["v_copied"], p + 1)
                for n, (t0, t1) in enumerate(v_groups):
                    if n == 2:
                        pe.wait_ge(s["v_lo_ready"], p * 3 + 1)
                    for t in range(t0, t1):
                        last = nc.tensor.transpose(ps[0:R, 6 + n % 2, (t - t0) * 128:(t - t0 + 1) * 128],
                                                   v_turn[:, t * R:(t + 1) * R], ident[:, :])
                    last.then_inc(s["v_turned"], 1)
                pe.wait_ge(s["stacked"], p * 3 + 4)

                for h in range(2):
                    for g in range(2 * tiles):
                        t, half = divmod(g, 2)
                        if g >= 2:
                            pe.wait_ge(s["reduced"], p * 4 * tiles + 2 * tiles * h + g - 1)
                        for c in range(2):
                            at = (2 * half + c) * quarter
                            last = nc.tensor.matmul(ps[0:R, 2 * (g % 2) + c, 0:quarter], stack[:, h, t * R:(t + 1) * R],
                                                    stack[:, 2, at:at + quarter], start=True, stop=True)
                        last.then_inc(s["scored"], 1)
                    pe.wait_ge(s["max_ready"], p * 2 + h + 1)
                    nc.tensor.transpose(ps[0:tiles, 0, 0:R], row_max[:, :], ident[0:R, 0:R]).then_inc(s["max_turned"], 1)
                    pe.wait_ge(s["shift_in"], p * 64 + 32 * h + 32)
                    def logits(n):
                        half, t = divmod(n, tiles)
                        if n >= 2:
                            pe.wait_ge(s["prob_ready"], p * 4 * tiles + 2 * tiles * h + n - 1)
                        for c in range(2):
                            at = (2 * half + c) * quarter
                            last = nc.tensor.matmul(ps[0:R, 2 + 2 * (n % 2) + c, 0:quarter], stack[:, 2, t * R:(t + 1) * R],
                                                    stack[:, h, at:at + quarter], start=True, stop=True)
                        last.then_inc(s["logits_ready"], 1)

                    def mix(n):
                        half, t = divmod(n, tiles)
                        at = p * 4 * tiles + 2 * tiles * h + n
                        if t == 0:
                            pe.wait_ge(s["mixed_out"], p * 4 + 2 * h + half + 1)
                        pe.wait_ge(s["prob_hi_ready"], at + 1)
                        for m, (v, prb) in enumerate(((v_hi, prob_hi), (v_lo, prob_hi), (v_hi, prob_lo))):
                            if m == 2:
                                pe.wait_ge(s["prob_lo_ready"], at + 1)
                            for c in range(2):
                                last = nc.tensor.matmul(ps[0:depth + 1, 6 + c, 0:quarter], v[:, t, h, :],
                                                        prb[:, n % 2, c * quarter:(c + 1) * quarter],
                                                        start=(t == 0 and m == 0), stop=(t == tiles - 1 and m == 2),
                                                        skip_group_check=True)
                        last.then_inc(s["mix_step"], 1)

                    logits(0)
                    for n in range(2 * tiles):
                        if n + 1 < 2 * tiles:
                            logits(n + 1)
                        mix(n)

def combine(nc, x, attended, graph_w, graph_b, out_w, ident, kept, x_tiles):
    tiles, width = x_tiles.shape[1], x_tiles.shape[2]
    n_nodes = kept.shape[2]
    blocks = width // 128
    depth = attended.shape[1] - 1
    with ExitStack() as ctx:
        sb, banks, sem = tools(nc, ctx, "combine")
        raw = sb("raw", [128, 2, width])
        w_hi = sb("w_hi", [128, 2, blocks, width], F32R)
        w_lo = sb("w_lo", [128, 2, blocks, width], F32R)
        offset = sb("offset", [R, width])
        heads = sb("heads", [128, 2, n_nodes])
        total = sb("total", [128, 2, n_nodes])
        part_hi = sb("part_hi", [128, 2 * blocks, n_nodes], F32R)
        part_lo = sb("part_lo", [128, 2 * blocks, n_nodes], F32R)
        ps = banks("ps", 4)
        names = "x_in offset_in raw_turned w_hi_ready w_lo_ready offset_added reciprocal_ready divided hi_ready lo_ready summed tile_out"
        s = {name: sem(name) for name in names.split()}
        raw_in = [sem("raw_in_0"), sem("raw_in_1")]
        heads_in = [sem("heads_in_0"), sem("heads_in_1")]
        block = ctx.enter_context(nc.Block())

        @block.sync
        def _(sp):
            for n in range(2 * blocks):
                w = (graph_w, out_w)[n // blocks]
                if n >= 2:
                    sp.wait_ge(s["raw_turned"], n - 1)
                sp.dma_start(raw[:, n % 2, :], w[n % blocks * 128:(n % blocks + 1) * 128, :]).then_inc(raw_in[n % 2], 16)
                if n == 0:
                    sp.dma_start(x_tiles[:, :, :], x.rearrange("(t p) n -> p t n", p=R)).then_inc(s["x_in"], 16)
                    sp.dma_start(offset[:, :], graph_b.partition_broadcast(R)).then_inc(s["offset_in"], 16)

        @block.gpsimd
        def _(pool):
            for k in range(blocks):
                if k >= 2:
                    pool.wait_ge(s["lo_ready"], k - 1)
                for h in range(2):
                    rows = slice(depth * h, depth * (h + 1))
                    pool.dma_start(heads[rows, k % 2, :], attended[2 * k + h, 0:depth, 0:n_nodes]).then_inc(heads_in[k % 2], 16)
                    pool.dma_start(total[rows, k % 2, :],
                                   attended[2 * k + h, depth, 0:n_nodes].partition_broadcast(depth)).then_inc(heads_in[k % 2], 16)
            pool.wait_ge(s["x_in"], 16)
            pool.wait_ge(s["offset_in"], 16)
            for t in range(tiles):
                nc.gpsimd.tensor_tensor(x_tiles[:, t, :], x_tiles[:, t, :], offset[:, :], ALU.add).then_inc(s["offset_added"], 1)

        @block.vector
        def _(dve):
            for n in range(2 * blocks):
                dve.wait_ge(s["w_hi_ready"], n + 1)
                w, o = divmod(n, blocks)
                nc.vector.tensor_tensor(w_lo[:, w, :, o * 128:(o + 1) * 128], ps[:, n % 2, :].rearrange("p (k n) -> p k n", n=128),
                                        w_hi[:, w, :, o * 128:(o + 1) * 128].bitcast(F32), ALU.subtract).then_inc(s["w_lo_ready"], 1)
            for k in range(blocks):
                dve.wait_ge(heads_in[k % 2], 64 * (k // 2 + 1))
                nc.vector.reciprocal(total[:, k % 2, :], total[:, k % 2, :]).then_inc(s["reciprocal_ready"], 1)
                dve.wait_ge(s["reciprocal_ready"], k + 1)
                nc.vector.tensor_tensor(heads[:, k % 2, :], heads[:, k % 2, :], total[:, k % 2, :], ALU.mult).then_inc(s["divided"], 1)
                dve.wait_ge(s["hi_ready"], blocks + k + 1)
                nc.vector.tensor_tensor(part_lo[:, blocks + k, :], heads[:, k % 2, :], part_hi[:, blocks + k, :].bitcast(F32),
                                        ALU.subtract).then_inc(s["lo_ready"], 1)
            for k in range(blocks):
                dve.wait_ge(s["hi_ready"], k + 1)
                nc.vector.tensor_tensor(part_lo[:, k, :], kept[:, k, :], part_hi[:, k, :].bitcast(F32),
                                        ALU.subtract).then_inc(s["lo_ready"], 1)
            dve.wait_ge(s["offset_added"], tiles)
            for t in range(tiles):
                dve.wait_ge(s["summed"], t + 1)
                nc.vector.tensor_tensor(x_tiles[:, t, :], ps[0:R, 2 + t % 2, :], x_tiles[:, t, :], ALU.add).then_inc(s["tile_out"], 1)

        @block.scalar
        def _(act):
            for n in range(2 * blocks):
                act.wait_ge(s["raw_turned"], n + 1)
                w, o = divmod(n, blocks)
                nc.scalar.copy(w_hi[:, w, :, o * 128:(o + 1) * 128], ps[:, n % 2, :].rearrange("p (k n) -> p k n", n=128)).then_inc(s["w_hi_ready"], 1)
            for k in range(blocks):
                nc.scalar.copy(part_hi[:, k, :], kept[:, k, :]).then_inc(s["hi_ready"], 1)
            for k in range(blocks):
                act.wait_ge(s["divided"], k + 1)
                nc.scalar.copy(part_hi[:, blocks + k, :], heads[:, k % 2, :]).then_inc(s["hi_ready"], 1)

        @block.tensor
        def _(pe):
            for n in range(2 * blocks):
                pe.wait_ge(raw_in[n % 2], 16 * (n // 2 + 1))
                if n >= 2:
                    pe.wait_ge(s["w_lo_ready"], n - 1)
                for k in range(blocks):
                    last = nc.tensor.transpose(ps[:, n % 2, k * 128:(k + 1) * 128], raw[:, n % 2, k * 128:(k + 1) * 128], ident[:, :])
                last.then_inc(s["raw_turned"], 1)
            pe.wait_ge(s["w_lo_ready"], 2 * blocks)
            pe.wait_ge(s["lo_ready"], 2 * blocks)
            for t in range(tiles):
                if t >= 2:
                    pe.wait_ge(s["tile_out"], t - 1)
                at = slice(t * R, (t + 1) * R)
                for k in range(2 * blocks):
                    w, kk = divmod(k, blocks)
                    for m, (left, right) in enumerate(((part_hi, w_hi), (part_hi, w_lo), (part_lo, w_hi))):
                        last = nc.tensor.matmul(ps[0:R, 2 + t % 2, :], left[:, k, at], right[:, w, kk, :],
                                                start=(k == 0 and m == 0), stop=(k == 2 * blocks - 1 and m == 2))
                last.then_inc(s["summed"], 1)


def normalise(nc, name, x_tiles, out_tiles, eps, gain=None, offset=None, residual=None, out=None):
    tiles, width = x_tiles.shape[1], x_tiles.shape[2]
    with ExitStack() as ctx:
        sb, banks, sem = tools(nc, ctx, name)
        stats = sb("stats", [R, 2, 6])
        moments = sb("moments", [R, tiles, 2])
        root = sb("root", [R, tiles])
        scale = sb("scale", [R, tiles])
        eps_col = sb("eps_col", [R, 1])
        rows = sb("rows", [R, 2, width])
        names = "eps_in rows_in stats_ready moments_ready root_ready scale_ready unit_ready gained shifted finished stored"
        s = {n: sem(n) for n in names.split()}
        block = ctx.enter_context(nc.Block())

        @block.sync
        def _(sp):
            if gain is not None:
                sp.dma_start(rows[:, 0, :], gain.partition_broadcast(R)).then_inc(s["rows_in"], 16)
                sp.dma_start(rows[:, 1, :], offset.partition_broadcast(R)).then_inc(s["rows_in"], 16)
                for t in range(tiles):
                    sp.wait_ge(s["finished"], t + 1)
                    sp.dma_start(out[t * R:(t + 1) * R, :], x_tiles[:, t, :]).then_inc(s["stored"], 16)
                sp.wait_ge(s["stored"], 16 * tiles)

        @block.gpsimd
        def _(pool):
            nc.gpsimd.memset(eps_col[:, :], eps).then_inc(s["eps_in"], 1)
            if gain is not None:
                pool.wait_ge(s["rows_in"], 32)
                for t in range(tiles):
                    pool.wait_ge(s["gained"], t + 1)
                    nc.gpsimd.tensor_tensor(x_tiles[:, t, :], out_tiles[:, t, :], rows[:, 1, :], ALU.add).then_inc(s["shifted"], 1)

        @block.vector
        def _(dve):
            for t in range(tiles):
                if t >= 2:
                    dve.wait_ge(s["moments_ready"], t - 1)
                nc.vector.bn_stats(stats[:, t % 2, :], x_tiles[:, t, :]).then_inc(s["stats_ready"], 1)
                dve.wait_ge(s["stats_ready"], t + 1)
                nc.vector.bn_aggr(moments[:, t, :], stats[:, t % 2, :]).then_inc(s["moments_ready"], 1)
            dve.wait_ge(s["root_ready"], 1)
            nc.vector.reciprocal(scale[:, :], root[:, :]).then_inc(s["scale_ready"], 1)
            dve.wait_ge(s["scale_ready"], 1)
            for t in range(tiles):
                nc.vector.tensor_scalar(out_tiles[:, t, :], x_tiles[:, t, :], moments[:, t, 0:1], scale[:, t:t + 1],
                                        ALU.subtract, ALU.mult).then_inc(s["unit_ready"], 1)
                if gain is not None:
                    dve.wait_ge(s["rows_in"], 32)
                    dve.wait_ge(s["unit_ready"], t + 1)
                    nc.vector.tensor_tensor(out_tiles[:, t, :], out_tiles[:, t, :], rows[:, 0, :], ALU.mult).then_inc(s["gained"], 1)
                    if t >= 1:
                        dve.wait_ge(s["shifted"], t)
                        nc.vector.tensor_tensor(x_tiles[:, t - 1, :], x_tiles[:, t - 1, :], residual[:, t - 1, :], ALU.add).then_inc(s["finished"], 1)
            if gain is not None:
                dve.wait_ge(s["shifted"], tiles)
                nc.vector.tensor_tensor(x_tiles[:, tiles - 1, :], x_tiles[:, tiles - 1, :], residual[:, tiles - 1, :], ALU.add).then_inc(s["finished"], 1)

        @block.scalar
        def _(act):
            act.wait_ge(s["moments_ready"], tiles)
            act.wait_ge(s["eps_in"], 1)
            nc.scalar.activation(root[:, :], moments[:, :, 1], ACT.Sqrt, bias=eps_col[:, 0:1]).then_inc(s["root_ready"], 1)


def gate(nc, x_hi, x_lo, w_gate, b2, ident, unit, share, mixed):
    tiles, experts = share.shape[1], share.shape[2]
    width = b2.shape[1]
    blocks = w_gate.shape[0] // 128
    with ExitStack() as ctx:
        sb, banks, sem = tools(nc, ctx, "gate")
        w = sb("w", [128, blocks, experts])
        w_hi = sb("w_hi", [128, blocks, experts], F32R)
        w_lo = sb("w_lo", [128, blocks, experts], F32R)
        bias = sb("bias", [experts, width])
        number = sb("number", [R, tiles, experts])
        logit = sb("logit", [R, tiles, experts])
        top_logit = sb("top_logit", [R, tiles])
        less = sb("less", [R, tiles, experts])
        exps = sb("exps", [R, tiles, experts])
        total = sb("total", [R, tiles])
        total_rec = sb("total_rec", [R, tiles])
        prob = sb("prob", [R, tiles, experts])
        best = sb("best", [R, tiles, 8])
        best_at = sb("best_at", [R, tiles, 8], mybir.dt.uint32)
        best_f = sb("best_f", [R, tiles, 8])
        pair_sum = sb("pair_sum", [R, tiles])
        pair_rec = sb("pair_rec", [R, tiles])
        conf = sb("conf", [R, tiles, 2])
        chosen = sb("chosen", [R, 2, tiles, experts])
        weighed = sb("weighed", [R, 2, tiles, experts])
        share_turn = sb("share_turn", [experts, tiles, R])
        ps = banks("ps", 5)
        names = "w_in bias_in numbers parted scored step less_ready exp_ready shared turned turn_out biased bias_out"
        s = {n: sem(n) for n in names.split()}
        block = ctx.enter_context(nc.Block())

        @block.sync
        def _(sp):
            sp.dma_start(w[:, :, :], w_gate.rearrange("(k p) e -> p k e", p=128)).then_inc(s["w_in"], 16)
            sp.dma_start(bias[:, :], b2).then_inc(s["bias_in"], 16)

        @block.gpsimd
        def _(pool):
            nc.gpsimd.iota(number[:, :, :], [[0, tiles], [1, experts]], base=0, channel_multiplier=0,
                           allow_small_or_imprecise_dtypes=True).then_inc(s["numbers"], 1)

        @block.scalar
        def _(act):
            act.wait_ge(s["less_ready"], 1)
            nc.scalar.activation(exps[:, :, :], less[:, :, :], ACT.Exp).then_inc(s["exp_ready"], 1)

        @block.vector
        def _(dve):
            count = [0]

            def link(instruction):
                count[0] += 1
                instruction.then_inc(s["step"], 1)
                dve.wait_ge(s["step"], count[0])

            def along(column):
                return column.unsqueeze(2).to_broadcast([R, tiles, experts])

            dve.wait_ge(s["w_in"], 16)
            link(nc.vector.tensor_copy(w_hi[:, :, :], w[:, :, :]))
            nc.vector.tensor_tensor(w_lo[:, :, :], w[:, :, :], w_hi[:, :, :].bitcast(F32), ALU.subtract).then_inc(s["parted"], 1)
            dve.wait_ge(s["scored"], 1)
            link(nc.vector.tensor_copy(logit[:, :, :], ps[0:R, 0, 0:tiles * experts].rearrange("p (t e) -> p t e", e=experts)))
            link(nc.vector.tensor_reduce(top_logit[:, :], logit[:, :, :], AX.X, ALU.max))
            nc.vector.tensor_tensor(less[:, :, :], logit[:, :, :], along(top_logit[:, :]), ALU.subtract).then_inc(s["less_ready"], 1)
            dve.wait_ge(s["exp_ready"], 1)
            link(nc.vector.tensor_reduce(total[:, :], exps[:, :, :], AX.X, ALU.add))
            link(nc.vector.reciprocal(total_rec[:, :], total[:, :]))
            link(nc.vector.tensor_tensor(prob[:, :, :], exps[:, :, :], along(total_rec[:, :]), ALU.mult))
            for t in range(tiles):
                last = nc.vector.max(best[:, t, :], prob[:, t, :])
            link(last)
            for t in range(tiles):
                last = nc.vector.max_index(best_at[:, t, :], best[:, t, :], prob[:, t, :])
            link(last)
            link(nc.vector.tensor_copy(best_f[:, :, :], best_at[:, :, :]))
            link(nc.vector.tensor_tensor(pair_sum[:, :], best[:, :, 0], best[:, :, 1], ALU.add))
            link(nc.vector.reciprocal(pair_rec[:, :], pair_sum[:, :]))
            dve.wait_ge(s["numbers"], 1)
            for n in range(2):
                link(nc.vector.tensor_tensor(conf[:, :, n], best[:, :, n], pair_rec[:, :], ALU.mult))
                link(nc.vector.tensor_tensor(chosen[:, n, :, :], number[:, :, :], along(best_f[:, :, n]), ALU.is_equal))
                link(nc.vector.tensor_tensor(weighed[:, n, :, :], chosen[:, n, :, :], along(conf[:, :, n]), ALU.mult))
            nc.vector.tensor_tensor(share[:, :, :], weighed[:, 0, :, :], weighed[:, 1, :, :], ALU.add).then_inc(s["shared"], 1)
            for t0 in range(0, tiles, 4):
                t1 = min(t0 + 4, tiles)
                dve.wait_ge(s["turned"], t0 // 4 + 1)
                nc.vector.tensor_copy(share_turn[:, t0:t1, :], ps[0:experts, 1 + t0 // 4 % 2, 0:(t1 - t0) * R].rearrange("p (t n) -> p t n", n=R)).then_inc(s["turn_out"], 1)
            for t in range(tiles):
                dve.wait_ge(s["biased"], t + 1)
                nc.vector.tensor_tensor(mixed[:, t, :], ps[0:R, 3 + t % 2, :], unit[:, t, :], ALU.add).then_inc(s["bias_out"], 1)

        @block.tensor
        def _(pe):
            pe.wait_ge(s["parted"], 1)
            for t in range(tiles):
                at = slice(t * R, (t + 1) * R)
                for k in range(blocks):
                    for m, (left, right) in enumerate(((x_hi, w_hi), (x_hi, w_lo), (x_lo, w_hi))):
                        last = nc.tensor.matmul(ps[0:R, 0, t * experts:(t + 1) * experts], left[:, k, at], right[:, k, :],
                                                start=(k == 0 and m == 0), stop=(k == blocks - 1 and m == 2))
            last.then_inc(s["scored"], 1)
            pe.wait_ge(s["shared"], 1)
            for t in range(tiles):
                if t == 8:
                    pe.wait_ge(s["turn_out"], 1)
                last = nc.tensor.transpose(ps[0:experts, 1 + t // 4 % 2, t % 4 * R:(t % 4 + 1) * R], share[:, t, :], ident[0:R, 0:R])
                if t % 4 == 3 or t == tiles - 1:
                    last.then_inc(s["turned"], 1)
            pe.wait_ge(s["turn_out"], (tiles + 3) // 4)
            pe.wait_ge(s["bias_in"], 16)
            for t in range(tiles):
                if t >= 2:
                    pe.wait_ge(s["bias_out"], t - 1)
                nc.tensor.matmul(ps[0:R, 3 + t % 2, :], share_turn[:, t, :], bias[:, :], start=True, stop=True).then_inc(s["biased"], 1)


def experts_mix(nc, x_hi, x_lo, w1, b1, w2, share, mixed):
    tiles = mixed.shape[1]
    n_nodes = x_hi.shape[2]
    experts, width, hidden = w1.shape
    k1, k2 = width // 128, hidden // 128
    chunks = spans(n_nodes, 500)
    with ExitStack() as ctx:
        sb, banks, sem = tools(nc, ctx, "experts")
        raw1 = sb("raw1", [128, k1, hidden])
        raw2 = sb("raw2", [128, k2, width])
        bias = sb("bias", [128, k2])
        w1_hi = sb("w1_hi", [128, k1, hidden], F32R)
        w1_lo = sb("w1_lo", [128, k1, hidden], F32R)
        w2_hi = sb("w2_hi", [128, k2, width], F32R)
        w2_lo = sb("w2_lo", [128, k2, width], F32R)
        act_f = sb("act_f", [128, k2, n_nodes])
        act_hi = sb("act_hi", [128, k2, n_nodes], F32R)
        act_lo = sb("act_lo", [128, k2, n_nodes], F32R)
        ps = banks("ps", 8)
        names = ("w_in w1_hi_ready w1_lo_ready w2_hi_ready w2_lo_ready projected act_ready act_hi_ready act_lo_ready output added")
        s = {n: sem(n) for n in names.split()}
        block = ctx.enter_context(nc.Block())

        @block.sync
        def _(sp):
            sp.sem_inc(s["w2_lo_ready"], 1)
            sp.sem_inc(s["act_ready"], k2)
            with sp.Fori(0, experts) as e:
                sp.wait_ge(s["w2_lo_ready"], e + 1)
                sp.wait_ge(s["act_ready"], e * k2 + k2)
                sp.dma_start(raw1[:, :, :], w1[bass.ds(e, 1), :, :].rearrange("a (k p) n -> p (a k) n", p=128)).then_inc(s["w_in"], 16)
                sp.dma_start(raw2[:, :, :], w2[bass.ds(e, 1), :, :].rearrange("a (k p) n -> p (a k) n", p=128)).then_inc(s["w_in"], 16)
                sp.dma_start(bias[:, :], b1[bass.ds(e, 1), :].rearrange("a (k p) -> p (a k)", p=128),
                             allow_slow_non_contiguous=True).then_inc(s["w_in"], 16)

        @block.vector
        def _(dve):
            dve.sem_inc(s["added"], tiles)
            with dve.Fori(0, experts) as e:
                dve.wait_ge(s["w_in"], e * 48 + 48)
                dve.wait_ge(s["added"], e * tiles + tiles)
                nc.vector.tensor_copy(w1_hi[:, :, :], raw1[:, :, :]).then_inc(s["w1_hi_ready"], 1)
                nc.vector.tensor_copy(w2_hi[:, :, :], raw2[:, :, :]).then_inc(s["w2_hi_ready"], 1)
                dve.wait_ge(s["w1_hi_ready"], e + 1)
                nc.vector.tensor_tensor(w1_lo[:, :, :], raw1[:, :, :], w1_hi[:, :, :].bitcast(F32), ALU.subtract).then_inc(s["w1_lo_ready"], 1)
                dve.wait_ge(s["w2_hi_ready"], e + 1)
                nc.vector.tensor_tensor(w2_lo[:, :, :], raw2[:, :, :], w2_hi[:, :, :].bitcast(F32), ALU.subtract).then_inc(s["w2_lo_ready"], 1)
                for m in range(k2):
                    dve.wait_ge(s["act_ready"], e * k2 + k2 + m + 1)
                    nc.vector.tensor_copy(act_hi[:, m, :], act_f[:, m, :]).then_inc(s["act_hi_ready"], 1)
                    dve.wait_ge(s["act_hi_ready"], e * k2 + m + 1)
                    nc.vector.tensor_tensor(act_lo[:, m, :], act_f[:, m, :], act_hi[:, m, :].bitcast(F32), ALU.subtract).then_inc(s["act_lo_ready"], 1)
                for t in range(tiles):
                    dve.wait_ge(s["output"], e * tiles + t + 1)
                    nc.vector.scalar_tensor_tensor(out=mixed[:, t, :], in0=ps[0:R, 6 + t % 2, :],
                                                   scalar=share[:, t, bass.ds(e, 1)], in1=mixed[:, t, :],
                                                   op0=ALU.mult, op1=ALU.add).then_inc(s["added"], 1)

        @block.scalar
        def _(act):
            act.sem_inc(s["act_lo_ready"], k2)
            with act.Fori(0, experts) as e:
                act.wait_ge(s["w_in"], e * 48 + 48)
                for m in range(k2):
                    act.wait_ge(s["projected"], e * k2 + m + 1)
                    act.wait_ge(s["act_lo_ready"], e * k2 + k2)
                    for c, (a, b) in enumerate(chunks):
                        last = nc.scalar.activation(act_f[:, m, a:b], ps[:, 3 * m + c, 0:b - a], ACT.Gelu_apprx_tanh,
                                                    bias=bias[:, m:m + 1])
                    last.then_inc(s["act_ready"], 1)

        @block.tensor
        def _(pe):
            with pe.Fori(0, experts) as e:
                pe.wait_ge(s["w1_lo_ready"], e + 1)
                for m in range(k2):
                    for k in range(k1):
                        for n, (w, x) in enumerate(((w1_hi, x_hi), (w1_hi, x_lo), (w1_lo, x_hi))):
                            for c, (a, b) in enumerate(chunks):
                                last = nc.tensor.matmul(ps[:, 3 * m + c, 0:b - a], w[:, k, m * 128:(m + 1) * 128], x[:, k, a:b],
                                                        start=(k == 0 and n == 0), stop=(k == k1 - 1 and n == 2))
                    last.then_inc(s["projected"], 1)
                pe.wait_ge(s["w2_lo_ready"], e + 2)
                pe.wait_ge(s["act_lo_ready"], e * k2 + 2 * k2)
                for t in range(tiles):
                    pe.wait_ge(s["added"], e * tiles + tiles + t - 1)
                    at = slice(t * R, (t + 1) * R)
                    for k in range(k2):
                        for n, (h, w) in enumerate(((act_hi, w2_hi), (act_hi, w2_lo), (act_lo, w2_hi))):
                            last = nc.tensor.matmul(ps[0:R, 6 + t % 2, :], h[:, k, at], w[:, k, :],
                                                    start=(k == 0 and n == 0), stop=(k == k2 - 1 and n == 2))
                    last.then_inc(s["output"], 1)


def constants(nc, ident, zero_hot, x, x_tiles):
    with ExitStack() as ctx:
        sb, banks, sem = tools(nc, ctx, "constants")
        zeroed = sem("zeroed")
        x_in = sem("x_in")
        block = ctx.enter_context(nc.Block())

        @block.sync
        def _(sp):
            sp.dma_start(x_tiles[:, :, :], x.rearrange("(t p) n -> p t n", p=R)).then_inc(x_in, 16)
            sp.wait_ge(x_in, 16)

        @block.gpsimd
        def _(pool):
            nc.gpsimd.memset(ident[:, :], 0.0).then_inc(zeroed, 1)
            nc.gpsimd.memset(zero_hot[:, :], 0.0)
            pool.wait_ge(zeroed, 1)
            nc.gpsimd.affine_select(out=ident[:, :], in_=ident[:, :], compare_op=ALU.not_equal, fill=1.0,
                                    base=0, pattern=[[-1, 128]], channel_multiplier=1)


def graph_transformer(nc, a, out):
    n_nodes, width = a["x"].shape
    tiles = n_nodes // R
    blocks = width // 128
    heads, _, depth = a["L0_mix_base_centers"].shape
    experts = a["L0_ffn_W1"].shape[0]
    padded = (n_nodes + 7) // 8 * 8
    eps = 1e-5
    attended = nc.dram_tensor("attended", (heads, depth + 1, padded), F32, kind="Internal").ap()
    with ExitStack() as ctx:
        sb, banks, sem = tools(nc, ctx, "layer")
        ident = sb("ident", [128, 128])
        with ExitStack() as first:
            sb, banks, sem = tools(nc, first, "mixers")
            kept = sb("kept", [128, blocks, n_nodes])
            with ExitStack() as own:
                sb, banks, sem = tools(nc, own, "inputs")
                x_hi = sb("x_hi", [128, blocks, n_nodes], F32R)
                x_lo = sb("x_lo", [128, blocks, n_nodes], F32R)
                with ExitStack() as graph:
                    sb, banks, sem = tools(nc, graph, "edges")
                    zero_hot = sb("zero_hot", [R, 512], F16)
                    x_tiles = sb("x_tiles", [R, tiles, width])
                    adj = sb("adj", [R, tiles, n_nodes])
                    dinv = sb("dinv", [R, tiles])
                    constants(nc, ident, zero_hot, a["x"], x_tiles)
                    turn_normalised(nc, "norm1", x_tiles, ident, x_hi, x_lo, eps)
                    adjacency(nc, a["src"], a["dst"], ident, zero_hot, adj, dinv)
                    graph_layers(nc, x_hi, x_lo, adj, dinv, [a[f"L0_gnn_W{n}"] for n in (1, 2, 3)],
                                 [a[f"L0_gnn_b{n}"] for n in (1, 2, 3)], kept)
                attention(nc, {k[len("L0_mix_"):]: v for k, v in a.items() if k.startswith("L0_mix_")}, ident, x_hi, x_lo, attended)
            second = ctx.enter_context(ExitStack())
            sb, banks, sem = tools(nc, first, "residual")
            x_new = sb("x_new", [R, tiles, width])
            combine(nc, a["x"], attended, a["L0_gnn_W4"], a["L0_gnn_b4"], a["L0_mix_out_w"], ident, kept, x_new)
            sb, banks, sem = tools(nc, first, "mixture")
            unit = sb("unit", [R, tiles, width])
            mixed = sb("mixed", [R, tiles, width])
            share = sb("share", [R, tiles, experts])
            f_hi = sb("f_hi", [128, blocks, n_nodes], F32R)
            f_lo = sb("f_lo", [128, blocks, n_nodes], F32R)
            normalise(nc, "norm2", x_new, unit, eps)
            turn_normalised(nc, "norm3", unit, ident, f_hi, f_lo, eps, a["L0_ffn_ln_g"], a["L0_ffn_ln_b"])
            gate(nc, f_hi, f_lo, a["L0_ffn_Wg"], a["L0_ffn_b2"], ident, unit, share, mixed)
            experts_mix(nc, f_hi, f_lo, a["L0_ffn_W1"], a["L0_ffn_b1"], a["L0_ffn_W2"], share, mixed)
            normalise(nc, "norm4", mixed, unit, eps, a["L0_ffn_out_g"], a["L0_ffn_out_b"], x_new, out)


INPUTS = (["x", "src", "dst"] + [f"L0_gnn_{w}{n}" for n in (1, 2, 3, 4) for w in "Wb"]
          + ["L0_mix_" + n for n in ("base_centers", "center_deltas", "log_scales", "log_amps", "movement_scale_param",
                                     "temperature", "qkv_w", "out_w")]
          + ["L0_ffn_" + n for n in ("Wg", "W1", "b1", "W2", "b2", "ln_g", "ln_b", "out_g", "out_b")])


def kernel(**inputs):
    import numpy as np
    import concourse.bacc as bacc
    from concourse.bass_utils import run_bass_kernel_spmd as run

    nc = bacc.Bacc("TRN2", target_bir_lowering=False, num_devices=1)
    arrays = {f"in_{name}": np.ascontiguousarray(inputs[name]) for name in INPUTS}
    args = {name[3:]: nc.dram_tensor(name, v.shape, mybir.dt.from_np(v.dtype), kind="ExternalInput").ap()
            for name, v in arrays.items()}
    out = nc.dram_tensor("out_0", inputs["x"].shape, F32, kind="ExternalOutput").ap()
    graph_transformer(nc, args, out)
    return run(nc, [arrays], core_ids=[0]).results[0]["out_0"]
```

```python
from contextlib import ExitStack
import concourse.bass as bass
from concourse import mybir
ALU = mybir.AluOpType
ACT = mybir.ActivationFunctionType
AX = mybir.AxisListType
F32 = mybir.dt.float32
F32R = mybir.dt.float32r
F16 = mybir.dt.float16
I32 = mybir.dt.int32

R = 125
DUO = 2
ROUND = 12582912.0


def tools(nc, ctx, phase):
    def sb(name, shape, dtype=F32):
        return ctx.enter_context(nc.sbuf_tensor(f"{phase}_{name}", shape, dtype))

    def banks(name, count):
        return ctx.enter_context(nc.psum_tensor(f"{phase}_{name}", [128, count, 512], F32))

    def sem(name):
        return ctx.enter_context(nc.semaphore(f"{phase}_{name}"))
    return sb, banks, sem


def cleared_semaphores(nc, ctx, phase):
    taken = []

    def give_back():
        nc.clear_and_free_semaphores(taken)
        nc.all_engine_barrier()

    def sem(name):
        taken.append(nc.alloc_semaphore(f"{phase}_{name}"))
        return taken[-1]
    ctx.callback(give_back)
    return sem


def adjacency(nc, src, dst, ident, zero_hot, adj, dinv):
    n_nodes = adj.shape[2]
    tiles = n_nodes // R
    groups = src.shape[0] // (DUO * R)
    rows_in = groups // 2
    visits = 6
    part = 250
    with ExitStack() as ctx:
        sb, banks, sem = tools(nc, ctx, "adjacency")
        src_i = sb("src_i", [rows_in, 2 * DUO * R], I32)
        dst_i = sb("dst_i", [rows_in, 2 * DUO * R], I32)
        src_f = sb("src_f", [rows_in, 2 * DUO * R])
        dst_f = sb("dst_f", [rows_in, 2 * DUO * R])
        src_col = sb("src_col", [R, DUO, 2 * groups + 2 * visits])
        dst_col = sb("dst_col", [R, DUO, 2 * groups + 2 * visits])
        node_row = sb("node_row", [R, n_nodes], F16)
        block_row = sb("block_row", [rows_in, 2, tiles])
        group_col = sb("group_col", [rows_in, 2, tiles])
        low = sb("low", [rows_in, 2])
        low_end = sb("low_end", [rows_in, 2])
        high = sb("high", [rows_in, 2])
        begins = sb("begins", [rows_in, 2, tiles])
        ends = sb("ends", [rows_in, 2, tiles])
        touches = sb("touches", [rows_in, 2, tiles])
        first_less = sb("first_less", [rows_in, 2, tiles])
        last_less = sb("last_less", [rows_in, 2, tiles])
        candidates = sb("candidates", [rows_in, 2, 2 * tiles])
        extreme = sb("extreme", [2 * tiles, 1])
        bounds_f = sb("bounds_f", [1, 2 * tiles])
        span_f = sb("span_f", [1, 4, tiles])
        bounds = sb("bounds", [1, 2 * tiles], I32)
        src_hot = sb("src_hot", [R, visits * DUO, n_nodes], F16)
        dst_hot = sb("dst_hot", [R, visits * DUO, R], F16)
        rows = sb("rows", [R, 3, n_nodes])
        degree = sb("degree", [R, tiles])
        root = sb("root", [R, tiles])
        ps = banks("ps", 8)

        def count_rows(b):
            first = 3 * (b % 2)
            return ps[0:R, first:first + 3, :].rearrange("p a (c n) -> p (a c) n", n=256)[:, 0:5, 0:part]

        edges_in = sem("edges_in")
        iotas = sem("iotas")
        edge_f = sem("edge_f")
        edge_turned = sem("edge_turned")
        edge_cols = sem("edge_cols")
        range_step = sem("range_step")
        cand_ready = sem("cand_ready")
        cand_turned = sem("cand_turned")
        extreme_ready = sem("extreme_ready")
        extreme_turned = sem("extreme_turned")
        bounds_ready = sem("bounds_ready")
        hot_ready = sem("hot_ready")
        hot_free = sem("hot_free")
        counted = sem("counted")
        counts_out = sem("counts_out")
        loops_in = sem("loops_in")
        root_ready = sem("root_ready")
        dinv_ready = sem("dinv_ready")
        rows_scaled = sem("rows_scaled")
        block_turned = sem("block_turned")
        block_out = sem("block_out")
        block = ctx.enter_context(nc.Block())
        turn_groups = [(0, 4), (4, 8), (8, tiles)]

        @block.sync
        def _(sp):
            sp.dma_start(src_i[:, :], src.rearrange("(g e) -> g e", e=2 * DUO * R)).then_inc(edges_in, 16)
            sp.dma_start(dst_i[:, :], dst.rearrange("(g e) -> g e", e=2 * DUO * R)).then_inc(edges_in, 16)

        @block.gpsimd
        def _(pool):
            nc.gpsimd.iota(node_row[:, :], [[1, n_nodes]], base=0, channel_multiplier=0,
                           allow_small_or_imprecise_dtypes=True).then_inc(iotas, 1)
            nc.gpsimd.iota(block_row[:, :, :], [[0, 2], [R, tiles]], base=0, channel_multiplier=0,
                           allow_small_or_imprecise_dtypes=True).then_inc(iotas, 1)
            nc.gpsimd.iota(group_col[:, :, :], [[1, 2], [0, tiles]], base=0, channel_multiplier=2,
                           allow_small_or_imprecise_dtypes=True).then_inc(iotas, 1)
            for tile in (src_col, dst_col):
                nc.gpsimd.memset(tile[:, :, :], -1.0).then_inc(iotas, 1)
            for b in range(tiles):
                own = rows[:, b % 3, b * R:(b + 1) * R]
                pool.wait_ge(counts_out, b + 1)
                nc.gpsimd.tensor_tensor(own, own, ident[0:R, 0:R], ALU.add).then_inc(loops_in, 1)

        @block.vector
        def _(dve):
            dve.wait_ge(edges_in, 32)
            nc.vector.tensor_copy(src_f[:, :], src_i[:, :]).then_inc(edge_f, 1)
            nc.vector.tensor_copy(dst_f[:, :], dst_i[:, :]).then_inc(edge_f, 1)
            dve.wait_ge(edge_f, 2)
            count = [0]

            def link(instruction):
                count[0] += 1
                instruction.then_inc(range_step, 1)
                dve.wait_ge(range_step, count[0])

            by_group = dst_f[:, :].rearrange("p (g e) -> p g e", g=2)
            link(nc.vector.tensor_reduce(low[:, :], by_group, AX.X, ALU.min))
            link(nc.vector.tensor_reduce(high[:, :], by_group, AX.X, ALU.max))
            dve.wait_ge(iotas, 5)
            link(nc.vector.tensor_scalar(first_less[:, :, :], group_col[:, :, :], -float(groups), None, ALU.add))
            link(nc.vector.tensor_scalar(last_less[:, :, :], group_col[:, :, :], -1.0, -1.0, ALU.mult, ALU.add))
            link(nc.vector.tensor_scalar(low_end[:, :], low[:, :], -float(R - 1), None, ALU.add))
            for g in range(2):
                link(nc.vector.tensor_scalar(begins[:, g, :], block_row[:, g, :], low_end[:, g:g + 1], None, ALU.is_ge))
                link(nc.vector.tensor_scalar(ends[:, g, :], block_row[:, g, :], high[:, g:g + 1], None, ALU.is_le))
            link(nc.vector.tensor_tensor(touches[:, :, :], begins[:, :, :], ends[:, :, :], ALU.mult))
            nc.vector.tensor_tensor(candidates[:, :, 0:tiles], touches[:, :, :], first_less[:, :, :], ALU.mult).then_inc(cand_ready, 1)
            nc.vector.tensor_tensor(candidates[:, :, tiles:2 * tiles], touches[:, :, :], last_less[:, :, :], ALU.mult).then_inc(cand_ready, 1)
            for n, col in enumerate((src_col, dst_col)):
                dve.wait_ge(edge_turned, n + 1)
                for g in range(2):
                    for q in range(DUO):
                        at = (g * DUO + q) * rows_in
                        last = nc.vector.tensor_copy(col[:, q, g:groups:2], ps[0:R, 2 + n, at:at + rows_in])
                last.then_inc(edge_cols, 1)
            dve.wait_ge(cand_turned, 1)
            nc.vector.tensor_reduce(extreme[:, :], ps[0:2 * tiles, 0, 0:groups], AX.X, ALU.min).then_inc(extreme_ready, 1)
            dve.wait_ge(extreme_turned, 1)
            link(nc.vector.tensor_scalar(bounds_f[:, 0:tiles], ps[0:1, 1, 0:tiles], float(groups), float(groups - 1), ALU.add, ALU.min))
            link(nc.vector.tensor_scalar(span_f[:, 0, :], ps[0:1, 1, tiles:2 * tiles], -1.0, None, ALU.mult))
            link(nc.vector.tensor_tensor(span_f[:, 1, :], span_f[:, 0, :], bounds_f[:, 0:tiles], ALU.subtract))
            link(nc.vector.tensor_scalar(span_f[:, 2, :], span_f[:, 1, :], 1.0 / visits, 0.5 - 0.5 / visits, ALU.mult, ALU.add))
            link(nc.vector.tensor_scalar(span_f[:, 3, :], span_f[:, 2, :], ROUND, None, ALU.add))
            link(nc.vector.tensor_scalar(bounds_f[:, tiles:2 * tiles], span_f[:, 3, :], -ROUND, 1.0, ALU.add, ALU.max))
            nc.vector.tensor_copy(bounds[:, :], bounds_f[:, :]).then_inc(bounds_ready, 1)
            dve.wait_ge(edge_cols, 2)
            dve.wait_ge(bounds_ready, 1)
            before = 0
            for b in range(tiles):
                start = dve.value_load(bounds[0:1, b:b + 1], min_val=0, max_val=groups - 1)
                rounds = dve.value_load(bounds[0:1, tiles + b:tiles + b + 1], min_val=1, max_val=groups // visits + 1)
                with dve.Fori(0, rounds) as k:
                    first = dve.snap(start + k * visits)
                    free = dve.snap((before + k) * visits)
                    for v in range(visits):
                        dve.wait_ge(hot_free, free + (v + 1))
                        for q in range(DUO):
                            nc.vector.tensor_scalar(src_hot[:, DUO * v + q, :], node_row[:, :], src_col[:, q, bass.ds(first + v, 1)],
                                                    None, ALU.is_equal)
                            last = nc.vector.tensor_scalar(dst_hot[:, DUO * v + q, :], node_row[:, b * R:(b + 1) * R],
                                                           dst_col[:, q, bass.ds(first + v, 1)], None, ALU.is_equal)
                        last.then_inc(hot_ready, 1)
                before = dve.snap(before + rounds)
                if b >= 1:
                    dve.wait_ge(root_ready, b)
                    nc.vector.reciprocal(dinv[:, b - 1:b], root[:, b - 1:b]).then_inc(dinv_ready, 1)
            dve.wait_ge(root_ready, tiles)
            nc.vector.reciprocal(dinv[:, tiles - 1:tiles], root[:, tiles - 1:tiles]).then_inc(dinv_ready, 1)

        @block.scalar
        def _(act):
            def scale_rows(b):
                act.wait_ge(loops_in, b + 1)
                act.wait_ge(dinv_ready, b + 1)
                nc.scalar.mul(rows[:, b % 3, :], rows[:, b % 3, :], dinv[:, b:b + 1]).then_inc(rows_scaled, 1)

            def blocks_out(b):
                for n, (t0, t1) in enumerate(turn_groups):
                    act.wait_ge(block_turned, 3 * b + n + 1)
                    nc.scalar.copy(adj[:, t0:t1, b * R:(b + 1) * R],
                                   ps[0:R, 6 + (b + n) % 2, 0:(t1 - t0) * R].rearrange("p (t n) -> p t n", n=R)).then_inc(block_out, 1)

            for b in range(tiles):
                if b >= 2:
                    blocks_out(b - 2)
                act.wait_ge(counted, b + 1)
                if b >= 3:
                    act.wait_ge(block_turned, 3 * (b - 2))
                nc.scalar.activation(rows[:, b % 3, :].rearrange("p (c n) -> p c n", n=part), count_rows(b),
                                     ACT.Identity, accum_out=degree[:, b:b + 1]).then_inc(counts_out, 1)
                act.wait_ge(counts_out, b + 1)
                nc.scalar.activation(root[:, b:b + 1], degree[:, b:b + 1], ACT.Sqrt, bias=1.0).then_inc(root_ready, 1)
                if b >= 1:
                    scale_rows(b - 1)
            scale_rows(tiles - 1)
            blocks_out(tiles - 2)
            blocks_out(tiles - 1)

        @block.tensor
        def _(pe):
            pe.wait_ge(edge_f, 2)
            for n, edges in enumerate((src_f, dst_f)):
                for q in range(2 * DUO):
                    last = nc.tensor.transpose(ps[0:R, 2 + n, q * rows_in:(q + 1) * rows_in], edges[:, q * R:(q + 1) * R],
                                               ident[0:rows_in, 0:rows_in])
                last.then_inc(edge_turned, 1)
            pe.wait_ge(cand_ready, 2)
            for g in range(2):
                last = nc.tensor.transpose(ps[0:2 * tiles, 0, g * rows_in:(g + 1) * rows_in], candidates[:, g, :],
                                           ident[0:rows_in, 0:rows_in])
            last.then_inc(cand_turned, 1)
            pe.wait_ge(extreme_ready, 1)
            nc.tensor.transpose(ps[0:1, 1, 0:2 * tiles], extreme[:, :], ident[0:2 * tiles, 0:2 * tiles]).then_inc(extreme_turned, 1)
            pe.wait_ge(bounds_ready, 1)
            pe.wait_ge(edge_cols, 2)
            pe.sem_inc(hot_free, visits)

            def turn(b):
                pe.wait_ge(rows_scaled, b + 1)
                for n, (t0, t1) in enumerate(turn_groups):
                    g = 3 * b + n
                    if g >= 2:
                        pe.wait_ge(block_out, g - 1)
                    for t in range(t0, t1):
                        last = nc.tensor.transpose(ps[0:R, 6 + (b + n) % 2, (t - t0) * R:(t - t0 + 1) * R],
                                                   rows[:, b % 3, t * R:(t + 1) * R], ident[0:R, 0:R])
                    last.then_inc(block_turned, 1)

            before = 0
            for b in range(tiles):
                if b >= 2:
                    pe.wait_ge(counts_out, b - 1)
                    turn(b - 2)
                rounds = pe.value_load(bounds[0:1, tiles + b:tiles + b + 1], min_val=1, max_val=groups // visits + 1)
                first = 3 * (b % 2)
                for c, width in enumerate((512, 512, 256)):
                    nc.tensor.matmul(ps[0:R, first + c, 0:width], zero_hot[:, 0:R], zero_hot[:, 0:width], start=True,
                                     stop=False, skip_group_check=True)
                with pe.Fori(0, rounds) as k:
                    ready = pe.snap((before + k) * visits)
                    for v in range(visits):
                        pe.wait_ge(hot_ready, ready + (v + 1))
                        for q in range(DUO * v, DUO * v + DUO):
                            for c in range(5):
                                last = nc.tensor.matmul(count_rows(b)[:, c, :], dst_hot[:, q, :],
                                                        src_hot[:, q, c * part:(c + 1) * part],
                                                        start=False, stop=False, skip_group_check=True)
                        last.then_inc(hot_free, 1)
                before = pe.snap(before + rounds)
                nc.tensor.matmul(ps[0:R, first, 0:256], zero_hot[:, 0:R], zero_hot[:, 0:256], start=False, stop=True,
                                 skip_group_check=True).then_inc(counted, 1)
            turn(tiles - 2)
            turn(tiles - 1)

def turn_normalised(nc, name, x_tiles, ident, turned_hi, turned_lo, eps, gain=None, offset=None):
    tiles = x_tiles.shape[1]
    width = x_tiles.shape[2]
    blocks = width // 128
    with ExitStack() as ctx:
        sb, banks, sem = tools(nc, ctx, name)
        stats = sb("stats", [R, 2, 6])
        moments = sb("moments", [R, tiles, 2])
        root = sb("root", [R, tiles])
        scale = sb("scale", [R, tiles])
        eps_col = sb("eps_col", [R, 1])
        unit = sb("unit", [R, 2, width])
        affine = sb("affine", [128, 2, blocks * R])
        gains = sb("gains", [128, 2, blocks])
        ps = banks("ps", 2)
        eps_in = sem("eps_in")
        stats_ready = sem("stats_ready")
        moments_ready = sem("moments_ready")
        root_ready = sem("root_ready")
        scale_ready = sem("scale_ready")
        unit_ready = sem("unit_ready")
        turned = sem("turned")
        hi_ready = sem("hi_ready")
        lo_ready = sem("lo_ready")
        gains_in = sem("gains_in")
        affine_ready = sem("affine_ready")
        block = ctx.enter_context(nc.Block())

        def turned_view(n):
            return ps[:, n % 2, 0:blocks * R].rearrange("p (k n) -> p k n", n=R)

        @block.sync
        def _(sp):
            for n, row in enumerate((gain, offset)):
                if row is not None:
                    sp.dma_start(gains[:, n, :], row.rearrange("(k p) -> p k", p=128),
                                 allow_slow_non_contiguous=True).then_inc(gains_in, 16)

        @block.gpsimd
        def _(pool):
            nc.gpsimd.memset(eps_col[:, :], eps).then_inc(eps_in, 1)

        @block.vector
        def _(dve):
            for t in range(tiles):
                if t >= 2:
                    dve.wait_ge(moments_ready, t - 1)
                nc.vector.bn_stats(stats[:, t % 2, :], x_tiles[:, t, :]).then_inc(stats_ready, 1)
                dve.wait_ge(stats_ready, t + 1)
                nc.vector.bn_aggr(moments[:, t, :], stats[:, t % 2, :]).then_inc(moments_ready, 1)
            dve.wait_ge(root_ready, 1)
            nc.vector.reciprocal(scale[:, :], root[:, :]).then_inc(scale_ready, 1)
            dve.wait_ge(scale_ready, 1)
            for t in range(tiles + 1):
                if t < tiles:
                    if t >= 2:
                        dve.wait_ge(turned, t - 1)
                    nc.vector.tensor_scalar(unit[:, t % 2, :], x_tiles[:, t, :], moments[:, t, 0:1], scale[:, t:t + 1],
                                            ALU.subtract, ALU.mult).then_inc(unit_ready, 1)
                if t >= 1:
                    n = t - 1
                    at = slice(n * R, (n + 1) * R)
                    dve.wait_ge(hi_ready, n + 1)
                    whole = turned_view(n) if gain is None else affine[:, n % 2, :].rearrange("p (k n) -> p k n", n=R)
                    nc.vector.tensor_tensor(turned_lo[:, :, at], whole, turned_hi[:, :, at].bitcast(F32),
                                            ALU.subtract).then_inc(lo_ready, 1)

        @block.scalar
        def _(act):
            act.wait_ge(moments_ready, tiles)
            act.wait_ge(eps_in, 1)
            nc.scalar.activation(root[:, :], moments[:, :, 1], ACT.Sqrt, bias=eps_col[:, 0:1]).then_inc(root_ready, 1)
            for t in range(tiles):
                act.wait_ge(turned, t + 1)
                whole = turned_view(t)
                if gain is not None:
                    act.wait_ge(gains_in, 32)
                    if t >= 2:
                        act.wait_ge(lo_ready, t - 1)
                    whole = affine[:, t % 2, :].rearrange("p (k n) -> p k n", n=R)
                    for k in range(blocks):
                        last = nc.scalar.activation(whole[:, k, :], turned_view(t)[:, k, :], ACT.Identity,
                                                    scale=gains[:, 0, k:k + 1], bias=gains[:, 1, k:k + 1])
                    last.then_inc(affine_ready, 1)
                    act.wait_ge(affine_ready, t + 1)
                nc.scalar.copy(turned_hi[:, :, t * R:(t + 1) * R], whole).then_inc(hi_ready, 1)

        @block.tensor
        def _(pe):
            for t in range(tiles):
                pe.wait_ge(unit_ready, t + 1)
                if t >= 2:
                    pe.wait_ge(lo_ready, t - 1)
                for k in range(blocks):
                    last = nc.tensor.transpose(turned_view(t)[:, k, :], unit[:, t % 2, k * 128:(k + 1) * 128],
                                               ident[0:R, 0:R])
                last.then_inc(turned, 1)


def spans(width, step):
    return [(a, min(a + step, width)) for a in range(0, width, step)]


def graph_layers(nc, turned_hi, turned_lo, adj, dinv, weights, biases, kept):
    n_nodes = adj.shape[2]
    tiles = n_nodes // R
    chunks = spans(n_nodes, 500)
    sizes = [tuple(w.shape) for w in weights]
    with ExitStack() as ctx:
        sb, banks, sem = tools(nc, ctx, "graph")
        w1 = sb("w1", [128, sizes[0][0] // 128, sizes[0][1]])
        w1_hi = sb("w1_hi", [128, sizes[0][0] // 128, sizes[0][1]], F32R)
        w1_lo = sb("w1_lo", [128, sizes[0][0] // 128, sizes[0][1]], F32R)
        w2 = sb("w2", [128, sizes[1][0] // 128, sizes[1][1]])
        w3 = sb("w3", [128, sizes[2][0] // 128, sizes[2][1]])
        bias = sb("bias", [128, 4])
        projected = sb("projected", [R, tiles, sizes[0][1]])
        ps = banks("ps", 8)
        w1_in = sem("w1_in")
        w_in = sem("w_in")
        w1_part = sem("w1_part")
        rows_done = sem("rows_done")
        rows_out = sem("rows_out")
        gathered = sem("gathered")
        kept_ready = sem("kept_ready")
        block = ctx.enter_context(nc.Block())
        layers = [(None, 4, None, 2, 0), (w2, 2, 0, 1, 2), (w3, 1, 2, 1, 3)]

        @block.sync
        def _(sp):
            sp.dma_start(w1[:, :, :], weights[0].rearrange("(k p) n -> p k n", p=128)).then_inc(w1_in, 16)
            sp.dma_start(w2[:, :, :], weights[1].rearrange("(k p) n -> p k n", p=128)).then_inc(w_in, 16)
            sp.dma_start(w3[:, :, :], weights[2].rearrange("(k p) n -> p k n", p=128)).then_inc(w_in, 16)
            at = 0
            for b in biases:
                m = b.shape[0] // 128
                sp.dma_start(bias[:, at:at + m], b.rearrange("(m p) -> p m", p=128),
                             allow_slow_non_contiguous=True).then_inc(w_in, 16)
                at += m

        @block.vector
        def _(dve):
            dve.wait_ge(w1_in, 16)
            nc.vector.tensor_copy(w1_hi[:, :, :], w1[:, :, :]).then_inc(w1_part, 1)
            dve.wait_ge(w1_part, 1)
            nc.vector.tensor_tensor(w1_lo[:, :, :], w1[:, :, :], w1_hi[:, :, :].bitcast(F32), ALU.subtract).then_inc(w1_part, 1)
            done = 0
            for n in range(3):
                wide = sizes[n][1]
                for t in range(tiles):
                    dve.wait_ge(rows_done, done + 1)
                    if n and t == 0:
                        dve.wait_ge(gathered, (2, 3)[n - 1])
                    nc.vector.tensor_scalar(projected[:, t, 0:wide], ps[0:R, 6 + t % 2, 0:wide], dinv[:, t:t + 1], None,
                                            ALU.mult).then_inc(rows_out, 1)
                    done += 1

        @block.scalar
        def _(act):
            act.wait_ge(w_in, 16 * 5)
            done = 0
            for n in range(3):
                _, _, _, out_blocks, first = layers[n]
                for m in range(out_blocks):
                    act.wait_ge(gathered, done + 1)
                    for c, (a, b) in enumerate(chunks):
                        nc.scalar.activation(kept[:, first + m, a:b], ps[:, 3 * (done % 2) + c, 0:b - a], ACT.Relu,
                                             bias=bias[:, first + m:first + m + 1]).then_inc(kept_ready, 1)
                    done += 1

        @block.tensor
        def _(pe):
            pe.wait_ge(w1_part, 2)
            pe.wait_ge(w_in, 16 * 5)
            rows = 0
            done = 0
            for n in range(3):
                w, depth, source, out_blocks, first = layers[n]
                wide = sizes[n][1]
                if n:
                    pe.wait_ge(kept_ready, len(chunks) * done)
                for t in range(tiles):
                    if rows >= 2:
                        pe.wait_ge(rows_out, rows - 1)
                    to = ps[0:R, 6 + t % 2, 0:wide]
                    at = slice(t * R, (t + 1) * R)
                    for k in range(depth):
                        if n:
                            last = nc.tensor.matmul(to, kept[:, source + k, at], w[:, k, :],
                                                    start=(k == 0), stop=(k == depth - 1))
                        else:
                            nc.tensor.matmul(to, turned_hi[:, k, at], w1_hi[:, k, :], start=(k == 0), stop=False)
                            nc.tensor.matmul(to, turned_hi[:, k, at], w1_lo[:, k, :], start=False, stop=False)
                            last = nc.tensor.matmul(to, turned_lo[:, k, at], w1_hi[:, k, :],
                                                    start=False, stop=(k == depth - 1))
                    last.then_inc(rows_done, 1)
                    rows += 1
                for m in range(out_blocks):
                    if done >= 2:
                        pe.wait_ge(kept_ready, len(chunks) * (done - 1))
                    for t in range(tiles):
                        if m == 0:
                            pe.wait_ge(rows_out, rows - tiles + t + 1)
                        for c, (a, b) in enumerate(chunks):
                            last = nc.tensor.matmul(ps[:, 3 * (done % 2) + c, 0:b - a], projected[:, t, m * 128:(m + 1) * 128],
                                                    adj[:, t, a:b], start=(t == 0), stop=(t == tiles - 1))
                    last.then_inc(gathered, 1)
                    done += 1

PAIR = 128
CODES = 64


def splat_constants(nc, a, ident, center_hi, center_lo, columns, part_mask, head_sum, inv_temp):
    heads, splats, depth = a["base_centers"].shape
    pairs = heads // 2
    with ExitStack() as ctx:
        sb, banks, sem = tools(nc, ctx, "splats")
        base = sb("base", [128, pairs, 128])
        delta = sb("delta", [128, pairs, 128])
        log_scale = sb("log_scale", [128, pairs])
        log_amp = sb("log_amp", [128, pairs])
        move = sb("move", [128, 1])
        move_exp = sb("move_exp", [128, 1])
        move_one = sb("move_one", [128, 1])
        move_rec = sb("move_rec", [128, 1])
        move_by = sb("move_by", [128, 1])
        temp = sb("temp", [R, 1])
        temp_max = sb("temp_max", [R, 1])
        centers = sb("centers", [128, pairs, 128])
        squares = sb("squares", [128, pairs, 128])
        center_sq = sb("center_sq", [128, pairs])
        scales = sb("scales", [128, pairs])
        clipped = sb("clipped", [128, pairs])
        scale_sq = sb("scale_sq", [128, pairs])
        var_eps = sb("var_eps", [128, pairs])
        inv_var = sb("inv_var", [128, pairs])
        amps = sb("amps", [128, pairs])
        kept_amp = sb("kept_amp", [128, pairs])
        mask_rows = sb("mask_rows", [1, 3, 128])
        keep_rows = sb("keep_rows", [128, 1])
        center_f = sb("center_f", [128, pairs, 128])
        ps = banks("ps", 2)
        cleared = sem("cleared")
        loaded = sem("loaded")
        exps = sem("exps")
        step = sem("step")
        centers_ready = sem("centers_ready")
        centers_turned = sem("centers_turned")
        masks_turned = sem("masks_turned")
        halved = sem("halved")
        block = ctx.enter_context(nc.Block())

        @block.gpsimd
        def _(pool):
            for tile in (base, delta):
                nc.gpsimd.memset(tile[:, :, :], 0.0)
            nc.gpsimd.memset(log_scale[:, :], 0.0)
            nc.gpsimd.memset(log_amp[:, :], 0.0)
            nc.gpsimd.memset(mask_rows[:, :, :], 0.0)
            nc.gpsimd.memset(head_sum[:, :].bitcast(F32), 0.0).then_inc(cleared, 1)
            pool.wait_ge(cleared, 1)
            for h in range(2):
                at = CODES * h
                nc.gpsimd.memset(mask_rows[:, 0, at + splats:at + 2 * splats], 1.0)
                nc.gpsimd.memset(mask_rows[:, 1, at + 2 * splats:at + 3 * splats], 1.0)
                nc.gpsimd.memset(mask_rows[:, 2, at:at + 3 * splats], 1.0)
                last = nc.gpsimd.memset(head_sum[depth * h:depth * (h + 1), at:at + 3 * splats].bitcast(F32), 1.0)
            last.then_inc(cleared, 1)

        @block.sync
        def _(sp):
            sp.wait_ge(cleared, 1)
            for h in range(2):
                for r in range(3):
                    rows = slice(CODES * h + splats * r, CODES * h + splats * (r + 1))
                    own = slice(depth * h, depth * (h + 1))
                    for to, name in ((base, "base_centers"), (delta, "center_deltas")):
                        sp.dma_start(to[rows, :, own], a[name].rearrange("(p h) s d -> h s p d", h=2)[h]).then_inc(loaded, 16)
                    for to, name in ((log_scale, "log_scales"), (log_amp, "log_amps")):
                        sp.dma_start(to[rows, :], a[name].rearrange("(p h) s -> h s p", h=2)[h],
                                     allow_slow_non_contiguous=True).then_inc(loaded, 16)
            sp.dma_start(move[:, :], a["movement_scale_param"].partition_broadcast(128)).then_inc(loaded, 16)
            sp.dma_start(temp[:, :], a["temperature"].partition_broadcast(R)).then_inc(loaded, 16)

        @block.scalar
        def _(act):
            act.wait_ge(loaded, 16 * 26)
            nc.scalar.activation(move_exp[:, :], move[:, :], ACT.Exp, scale=-1.0).then_inc(exps, 1)
            nc.scalar.activation(scales[:, :], log_scale[:, :], ACT.Exp).then_inc(exps, 1)
            nc.scalar.activation(amps[:, :], log_amp[:, :], ACT.Exp).then_inc(exps, 1)
            act.wait_ge(centers_turned, 1)
            nc.scalar.mul(center_hi[:, :, :], ps[:, 0, :].rearrange("p (n m) -> p n m", n=pairs), -2.0)
            nc.scalar.mul(center_f[:, :, :], ps[:, 0, :].rearrange("p (n m) -> p n m", n=pairs), -2.0).then_inc(halved, 1)

        @block.vector
        def _(dve):
            count = [0]

            def link(instruction):
                count[0] += 1
                instruction.then_inc(step, 1)
                dve.wait_ge(step, count[0])

            dve.wait_ge(loaded, 16 * 26)
            dve.wait_ge(exps, 3)
            link(nc.vector.tensor_scalar(move_one[:, :], move_exp[:, :], 1.0, None, ALU.add))
            link(nc.vector.reciprocal(move_rec[:, :], move_one[:, :]))
            link(nc.vector.tensor_scalar(move_by[:, :], move_rec[:, :], 0.1, None, ALU.mult))
            link(nc.vector.scalar_tensor_tensor(out=centers[:, :, :], in0=delta[:, :, :], scalar=move_by[:, 0:1],
                                                in1=base[:, :, :], op0=ALU.mult, op1=ALU.add))
            nc.vector.tensor_copy(center_f[:, :, :], centers[:, :, :]).then_inc(centers_ready, 1)
            link(nc.vector.tensor_tensor(squares[:, :, :], centers[:, :, :], centers[:, :, :], ALU.mult))
            link(nc.vector.tensor_reduce(center_sq[:, :], squares[:, :, :], AX.X, ALU.add))
            link(nc.vector.tensor_scalar(clipped[:, :], scales[:, :], 0.0001, 2.0, ALU.max, ALU.min))
            link(nc.vector.tensor_tensor(scale_sq[:, :], clipped[:, :], clipped[:, :], ALU.mult))
            link(nc.vector.tensor_scalar(var_eps[:, :], scale_sq[:, :], 1e-8, None, ALU.add))
            link(nc.vector.reciprocal(inv_var[:, :], var_eps[:, :]))
            link(nc.vector.tensor_scalar(columns[:, 0, :], inv_var[:, :], -0.5, None, ALU.mult))
            link(nc.vector.tensor_tensor(columns[:, 1, :], columns[:, 0, :], center_sq[:, :], ALU.mult))
            link(nc.vector.tensor_scalar(kept_amp[:, :], amps[:, :], 0.02, None, ALU.is_gt))
            link(nc.vector.tensor_tensor(columns[:, 3, :], kept_amp[:, :], amps[:, :], ALU.mult))
            dve.wait_ge(masks_turned, 1)
            link(nc.vector.tensor_scalar(part_mask[:, :], ps[:, 1, 0:2], -1.0, None, ALU.mult))
            link(nc.vector.tensor_copy(keep_rows[:, :], ps[:, 1, 2:3]))
            link(nc.vector.tensor_scalar(columns[:, 2, :], columns[:, 3, :], keep_rows[:, 0:1], None, ALU.mult))
            link(nc.vector.tensor_scalar(temp_max[:, :], temp[:, :], 0.1, None, ALU.max))
            link(nc.vector.reciprocal(inv_temp[:, :], temp_max[:, :]))
            dve.wait_ge(halved, 1)
            nc.vector.tensor_tensor(center_lo[:, :, :], center_f[:, :, :], center_hi[:, :, :].bitcast(F32), ALU.subtract)

        @block.tensor
        def _(pe):
            pe.wait_ge(cleared, 2)
            for n in range(3):
                last = nc.tensor.matmul(ps[:, 1, n:n + 1], mask_rows[:, n, :], ident[0:1, 0:1], start=True, stop=True)
            last.then_inc(masks_turned, 1)
            pe.wait_ge(centers_ready, 1)
            for p in range(pairs):
                last = nc.tensor.transpose(ps[:, 0, p * 128:(p + 1) * 128], center_f[:, p, :], ident[:, :])
            last.then_inc(centers_turned, 1)


def attention(nc, a, ident, x_hi, x_lo, attended):
    n_nodes = x_hi.shape[2]
    tiles = n_nodes // R
    pairs = a["base_centers"].shape[0] // 2
    splats = a["base_centers"].shape[1]
    depth = a["base_centers"].shape[2]
    features = x_hi.shape[1] * 128
    blocks = x_hi.shape[1]
    wide = attended.shape[2]
    quarter = wide // 4
    part = n_nodes // 5
    with ExitStack() as ctx:
        sb, banks, sem = tools(nc, ctx, "attention")
        center_hi = sb("center_hi", [128, pairs, 128], F32R)
        center_lo = sb("center_lo", [128, pairs, 128], F32R)
        columns = sb("columns", [128, 4, pairs])
        part_mask = sb("part_mask", [128, 2])
        head_sum = sb("head_sum", [128, 128], F32R)
        inv_temp = sb("inv_temp", [R, 1])
        splat_constants(nc, a, ident, center_hi, center_lo, columns, part_mask, head_sum, inv_temp)
        own_hi = sb("own_hi", [128, 128], F32R)
        own_lo = sb("own_lo", [128, 128], F32R)
        own_cols = sb("own_cols", [128, 4])
        raw = sb("raw", [128, 3, features])
        w_hi = sb("w_hi", [128, 3, blocks, 128], F32R)
        w_lo = sb("w_lo", [128, 3, blocks, 128], F32R)
        side_hi = sb("side_hi", [128, 2, n_nodes], F32R)
        side_lo = sb("side_lo", [128, 2, n_nodes], F32R)
        square = sb("square", [128, 2, n_nodes])
        square_hi = sb("square_hi", [128, 2, n_nodes], F32R)
        square_lo = sb("square_lo", [128, 2, n_nodes], F32R)
        weight = sb("weight", [128, n_nodes])
        weight_amp = sb("weight_amp", [128, n_nodes])
        weight_hi = sb("weight_hi", [128, n_nodes], F32R)
        stack = sb("stack", [128, 3, wide], F32R)
        v_turn = sb("v_turn", [128, n_nodes])
        v_hi = sb("v_hi", [R, tiles, 2, depth + 1], F32R)
        v_lo = sb("v_lo", [R, tiles, 2, depth + 1], F32R)
        part_max = sb("part_max", [R, tiles, 2])
        row_max = sb("row_max", [R, tiles])
        shift = sb("shift", [tiles, R])
        shift_hi = sb("shift_hi", [tiles, R], F32R)
        shift_lo = sb("shift_lo", [tiles, R], F32R)
        prob = sb("prob", [R, 2, 2 * quarter])
        prob_hi = sb("prob_hi", [R, 2, 2 * quarter], F32R)
        prob_lo = sb("prob_lo", [R, 2, 2 * quarter], F32R)
        mixed = sb("mixed", [depth + 1, 2, 2 * quarter])
        ps = banks("ps", 8)

        sem = cleared_semaphores(nc, ctx, "attention")
        names = ("ready raw_in raw_free own_in w_turned w_hi_ready w_lo_ready projected squared side_lo_ready "
                 "square_hi_ready square_lo_ready dist_ready weighted amped weight_parted stacked v_copied v_turned v_hi_ready "
                 "v_lo_ready scored reduced max_ready max_turned shift_step shift_in logits_ready prob_ready prob_hi_ready "
                 "prob_lo_ready mixed_out mix_step")
        s = {name: sem(name) for name in names.split()}
        stored = [sem("stored_0"), sem("stored_1")]
        block = ctx.enter_context(nc.Block())

        def five(first_bank):
            return ps[:, first_bank:first_bank + 3, :].rearrange("p a (c n) -> p (a c) n", n=256)[:, 0:5, 0:part]

        def fives(tile):
            return tile.rearrange("p (c n) -> p c n", n=part)

        def pair_of_banks(first, rows):
            return ps[0:rows, first:first + 2, 0:quarter]

        v_groups = [(0, 4), (4, 8), (8, tiles)]

        def v_bank(n, t0, t1):
            return ps[0:R, 6 + n % 2, 0:(t1 - t0) * 128].rearrange("p (t h d) -> p t h d", h=2, d=depth)

        @block.sync
        def _(sp):
            with sp.Fori(0, pairs) as p:
                sp.wait_ge(s["raw_free"], p + 1)
                for n in range(3):
                    sp.dma_start(raw[:, n, :], a["qkv_w"][bass.ds(p * PAIR + n * features, PAIR), :]).then_inc(s["raw_in"], 16)
                for h in range(2):
                    row = CODES * h + 3 * splats
                    sp.wait_ge(s["shift_step"], p * 6 + 3 * h + 3)
                    sp.dma_start(stack[row:row + 1, h, 0:n_nodes].bitcast(F32), shift_hi[:, :].bitcast(F32)).then_inc(s["shift_in"], 16)
                    sp.dma_start(stack[row + 1:row + 2, h, 0:n_nodes].bitcast(F32), shift_lo[:, :].bitcast(F32)).then_inc(s["shift_in"], 16)
                    for half in range(2):
                        g = 2 * h + half
                        sp.wait_ge(s["mixed_out"], p * 4 + g + 2)
                        sp.dma_start(attended[bass.ds(p * 2 + h, 1), :, 2 * quarter * half:2 * quarter * (half + 1)].rearrange("a d n -> (a d) n"),
                                     mixed[:, half, :]).then_inc(stored[half], 16)
            for half in range(2):
                sp.wait_ge(stored[half], 16 * (2 * pairs + 1))

        @block.gpsimd
        def _(pool):
            nc.gpsimd.memset(stack[:, :, :].bitcast(F32), 0.0).then_inc(s["ready"], 1)
            nc.gpsimd.memset(v_hi[:, :, :, :].bitcast(F32), 1.0).then_inc(s["ready"], 1)
            nc.gpsimd.memset(v_lo[:, :, :, :].bitcast(F32), 0.0).then_inc(s["ready"], 1)
            for half in range(2):
                pool.sem_inc(stored[half], 16)
            with pool.Fori(0, pairs) as p:
                pool.wait_ge(s["stacked"], p * 3 + 1)
                nc.gpsimd.tensor_copy(own_hi[:, :], center_hi[:, bass.ds(p, 1), :].rearrange("p a n -> p (a n)").bitcast(F32))
                nc.gpsimd.tensor_copy(own_lo[:, :], center_lo[:, bass.ds(p, 1), :].rearrange("p a n -> p (a n)").bitcast(F32))
                nc.gpsimd.tensor_copy(own_cols[:, :], columns[:, :, bass.ds(p, 1)].rearrange("p c a -> p (c a)")).then_inc(s["own_in"], 1)

        @block.vector
        def _(dve):
            dve.sem_inc(s["stacked"], 1)
            dve.wait_ge(s["ready"], 3)
            with dve.Fori(0, pairs) as p:
                for n in range(3):
                    dve.wait_ge(s["w_hi_ready"], p * 3 + n + 1)
                    nc.vector.tensor_tensor(w_lo[:, n, :, :], ps[:, 6 + n % 2, :].rearrange("p (k n) -> p k n", n=128),
                                            w_hi[:, n, :, :].bitcast(F32), ALU.subtract).then_inc(s["w_lo_ready"], 1)

                def parts(n):
                    dve.wait_ge(s["squared"], p * 2 + n + 1)
                    nc.vector.tensor_tensor(fives(side_lo[:, n, :]), five(0), fives(side_hi[:, n, :]).bitcast(F32),
                                            ALU.subtract).then_inc(s["side_lo_ready"], 1)
                    nc.vector.tensor_copy(square_hi[:, n, :], square[:, n, :]).then_inc(s["square_hi_ready"], 1)
                    dve.wait_ge(s["square_hi_ready"], p * 2 + n + 1)
                    nc.vector.tensor_tensor(square_lo[:, n, :], square[:, n, :], square_hi[:, n, :].bitcast(F32),
                                            ALU.subtract).then_inc(s["square_lo_ready"], 1)

                def stacks(n):
                    dve.wait_ge(s["own_in"], p + 1)
                    dve.wait_ge(s["stacked"], p * 3 + 2 * n + 1)
                    dve.wait_ge(s["weighted"], p * 2 + n + 1)
                    nc.vector.tensor_scalar(weight_amp[:, :], weight[:, :], own_cols[:, 2 + n:3 + n], None, ALU.mult).then_inc(s["amped"], 1)
                    dve.wait_ge(s["amped"], p * 2 + n + 1)
                    nc.vector.tensor_copy(weight_hi[:, :], weight_amp[:, :]).then_inc(s["weight_parted"], 1)
                    dve.wait_ge(s["weight_parted"], p * 2 + n + 1)
                    for to, rows in (((0, slice(0, CODES)), (1, slice(CODES, 2 * CODES))), ((2, slice(0, 2 * CODES)),))[n]:
                        nc.vector.scalar_tensor_tensor(out=stack[rows, to, 0:n_nodes], in0=weight_hi[rows, :].bitcast(F32),
                                                       scalar=part_mask[rows, n:n + 1], in1=weight_amp[rows, :],
                                                       op0=ALU.mult, op1=ALU.add).then_inc(s["stacked"], 1)

                parts(0)
                parts(1)
                stacks(0)
                stacks(1)
                for n, (t0, t1) in enumerate(v_groups):
                    dve.wait_ge(s["v_hi_ready"], p * 3 + n + 1)
                    nc.vector.tensor_tensor(v_lo[:, t0:t1, :, 0:depth], v_bank(n, t0, t1), v_hi[:, t0:t1, :, 0:depth].bitcast(F32),
                                            ALU.subtract).then_inc(s["v_lo_ready"], 1)
                for h in range(2):
                    for t in range(tiles):
                        for half in range(2):
                            g = 2 * t + half
                            dve.wait_ge(s["scored"], p * 4 * tiles + 2 * tiles * h + g + 1)
                            nc.vector.tensor_reduce(part_max[:, t, half:half + 1], pair_of_banks(2 * (g % 2), R), AX.XY, ALU.max).then_inc(s["reduced"], 1)
                    dve.wait_ge(s["reduced"], (p * 4 + 2 * h + 2) * tiles)
                    nc.vector.tensor_reduce(row_max[:, :], part_max[:, :, :], AX.X, ALU.max).then_inc(s["max_ready"], 1)
                    dve.wait_ge(s["max_turned"], p * 2 + h + 1)
                    nc.vector.tensor_scalar(shift[:, :], ps[0:tiles, 0, 0:R], -1.0, None, ALU.mult).then_inc(s["shift_step"], 1)
                    dve.wait_ge(s["shift_step"], p * 6 + 3 * h + 1)
                    nc.vector.tensor_copy(shift_hi[:, :], shift[:, :]).then_inc(s["shift_step"], 1)
                    dve.wait_ge(s["shift_step"], p * 6 + 3 * h + 2)
                    nc.vector.tensor_tensor(shift_lo[:, :], shift[:, :], shift_hi[:, :].bitcast(F32), ALU.subtract).then_inc(s["shift_step"], 1)
                    for n in range(2 * tiles):
                        at = p * 4 * tiles + 2 * tiles * h + n
                        dve.wait_ge(s["prob_hi_ready"], at + 1)
                        if n >= 2:
                            dve.wait_ge(s["mix_step"], at - 1)
                        nc.vector.tensor_tensor(prob_lo[:, n % 2, :], prob[:, n % 2, :], prob_hi[:, n % 2, :].bitcast(F32),
                                                ALU.subtract).then_inc(s["prob_lo_ready"], 1)

        @block.scalar
        def _(act):
            act.sem_inc(s["mixed_out"], 1)
            act.wait_ge(s["ready"], 3)
            with act.Fori(0, pairs) as p:
                for n in range(3):
                    act.wait_ge(s["w_turned"], p * 3 + n + 1)
                    nc.scalar.copy(w_hi[:, n, :, :], ps[:, 6 + n % 2, :].rearrange("p (k n) -> p k n", n=128)).then_inc(s["w_hi_ready"], 1)

                def parts(n):
                    act.wait_ge(s["projected"], p * 3 + n + 1)
                    nc.scalar.copy(fives(side_hi[:, n, :]), five(0))
                    nc.scalar.activation(fives(square[:, n, :]), five(0), ACT.Square).then_inc(s["squared"], 1)

                def weights(n):
                    act.wait_ge(s["own_in"], p + 1)
                    act.wait_ge(s["dist_ready"], p * 2 + n + 1)
                    if n:
                        act.wait_ge(s["amped"], p * 2 + 1)
                    nc.scalar.activation(fives(weight[:, :]), five(3), ACT.Exp, scale=own_cols[:, 0:1],
                                         bias=own_cols[:, 1:2]).then_inc(s["weighted"], 1)

                parts(0)
                parts(1)
                weights(0)
                act.wait_ge(s["projected"], p * 3 + 3)
                nc.scalar.copy(fives(v_turn[:, :]), five(0)).then_inc(s["v_copied"], 1)
                weights(1)
                for n, (t0, t1) in enumerate(v_groups):
                    act.wait_ge(s["v_turned"], p * 3 + n + 1)
                    nc.scalar.copy(v_hi[:, t0:t1, :, 0:depth], v_bank(n, t0, t1)).then_inc(s["v_hi_ready"], 1)
                for h in range(2):
                    for n in range(2 * tiles):
                        at = p * 4 * tiles + 2 * tiles * h + n
                        act.wait_ge(s["logits_ready"], at + 1)
                        if n >= 2:
                            act.wait_ge(s["prob_lo_ready"], at - 1)
                        nc.scalar.activation(prob[:, n % 2, :].rearrange("p (a n) -> p a n", a=2), pair_of_banks(2 + 2 * (n % 2), R),
                                             ACT.Exp, scale=inv_temp[:, 0:1]).then_inc(s["prob_ready"], 1)
                        act.wait_ge(s["prob_ready"], at + 1)
                        if n >= 2:
                            act.wait_ge(s["mix_step"], at - 1)
                        nc.scalar.copy(prob_hi[:, n % 2, :], prob[:, n % 2, :]).then_inc(s["prob_hi_ready"], 1)
                        if n % tiles == tiles - 1:
                            g = 2 * h + n // tiles
                            act.wait_ge(s["mix_step"], at + 1)
                            act.wait_ge(stored[g % 2], (p * 2 + h + 1) * 16)
                            nc.scalar.copy(mixed[:, g % 2, :].rearrange("p (a n) -> p a n", a=2), pair_of_banks(6, depth + 1)).then_inc(s["mixed_out"], 1)

        @block.tensor
        def _(pe):
            pe.sem_inc(s["raw_free"], 1)
            with pe.Fori(0, pairs) as p:
                pe.wait_ge(s["mixed_out"], p * 4 + 1)
                for n in range(3):
                    pe.wait_ge(s["raw_in"], p * 48 + 48)
                    if n == 2:
                        pe.wait_ge(s["w_lo_ready"], p * 3 + 1)
                    for k in range(blocks):
                        last = nc.tensor.transpose(ps[:, 6 + n % 2, k * 128:(k + 1) * 128], raw[:, n, k * 128:(k + 1) * 128], ident[:, :])
                    last.then_inc(s["w_turned"], 1)
                pe.sem_inc(s["raw_free"], 1)

                def project(n):
                    pe.wait_ge(s["w_lo_ready"], p * 3 + n + 1)
                    if n:
                        pe.wait_ge(s["side_lo_ready"], p * 2 + n)
                    for k in range(blocks):
                        for m, (w, x) in enumerate(((w_hi, x_hi), (w_hi, x_lo), (w_lo, x_hi))):
                            for c in range(5):
                                last = nc.tensor.matmul(five(0)[:, c, :], w[:, n, k, :], x[:, k, c * part:(c + 1) * part],
                                                        start=(k == 0 and m == 0 and c % 2 == 0), stop=(k == blocks - 1 and m == 2),
                                                        skip_group_check=True)
                    last.then_inc(s["projected"], 1)

                def distances(n):
                    pe.wait_ge(s["own_in"], p + 1)
                    if n:
                        pe.wait_ge(s["weighted"], p * 2 + n)
                    pe.wait_ge(s["square_lo_ready"], p * 2 + n + 1)
                    products = ((own_hi, side_hi), (own_lo, side_hi), (own_hi, side_lo), (head_sum, square_hi), (head_sum, square_lo))
                    for m, (w, x) in enumerate(products):
                        for c in range(5):
                            last = nc.tensor.matmul(five(3)[:, c, :], w[:, :], x[:, n, c * part:(c + 1) * part],
                                                    start=(m == 0 and c % 2 == 0), stop=(m == 4), skip_group_check=True)
                    last.then_inc(s["dist_ready"], 1)

                project(0)
                project(1)
                distances(0)
                project(2)
                distances(1)
                pe.wait_ge(s["v_copied"], p + 1)
                for n, (t0, t1) in enumerate(v_groups):
                    if n == 2:
                        pe.wait_ge(s["v_lo_ready"], p * 3 + 1)
                    for t in range(t0, t1):
                        last = nc.tensor.transpose(ps[0:R, 6 + n % 2, (t - t0) * 128:(t - t0 + 1) * 128],
                                                   v_turn[:, t * R:(t + 1) * R], ident[:, :])
                    last.then_inc(s["v_turned"], 1)
                pe.wait_ge(s["stacked"], p * 3 + 4)

                for h in range(2):
                    for g in range(2 * tiles):
                        t, half = divmod(g, 2)
                        if g >= 2:
                            pe.wait_ge(s["reduced"], p * 4 * tiles + 2 * tiles * h + g - 1)
                        for c in range(2):
                            at = (2 * half + c) * quarter
                            last = nc.tensor.matmul(ps[0:R, 2 * (g % 2) + c, 0:quarter], stack[:, h, t * R:(t + 1) * R],
                                                    stack[:, 2, at:at + quarter], start=True, stop=True)
                        last.then_inc(s["scored"], 1)
                    pe.wait_ge(s["max_ready"], p * 2 + h + 1)
                    nc.tensor.transpose(ps[0:tiles, 0, 0:R], row_max[:, :], ident[0:R, 0:R]).then_inc(s["max_turned"], 1)
                    pe.wait_ge(s["shift_in"], p * 64 + 32 * h + 32)
                    def logits(n):
                        half, t = divmod(n, tiles)
                        if n >= 2:
                            pe.wait_ge(s["prob_ready"], p * 4 * tiles + 2 * tiles * h + n - 1)
                        for c in range(2):
                            at = (2 * half + c) * quarter
                            last = nc.tensor.matmul(ps[0:R, 2 + 2 * (n % 2) + c, 0:quarter], stack[:, 2, t * R:(t + 1) * R],
                                                    stack[:, h, at:at + quarter], start=True, stop=True)
                        last.then_inc(s["logits_ready"], 1)

                    def mix(n):
                        half, t = divmod(n, tiles)
                        at = p * 4 * tiles + 2 * tiles * h + n
                        if t == 0:
                            pe.wait_ge(s["mixed_out"], p * 4 + 2 * h + half + 1)
                        pe.wait_ge(s["prob_hi_ready"], at + 1)
                        for m, (v, prb) in enumerate(((v_hi, prob_hi), (v_lo, prob_hi), (v_hi, prob_lo))):
                            if m == 2:
                                pe.wait_ge(s["prob_lo_ready"], at + 1)
                            for c in range(2):
                                last = nc.tensor.matmul(ps[0:depth + 1, 6 + c, 0:quarter], v[:, t, h, :],
                                                        prb[:, n % 2, c * quarter:(c + 1) * quarter],
                                                        start=(t == 0 and m == 0), stop=(t == tiles - 1 and m == 2),
                                                        skip_group_check=True)
                        last.then_inc(s["mix_step"], 1)

                    logits(0)
                    for n in range(2 * tiles):
                        if n + 1 < 2 * tiles:
                            logits(n + 1)
                        mix(n)

def combine(nc, x, attended, graph_w, graph_b, out_w, ident, kept, x_tiles):
    tiles, width = x_tiles.shape[1], x_tiles.shape[2]
    n_nodes = kept.shape[2]
    blocks = width // 128
    depth = attended.shape[1] - 1
    with ExitStack() as ctx:
        sb, banks, sem = tools(nc, ctx, "combine")
        raw = sb("raw", [128, 2, width])
        w_hi = sb("w_hi", [128, 2, blocks, width], F32R)
        w_lo = sb("w_lo", [128, 2, blocks, width], F32R)
        offset = sb("offset", [R, width])
        heads = sb("heads", [128, 2, n_nodes])
        total = sb("total", [128, 2, n_nodes])
        part_hi = sb("part_hi", [128, 2 * blocks, n_nodes], F32R)
        part_lo = sb("part_lo", [128, 2 * blocks, n_nodes], F32R)
        ps = banks("ps", 4)
        names = "x_in offset_in raw_turned w_hi_ready w_lo_ready offset_added reciprocal_ready divided hi_ready lo_ready summed tile_out"
        s = {name: sem(name) for name in names.split()}
        raw_in = [sem("raw_in_0"), sem("raw_in_1")]
        heads_in = [sem("heads_in_0"), sem("heads_in_1")]
        block = ctx.enter_context(nc.Block())

        @block.sync
        def _(sp):
            for n in range(2 * blocks):
                w = (graph_w, out_w)[n // blocks]
                if n >= 2:
                    sp.wait_ge(s["raw_turned"], n - 1)
                sp.dma_start(raw[:, n % 2, :], w[n % blocks * 128:(n % blocks + 1) * 128, :]).then_inc(raw_in[n % 2], 16)
                if n == 0:
                    sp.dma_start(x_tiles[:, :, :], x.rearrange("(t p) n -> p t n", p=R)).then_inc(s["x_in"], 16)
                    sp.dma_start(offset[:, :], graph_b.partition_broadcast(R)).then_inc(s["offset_in"], 16)

        @block.gpsimd
        def _(pool):
            for k in range(blocks):
                if k >= 2:
                    pool.wait_ge(s["lo_ready"], k - 1)
                for h in range(2):
                    rows = slice(depth * h, depth * (h + 1))
                    pool.dma_start(heads[rows, k % 2, :], attended[2 * k + h, 0:depth, 0:n_nodes]).then_inc(heads_in[k % 2], 16)
                    pool.dma_start(total[rows, k % 2, :],
                                   attended[2 * k + h, depth, 0:n_nodes].partition_broadcast(depth)).then_inc(heads_in[k % 2], 16)
            pool.wait_ge(s["x_in"], 16)
            pool.wait_ge(s["offset_in"], 16)
            for t in range(tiles):
                nc.gpsimd.tensor_tensor(x_tiles[:, t, :], x_tiles[:, t, :], offset[:, :], ALU.add).then_inc(s["offset_added"], 1)

        @block.vector
        def _(dve):
            for n in range(2 * blocks):
                dve.wait_ge(s["w_hi_ready"], n + 1)
                w, o = divmod(n, blocks)
                nc.vector.tensor_tensor(w_lo[:, w, :, o * 128:(o + 1) * 128], ps[:, n % 2, :].rearrange("p (k n) -> p k n", n=128),
                                        w_hi[:, w, :, o * 128:(o + 1) * 128].bitcast(F32), ALU.subtract).then_inc(s["w_lo_ready"], 1)
            for k in range(blocks):
                dve.wait_ge(heads_in[k % 2], 64 * (k // 2 + 1))
                nc.vector.reciprocal(total[:, k % 2, :], total[:, k % 2, :]).then_inc(s["reciprocal_ready"], 1)
                dve.wait_ge(s["reciprocal_ready"], k + 1)
                nc.vector.tensor_tensor(heads[:, k % 2, :], heads[:, k % 2, :], total[:, k % 2, :], ALU.mult).then_inc(s["divided"], 1)
                dve.wait_ge(s["hi_ready"], blocks + k + 1)
                nc.vector.tensor_tensor(part_lo[:, blocks + k, :], heads[:, k % 2, :], part_hi[:, blocks + k, :].bitcast(F32),
                                        ALU.subtract).then_inc(s["lo_ready"], 1)
            for k in range(blocks):
                dve.wait_ge(s["hi_ready"], k + 1)
                nc.vector.tensor_tensor(part_lo[:, k, :], kept[:, k, :], part_hi[:, k, :].bitcast(F32),
                                        ALU.subtract).then_inc(s["lo_ready"], 1)
            dve.wait_ge(s["offset_added"], tiles)
            for t in range(tiles):
                dve.wait_ge(s["summed"], t + 1)
                nc.vector.tensor_tensor(x_tiles[:, t, :], ps[0:R, 2 + t % 2, :], x_tiles[:, t, :], ALU.add).then_inc(s["tile_out"], 1)

        @block.scalar
        def _(act):
            for n in range(2 * blocks):
                act.wait_ge(s["raw_turned"], n + 1)
                w, o = divmod(n, blocks)
                nc.scalar.copy(w_hi[:, w, :, o * 128:(o + 1) * 128], ps[:, n % 2, :].rearrange("p (k n) -> p k n", n=128)).then_inc(s["w_hi_ready"], 1)
            for k in range(blocks):
                nc.scalar.copy(part_hi[:, k, :], kept[:, k, :]).then_inc(s["hi_ready"], 1)
            for k in range(blocks):
                act.wait_ge(s["divided"], k + 1)
                nc.scalar.copy(part_hi[:, blocks + k, :], heads[:, k % 2, :]).then_inc(s["hi_ready"], 1)

        @block.tensor
        def _(pe):
            for n in range(2 * blocks):
                pe.wait_ge(raw_in[n % 2], 16 * (n // 2 + 1))
                if n >= 2:
                    pe.wait_ge(s["w_lo_ready"], n - 1)
                for k in range(blocks):
                    last = nc.tensor.transpose(ps[:, n % 2, k * 128:(k + 1) * 128], raw[:, n % 2, k * 128:(k + 1) * 128], ident[:, :])
                last.then_inc(s["raw_turned"], 1)
            pe.wait_ge(s["w_lo_ready"], 2 * blocks)
            pe.wait_ge(s["lo_ready"], 2 * blocks)
            for t in range(tiles):
                if t >= 2:
                    pe.wait_ge(s["tile_out"], t - 1)
                at = slice(t * R, (t + 1) * R)
                for k in range(2 * blocks):
                    w, kk = divmod(k, blocks)
                    for m, (left, right) in enumerate(((part_hi, w_hi), (part_hi, w_lo), (part_lo, w_hi))):
                        last = nc.tensor.matmul(ps[0:R, 2 + t % 2, :], left[:, k, at], right[:, w, kk, :],
                                                start=(k == 0 and m == 0), stop=(k == 2 * blocks - 1 and m == 2))
                last.then_inc(s["summed"], 1)


def normalise(nc, name, x_tiles, out_tiles, eps, gain=None, offset=None, residual=None, out=None):
    tiles, width = x_tiles.shape[1], x_tiles.shape[2]
    with ExitStack() as ctx:
        sb, banks, sem = tools(nc, ctx, name)
        stats = sb("stats", [R, 2, 6])
        moments = sb("moments", [R, tiles, 2])
        root = sb("root", [R, tiles])
        scale = sb("scale", [R, tiles])
        eps_col = sb("eps_col", [R, 1])
        rows = sb("rows", [R, 2, width])
        names = "eps_in rows_in stats_ready moments_ready root_ready scale_ready unit_ready gained shifted finished stored"
        s = {n: sem(n) for n in names.split()}
        block = ctx.enter_context(nc.Block())

        @block.sync
        def _(sp):
            if gain is not None:
                sp.dma_start(rows[:, 0, :], gain.partition_broadcast(R)).then_inc(s["rows_in"], 16)
                sp.dma_start(rows[:, 1, :], offset.partition_broadcast(R)).then_inc(s["rows_in"], 16)
                for t in range(tiles):
                    sp.wait_ge(s["finished"], t + 1)
                    sp.dma_start(out[t * R:(t + 1) * R, :], x_tiles[:, t, :]).then_inc(s["stored"], 16)
                sp.wait_ge(s["stored"], 16 * tiles)

        @block.gpsimd
        def _(pool):
            nc.gpsimd.memset(eps_col[:, :], eps).then_inc(s["eps_in"], 1)
            if gain is not None:
                pool.wait_ge(s["rows_in"], 32)
                for t in range(tiles):
                    pool.wait_ge(s["gained"], t + 1)
                    nc.gpsimd.tensor_tensor(x_tiles[:, t, :], out_tiles[:, t, :], rows[:, 1, :], ALU.add).then_inc(s["shifted"], 1)

        @block.vector
        def _(dve):
            for t in range(tiles):
                if t >= 2:
                    dve.wait_ge(s["moments_ready"], t - 1)
                nc.vector.bn_stats(stats[:, t % 2, :], x_tiles[:, t, :]).then_inc(s["stats_ready"], 1)
                dve.wait_ge(s["stats_ready"], t + 1)
                nc.vector.bn_aggr(moments[:, t, :], stats[:, t % 2, :]).then_inc(s["moments_ready"], 1)
            dve.wait_ge(s["root_ready"], 1)
            nc.vector.reciprocal(scale[:, :], root[:, :]).then_inc(s["scale_ready"], 1)
            dve.wait_ge(s["scale_ready"], 1)
            for t in range(tiles):
                nc.vector.tensor_scalar(out_tiles[:, t, :], x_tiles[:, t, :], moments[:, t, 0:1], scale[:, t:t + 1],
                                        ALU.subtract, ALU.mult).then_inc(s["unit_ready"], 1)
                if gain is not None:
                    dve.wait_ge(s["rows_in"], 32)
                    dve.wait_ge(s["unit_ready"], t + 1)
                    nc.vector.tensor_tensor(out_tiles[:, t, :], out_tiles[:, t, :], rows[:, 0, :], ALU.mult).then_inc(s["gained"], 1)
                    if t >= 1:
                        dve.wait_ge(s["shifted"], t)
                        nc.vector.tensor_tensor(x_tiles[:, t - 1, :], x_tiles[:, t - 1, :], residual[:, t - 1, :], ALU.add).then_inc(s["finished"], 1)
            if gain is not None:
                dve.wait_ge(s["shifted"], tiles)
                nc.vector.tensor_tensor(x_tiles[:, tiles - 1, :], x_tiles[:, tiles - 1, :], residual[:, tiles - 1, :], ALU.add).then_inc(s["finished"], 1)

        @block.scalar
        def _(act):
            act.wait_ge(s["moments_ready"], tiles)
            act.wait_ge(s["eps_in"], 1)
            nc.scalar.activation(root[:, :], moments[:, :, 1], ACT.Sqrt, bias=eps_col[:, 0:1]).then_inc(s["root_ready"], 1)


def gate(nc, x_hi, x_lo, w_gate, b2, ident, unit, share, mixed):
    tiles, experts = share.shape[1], share.shape[2]
    width = b2.shape[1]
    blocks = w_gate.shape[0] // 128
    with ExitStack() as ctx:
        sb, banks, sem = tools(nc, ctx, "gate")
        w = sb("w", [128, blocks, experts])
        w_hi = sb("w_hi", [128, blocks, experts], F32R)
        w_lo = sb("w_lo", [128, blocks, experts], F32R)
        bias = sb("bias", [experts, width])
        number = sb("number", [R, tiles, experts])
        logit = sb("logit", [R, tiles, experts])
        top_logit = sb("top_logit", [R, tiles])
        less = sb("less", [R, tiles, experts])
        exps = sb("exps", [R, tiles, experts])
        total = sb("total", [R, tiles])
        total_rec = sb("total_rec", [R, tiles])
        prob = sb("prob", [R, tiles, experts])
        best = sb("best", [R, tiles, 8])
        best_at = sb("best_at", [R, tiles, 8], mybir.dt.uint32)
        best_f = sb("best_f", [R, tiles, 8])
        pair_sum = sb("pair_sum", [R, tiles])
        pair_rec = sb("pair_rec", [R, tiles])
        conf = sb("conf", [R, tiles, 2])
        chosen = sb("chosen", [R, 2, tiles, experts])
        weighed = sb("weighed", [R, 2, tiles, experts])
        share_turn = sb("share_turn", [experts, tiles, R])
        ps = banks("ps", 5)
        names = "w_in bias_in numbers parted scored step less_ready exp_ready shared turned turn_out biased bias_out"
        s = {n: sem(n) for n in names.split()}
        block = ctx.enter_context(nc.Block())

        @block.sync
        def _(sp):
            sp.dma_start(w[:, :, :], w_gate.rearrange("(k p) e -> p k e", p=128)).then_inc(s["w_in"], 16)
            sp.dma_start(bias[:, :], b2).then_inc(s["bias_in"], 16)

        @block.gpsimd
        def _(pool):
            nc.gpsimd.iota(number[:, :, :], [[0, tiles], [1, experts]], base=0, channel_multiplier=0,
                           allow_small_or_imprecise_dtypes=True).then_inc(s["numbers"], 1)

        @block.scalar
        def _(act):
            act.wait_ge(s["less_ready"], 1)
            nc.scalar.activation(exps[:, :, :], less[:, :, :], ACT.Exp).then_inc(s["exp_ready"], 1)

        @block.vector
        def _(dve):
            count = [0]

            def link(instruction):
                count[0] += 1
                instruction.then_inc(s["step"], 1)
                dve.wait_ge(s["step"], count[0])

            def along(column):
                return column.unsqueeze(2).to_broadcast([R, tiles, experts])

            dve.wait_ge(s["w_in"], 16)
            link(nc.vector.tensor_copy(w_hi[:, :, :], w[:, :, :]))
            nc.vector.tensor_tensor(w_lo[:, :, :], w[:, :, :], w_hi[:, :, :].bitcast(F32), ALU.subtract).then_inc(s["parted"], 1)
            dve.wait_ge(s["scored"], 1)
            link(nc.vector.tensor_copy(logit[:, :, :], ps[0:R, 0, 0:tiles * experts].rearrange("p (t e) -> p t e", e=experts)))
            link(nc.vector.tensor_reduce(top_logit[:, :], logit[:, :, :], AX.X, ALU.max))
            nc.vector.tensor_tensor(less[:, :, :], logit[:, :, :], along(top_logit[:, :]), ALU.subtract).then_inc(s["less_ready"], 1)
            dve.wait_ge(s["exp_ready"], 1)
            link(nc.vector.tensor_reduce(total[:, :], exps[:, :, :], AX.X, ALU.add))
            link(nc.vector.reciprocal(total_rec[:, :], total[:, :]))
            link(nc.vector.tensor_tensor(prob[:, :, :], exps[:, :, :], along(total_rec[:, :]), ALU.mult))
            for t in range(tiles):
                last = nc.vector.max(best[:, t, :], prob[:, t, :])
            link(last)
            for t in range(tiles):
                last = nc.vector.max_index(best_at[:, t, :], best[:, t, :], prob[:, t, :])
            link(last)
            link(nc.vector.tensor_copy(best_f[:, :, :], best_at[:, :, :]))
            link(nc.vector.tensor_tensor(pair_sum[:, :], best[:, :, 0], best[:, :, 1], ALU.add))
            link(nc.vector.reciprocal(pair_rec[:, :], pair_sum[:, :]))
            dve.wait_ge(s["numbers"], 1)
            for n in range(2):
                link(nc.vector.tensor_tensor(conf[:, :, n], best[:, :, n], pair_rec[:, :], ALU.mult))
                link(nc.vector.tensor_tensor(chosen[:, n, :, :], number[:, :, :], along(best_f[:, :, n]), ALU.is_equal))
                link(nc.vector.tensor_tensor(weighed[:, n, :, :], chosen[:, n, :, :], along(conf[:, :, n]), ALU.mult))
            nc.vector.tensor_tensor(share[:, :, :], weighed[:, 0, :, :], weighed[:, 1, :, :], ALU.add).then_inc(s["shared"], 1)
            for t0 in range(0, tiles, 4):
                t1 = min(t0 + 4, tiles)
                dve.wait_ge(s["turned"], t0 // 4 + 1)
                nc.vector.tensor_copy(share_turn[:, t0:t1, :], ps[0:experts, 1 + t0 // 4 % 2, 0:(t1 - t0) * R].rearrange("p (t n) -> p t n", n=R)).then_inc(s["turn_out"], 1)
            for t in range(tiles):
                dve.wait_ge(s["biased"], t + 1)
                nc.vector.tensor_tensor(mixed[:, t, :], ps[0:R, 3 + t % 2, :], unit[:, t, :], ALU.add).then_inc(s["bias_out"], 1)

        @block.tensor
        def _(pe):
            pe.wait_ge(s["parted"], 1)
            for t in range(tiles):
                at = slice(t * R, (t + 1) * R)
                for k in range(blocks):
                    for m, (left, right) in enumerate(((x_hi, w_hi), (x_hi, w_lo), (x_lo, w_hi))):
                        last = nc.tensor.matmul(ps[0:R, 0, t * experts:(t + 1) * experts], left[:, k, at], right[:, k, :],
                                                start=(k == 0 and m == 0), stop=(k == blocks - 1 and m == 2))
            last.then_inc(s["scored"], 1)
            pe.wait_ge(s["shared"], 1)
            for t in range(tiles):
                if t == 8:
                    pe.wait_ge(s["turn_out"], 1)
                last = nc.tensor.transpose(ps[0:experts, 1 + t // 4 % 2, t % 4 * R:(t % 4 + 1) * R], share[:, t, :], ident[0:R, 0:R])
                if t % 4 == 3 or t == tiles - 1:
                    last.then_inc(s["turned"], 1)
            pe.wait_ge(s["turn_out"], (tiles + 3) // 4)
            pe.wait_ge(s["bias_in"], 16)
            for t in range(tiles):
                if t >= 2:
                    pe.wait_ge(s["bias_out"], t - 1)
                nc.tensor.matmul(ps[0:R, 3 + t % 2, :], share_turn[:, t, :], bias[:, :], start=True, stop=True).then_inc(s["biased"], 1)


def experts_mix(nc, x_hi, x_lo, w1, b1, w2, share, mixed):
    tiles = mixed.shape[1]
    n_nodes = x_hi.shape[2]
    experts, width, hidden = w1.shape
    k1, k2 = width // 128, hidden // 128
    chunks = spans(n_nodes, 500)
    with ExitStack() as ctx:
        sb, banks, sem = tools(nc, ctx, "experts")
        raw1 = sb("raw1", [128, k1, hidden])
        raw2 = sb("raw2", [128, k2, width])
        bias = sb("bias", [128, k2])
        w1_hi = sb("w1_hi", [128, k1, hidden], F32R)
        w1_lo = sb("w1_lo", [128, k1, hidden], F32R)
        w2_hi = sb("w2_hi", [128, k2, width], F32R)
        w2_lo = sb("w2_lo", [128, k2, width], F32R)
        act_f = sb("act_f", [128, k2, n_nodes])
        act_hi = sb("act_hi", [128, k2, n_nodes], F32R)
        act_lo = sb("act_lo", [128, k2, n_nodes], F32R)
        ps = banks("ps", 8)
        names = ("raw1_in raw2_in bias_in w1_hi_ready w1_lo_ready w2_hi_ready w2_lo_ready projected act_ready act_hi_ready "
                 "act_lo_ready output added")
        s = {n: sem(n) for n in names.split()}
        block = ctx.enter_context(nc.Block())
        parts = k2 * len(chunks)

        @block.sync
        def _(sp):
            for name, amount in (("w1_lo_ready", 1), ("w2_lo_ready", 1), ("act_ready", parts)):
                sp.sem_inc(s[name], amount)
            with sp.Fori(0, experts) as e:
                sp.wait_ge(s["w1_lo_ready"], e + 1)
                sp.dma_start(raw1[:, :, :], w1[bass.ds(e, 1), :, :].rearrange("a (k p) n -> p (a k) n", p=128)).then_inc(s["raw1_in"], 16)
                sp.wait_ge(s["w2_lo_ready"], e + 1)
                sp.dma_start(raw2[:, :, :], w2[bass.ds(e, 1), :, :].rearrange("a (k p) n -> p (a k) n", p=128)).then_inc(s["raw2_in"], 16)
                sp.wait_ge(s["act_ready"], e * parts + parts)
                sp.dma_start(bias[:, :], b1[bass.ds(e, 1), :].rearrange("a (k p) -> p (a k)", p=128),
                             allow_slow_non_contiguous=True).then_inc(s["bias_in"], 16)

        @block.vector
        def _(dve):
            def split_w1(e):
                dve.wait_ge(s["raw1_in"], e * 16 + 16)
                nc.vector.tensor_copy(w1_hi[:, :, :], raw1[:, :, :]).then_inc(s["w1_hi_ready"], 1)
                dve.wait_ge(s["w1_hi_ready"], e + 1)
                nc.vector.tensor_tensor(w1_lo[:, :, :], raw1[:, :, :], w1_hi[:, :, :].bitcast(F32), ALU.subtract).then_inc(s["w1_lo_ready"], 1)

            def expert(e, last):
                dve.wait_ge(s["raw2_in"], e * 16 + 16)
                nc.vector.tensor_copy(w2_hi[:, :, :], raw2[:, :, :]).then_inc(s["w2_hi_ready"], 1)
                dve.wait_ge(s["w2_hi_ready"], e + 1)
                nc.vector.tensor_tensor(w2_lo[:, :, :], raw2[:, :, :], w2_hi[:, :, :].bitcast(F32), ALU.subtract).then_inc(s["w2_lo_ready"], 1)
                for m in range(k2):
                    for c, (a, b) in enumerate(chunks):
                        n = m * len(chunks) + c
                        dve.wait_ge(s["act_ready"], e * parts + (parts + n + 1))
                        nc.vector.tensor_copy(act_hi[:, m, a:b], act_f[:, m, a:b]).then_inc(s["act_hi_ready"], 1)
                        dve.wait_ge(s["act_hi_ready"], e * parts + (n + 1))
                        nc.vector.tensor_tensor(act_lo[:, m, a:b], act_f[:, m, a:b], act_hi[:, m, a:b].bitcast(F32), ALU.subtract).then_inc(s["act_lo_ready"], 1)
                if not last:
                    split_w1(e + 1)
                for t in range(tiles):
                    dve.wait_ge(s["output"], e * tiles + (t + 1))
                    nc.vector.scalar_tensor_tensor(out=mixed[:, t, :], in0=ps[0:R, 6 + t % 2, :],
                                                   scalar=share[:, t, e:e + 1] if last else share[:, t, bass.ds(e, 1)],
                                                   in1=mixed[:, t, :], op0=ALU.mult, op1=ALU.add).then_inc(s["added"], 1)
                dve.wait_ge(s["added"], e * tiles + 2 * tiles)

            dve.sem_inc(s["added"], tiles)
            split_w1(0)
            with dve.Fori(0, experts - 1) as e:
                expert(e, last=False)
            expert(experts - 1, last=True)

        @block.scalar
        def _(act):
            act.sem_inc(s["act_lo_ready"], parts)
            with act.Fori(0, experts) as e:
                act.wait_ge(s["bias_in"], e * 16 + 16)
                for m in range(k2):
                    for c, (a, b) in enumerate(chunks):
                        n = m * len(chunks) + c
                        act.wait_ge(s["projected"], e * parts + (n + 1))
                        act.wait_ge(s["act_lo_ready"], e * parts + (n + 1))
                        nc.scalar.activation(act_f[:, m, a:b], ps[:, 3 * m + c, 0:b - a], ACT.Gelu_apprx_tanh,
                                             bias=bias[:, m:m + 1]).then_inc(s["act_ready"], 1)

        @block.tensor
        def _(pe):
            with pe.Fori(0, experts) as e:
                pe.wait_ge(s["w1_lo_ready"], e + 2)
                for m in range(k2):
                    for c, (a, b) in enumerate(chunks):
                        n = m * len(chunks) + c
                        pe.wait_ge(s["act_ready"], e * parts + (n + 1))
                        for k in range(k1):
                            for i, (w, x) in enumerate(((w1_hi, x_hi), (w1_hi, x_lo), (w1_lo, x_hi))):
                                last = nc.tensor.matmul(ps[:, n, 0:b - a], w[:, k, m * 128:(m + 1) * 128], x[:, k, a:b],
                                                        start=(k == 0 and i == 0), stop=(k == k1 - 1 and i == 2))
                        last.then_inc(s["projected"], 1)
                pe.wait_ge(s["w2_lo_ready"], e + 2)
                for t in range(tiles):
                    at = slice(t * R, (t + 1) * R)
                    chunk = [c for c, (a, b) in enumerate(chunks) if a <= t * R < b][0]
                    pe.wait_ge(s["act_lo_ready"], e * parts + (parts + (k2 - 1) * len(chunks) + chunk + 1))
                    pe.wait_ge(s["added"], e * tiles + (tiles + t - 1))
                    for k in range(k2):
                        for i, (h, w) in enumerate(((act_hi, w2_hi), (act_hi, w2_lo), (act_lo, w2_hi))):
                            last = nc.tensor.matmul(ps[0:R, 6 + t % 2, :], h[:, k, at], w[:, k, :],
                                                    start=(k == 0 and i == 0), stop=(k == k2 - 1 and i == 2))
                    last.then_inc(s["output"], 1)


def constants(nc, ident, zero_hot, x, x_tiles):
    with ExitStack() as ctx:
        sb, banks, sem = tools(nc, ctx, "constants")
        zeroed = sem("zeroed")
        x_in = sem("x_in")
        block = ctx.enter_context(nc.Block())

        @block.sync
        def _(sp):
            sp.dma_start(x_tiles[:, :, :], x.rearrange("(t p) n -> p t n", p=R)).then_inc(x_in, 16)
            sp.wait_ge(x_in, 16)

        @block.gpsimd
        def _(pool):
            nc.gpsimd.memset(ident[:, :], 0.0).then_inc(zeroed, 1)
            nc.gpsimd.memset(zero_hot[:, :], 0.0)
            pool.wait_ge(zeroed, 1)
            nc.gpsimd.affine_select(out=ident[:, :], in_=ident[:, :], compare_op=ALU.not_equal, fill=1.0,
                                    base=0, pattern=[[-1, 128]], channel_multiplier=1)


def graph_transformer(nc, a, out):
    n_nodes, width = a["x"].shape
    tiles = n_nodes // R
    blocks = width // 128
    heads, _, depth = a["L0_mix_base_centers"].shape
    experts = a["L0_ffn_W1"].shape[0]
    padded = (n_nodes + 7) // 8 * 8
    eps = 1e-5
    attended = nc.dram_tensor("attended", (heads, depth + 1, padded), F32, kind="Internal").ap()
    with ExitStack() as ctx:
        sb, banks, sem = tools(nc, ctx, "layer")
        ident = sb("ident", [128, 128])
        with ExitStack() as first:
            sb, banks, sem = tools(nc, first, "mixers")
            kept = sb("kept", [128, blocks, n_nodes])
            with ExitStack() as own:
                sb, banks, sem = tools(nc, own, "inputs")
                x_hi = sb("x_hi", [128, blocks, n_nodes], F32R)
                x_lo = sb("x_lo", [128, blocks, n_nodes], F32R)
                with ExitStack() as graph:
                    sb, banks, sem = tools(nc, graph, "edges")
                    zero_hot = sb("zero_hot", [R, 512], F16)
                    x_tiles = sb("x_tiles", [R, tiles, width])
                    adj = sb("adj", [R, tiles, n_nodes])
                    dinv = sb("dinv", [R, tiles])
                    constants(nc, ident, zero_hot, a["x"], x_tiles)
                    turn_normalised(nc, "norm1", x_tiles, ident, x_hi, x_lo, eps)
                    adjacency(nc, a["src"], a["dst"], ident, zero_hot, adj, dinv)
                    graph_layers(nc, x_hi, x_lo, adj, dinv, [a[f"L0_gnn_W{n}"] for n in (1, 2, 3)],
                                 [a[f"L0_gnn_b{n}"] for n in (1, 2, 3)], kept)
                attention(nc, {k[len("L0_mix_"):]: v for k, v in a.items() if k.startswith("L0_mix_")}, ident, x_hi, x_lo, attended)
            second = ctx.enter_context(ExitStack())
            sb, banks, sem = tools(nc, first, "residual")
            x_new = sb("x_new", [R, tiles, width])
            combine(nc, a["x"], attended, a["L0_gnn_W4"], a["L0_gnn_b4"], a["L0_mix_out_w"], ident, kept, x_new)
            sb, banks, sem = tools(nc, first, "mixture")
            unit = sb("unit", [R, tiles, width])
            mixed = sb("mixed", [R, tiles, width])
            share = sb("share", [R, tiles, experts])
            f_hi = sb("f_hi", [128, blocks, n_nodes], F32R)
            f_lo = sb("f_lo", [128, blocks, n_nodes], F32R)
            normalise(nc, "norm2", x_new, unit, eps)
            turn_normalised(nc, "norm3", unit, ident, f_hi, f_lo, eps, a["L0_ffn_ln_g"], a["L0_ffn_ln_b"])
            gate(nc, f_hi, f_lo, a["L0_ffn_Wg"], a["L0_ffn_b2"], ident, unit, share, mixed)
            experts_mix(nc, f_hi, f_lo, a["L0_ffn_W1"], a["L0_ffn_b1"], a["L0_ffn_W2"], share, mixed)
            normalise(nc, "norm4", mixed, unit, eps, a["L0_ffn_out_g"], a["L0_ffn_out_b"], x_new, out)


INPUTS = (["x", "src", "dst"] + [f"L0_gnn_{w}{n}" for n in (1, 2, 3, 4) for w in "Wb"]
          + ["L0_mix_" + n for n in ("base_centers", "center_deltas", "log_scales", "log_amps", "movement_scale_param",
                                     "temperature", "qkv_w", "out_w")]
          + ["L0_ffn_" + n for n in ("Wg", "W1", "b1", "W2", "b2", "ln_g", "ln_b", "out_g", "out_b")])


def kernel(**inputs):
    import numpy as np
    import concourse.bacc as bacc
    from concourse.bass_utils import run_bass_kernel_spmd as run

    nc = bacc.Bacc("TRN2", target_bir_lowering=False, num_devices=1)
    arrays = {f"in_{name}": np.ascontiguousarray(inputs[name]) for name in INPUTS}
    args = {name[3:]: nc.dram_tensor(name, v.shape, mybir.dt.from_np(v.dtype), kind="ExternalInput").ap()
            for name, v in arrays.items()}
    out = nc.dram_tensor("out_0", inputs["x"].shape, F32, kind="ExternalOutput").ap()
    graph_transformer(nc, args, out)
    return run(nc, [arrays], core_ids=[0]).results[0]["out_0"]
```

```python
from contextlib import ExitStack
import concourse.bass as bass
from concourse import mybir
ALU = mybir.AluOpType
ACT = mybir.ActivationFunctionType
AX = mybir.AxisListType
F32 = mybir.dt.float32
F32R = mybir.dt.float32r
F16 = mybir.dt.float16
I32 = mybir.dt.int32

R = 125
DUO = 2
ROUND = 12582912.0


def tools(nc, ctx, phase):
    def sb(name, shape, dtype=F32):
        return ctx.enter_context(nc.sbuf_tensor(f"{phase}_{name}", shape, dtype))

    def banks(name, count):
        return ctx.enter_context(nc.psum_tensor(f"{phase}_{name}", [128, count, 512], F32))

    def sem(name):
        return ctx.enter_context(nc.semaphore(f"{phase}_{name}"))
    return sb, banks, sem


def cleared_semaphores(nc, ctx, phase):
    taken = []

    def give_back():
        nc.clear_and_free_semaphores(taken)
        nc.all_engine_barrier()

    def sem(name):
        taken.append(nc.alloc_semaphore(f"{phase}_{name}"))
        return taken[-1]
    ctx.callback(give_back)
    return sem


def adjacency(nc, src, dst, ident, zero_hot, adj, dinv):
    n_nodes = adj.shape[2]
    tiles = n_nodes // R
    groups = src.shape[0] // (DUO * R)
    rows_in = groups // 2
    visits = 6
    part = 250
    with ExitStack() as ctx:
        sb, banks, sem = tools(nc, ctx, "adjacency")
        src_i = sb("src_i", [rows_in, 2 * DUO * R], I32)
        dst_i = sb("dst_i", [rows_in, 2 * DUO * R], I32)
        src_f = sb("src_f", [rows_in, 2 * DUO * R])
        dst_f = sb("dst_f", [rows_in, 2 * DUO * R])
        src_col = sb("src_col", [R, DUO, 2 * groups + 2 * visits])
        dst_col = sb("dst_col", [R, DUO, 2 * groups + 2 * visits])
        node_row = sb("node_row", [R, n_nodes], F16)
        block_row = sb("block_row", [rows_in, 2, tiles])
        group_col = sb("group_col", [rows_in, 2, tiles])
        low = sb("low", [rows_in, 2])
        low_end = sb("low_end", [rows_in, 2])
        high = sb("high", [rows_in, 2])
        begins = sb("begins", [rows_in, 2, tiles])
        ends = sb("ends", [rows_in, 2, tiles])
        touches = sb("touches", [rows_in, 2, tiles])
        first_less = sb("first_less", [rows_in, 2, tiles])
        last_less = sb("last_less", [rows_in, 2, tiles])
        candidates = sb("candidates", [rows_in, 2, 2 * tiles])
        extreme = sb("extreme", [2 * tiles, 1])
        bounds_f = sb("bounds_f", [1, 2 * tiles])
        span_f = sb("span_f", [1, 4, tiles])
        bounds = sb("bounds", [1, 2 * tiles], I32)
        src_hot = sb("src_hot", [R, visits * DUO, n_nodes], F16)
        dst_hot = sb("dst_hot", [R, visits * DUO, R], F16)
        rows = sb("rows", [R, 3, n_nodes])
        degree = sb("degree", [R, tiles])
        root = sb("root", [R, tiles])
        ps = banks("ps", 8)

        def count_rows(b):
            first = 3 * (b % 2)
            return ps[0:R, first:first + 3, :].rearrange("p a (c n) -> p (a c) n", n=256)[:, 0:5, 0:part]

        edges_in = sem("edges_in")
        iotas = sem("iotas")
        edge_f = sem("edge_f")
        edge_turned = sem("edge_turned")
        edge_cols = sem("edge_cols")
        range_step = sem("range_step")
        cand_ready = sem("cand_ready")
        cand_turned = sem("cand_turned")
        extreme_ready = sem("extreme_ready")
        extreme_turned = sem("extreme_turned")
        bounds_ready = sem("bounds_ready")
        hot_ready = sem("hot_ready")
        hot_free = sem("hot_free")
        counted = sem("counted")
        counts_out = sem("counts_out")
        loops_in = sem("loops_in")
        root_ready = sem("root_ready")
        dinv_ready = sem("dinv_ready")
        rows_scaled = sem("rows_scaled")
        block_turned = sem("block_turned")
        block_out = sem("block_out")
        block = ctx.enter_context(nc.Block())
        turn_groups = [(0, 4), (4, 8), (8, tiles)]

        @block.sync
        def _(sp):
            sp.dma_start(src_i[:, :], src.rearrange("(g e) -> g e", e=2 * DUO * R)).then_inc(edges_in, 16)
            sp.dma_start(dst_i[:, :], dst.rearrange("(g e) -> g e", e=2 * DUO * R)).then_inc(edges_in, 16)

        @block.gpsimd
        def _(pool):
            nc.gpsimd.iota(node_row[:, :], [[1, n_nodes]], base=0, channel_multiplier=0,
                           allow_small_or_imprecise_dtypes=True).then_inc(iotas, 1)
            nc.gpsimd.iota(block_row[:, :, :], [[0, 2], [R, tiles]], base=0, channel_multiplier=0,
                           allow_small_or_imprecise_dtypes=True).then_inc(iotas, 1)
            nc.gpsimd.iota(group_col[:, :, :], [[1, 2], [0, tiles]], base=0, channel_multiplier=2,
                           allow_small_or_imprecise_dtypes=True).then_inc(iotas, 1)
            for tile in (src_col, dst_col):
                nc.gpsimd.memset(tile[:, :, :], -1.0).then_inc(iotas, 1)
            for b in range(tiles):
                own = rows[:, b % 3, b * R:(b + 1) * R]
                pool.wait_ge(counts_out, b + 1)
                nc.gpsimd.tensor_tensor(own, own, ident[0:R, 0:R], ALU.add).then_inc(loops_in, 1)

        @block.vector
        def _(dve):
            dve.wait_ge(edges_in, 32)
            nc.vector.tensor_copy(src_f[:, :], src_i[:, :]).then_inc(edge_f, 1)
            nc.vector.tensor_copy(dst_f[:, :], dst_i[:, :]).then_inc(edge_f, 1)
            dve.wait_ge(edge_f, 2)
            count = [0]

            def link(instruction):
                count[0] += 1
                instruction.then_inc(range_step, 1)
                dve.wait_ge(range_step, count[0])

            by_group = dst_f[:, :].rearrange("p (g e) -> p g e", g=2)
            link(nc.vector.tensor_reduce(low[:, :], by_group, AX.X, ALU.min))
            link(nc.vector.tensor_reduce(high[:, :], by_group, AX.X, ALU.max))
            dve.wait_ge(iotas, 5)
            link(nc.vector.tensor_scalar(first_less[:, :, :], group_col[:, :, :], -float(groups), None, ALU.add))
            link(nc.vector.tensor_scalar(last_less[:, :, :], group_col[:, :, :], -1.0, -1.0, ALU.mult, ALU.add))
            link(nc.vector.tensor_scalar(low_end[:, :], low[:, :], -float(R - 1), None, ALU.add))
            for g in range(2):
                link(nc.vector.tensor_scalar(begins[:, g, :], block_row[:, g, :], low_end[:, g:g + 1], None, ALU.is_ge))
                link(nc.vector.tensor_scalar(ends[:, g, :], block_row[:, g, :], high[:, g:g + 1], None, ALU.is_le))
            link(nc.vector.tensor_tensor(touches[:, :, :], begins[:, :, :], ends[:, :, :], ALU.mult))
            nc.vector.tensor_tensor(candidates[:, :, 0:tiles], touches[:, :, :], first_less[:, :, :], ALU.mult).then_inc(cand_ready, 1)
            nc.vector.tensor_tensor(candidates[:, :, tiles:2 * tiles], touches[:, :, :], last_less[:, :, :], ALU.mult).then_inc(cand_ready, 1)
            for n, col in enumerate((src_col, dst_col)):
                dve.wait_ge(edge_turned, n + 1)
                for g in range(2):
                    for q in range(DUO):
                        at = (g * DUO + q) * rows_in
                        last = nc.vector.tensor_copy(col[:, q, g:groups:2], ps[0:R, 2 + n, at:at + rows_in])
                last.then_inc(edge_cols, 1)
            dve.wait_ge(cand_turned, 1)
            nc.vector.tensor_reduce(extreme[:, :], ps[0:2 * tiles, 0, 0:groups], AX.X, ALU.min).then_inc(extreme_ready, 1)
            dve.wait_ge(extreme_turned, 1)
            link(nc.vector.tensor_scalar(bounds_f[:, 0:tiles], ps[0:1, 1, 0:tiles], float(groups), float(groups - 1), ALU.add, ALU.min))
            link(nc.vector.tensor_scalar(span_f[:, 0, :], ps[0:1, 1, tiles:2 * tiles], -1.0, None, ALU.mult))
            link(nc.vector.tensor_tensor(span_f[:, 1, :], span_f[:, 0, :], bounds_f[:, 0:tiles], ALU.subtract))
            link(nc.vector.tensor_scalar(span_f[:, 2, :], span_f[:, 1, :], 1.0 / visits, 0.5 - 0.5 / visits, ALU.mult, ALU.add))
            link(nc.vector.tensor_scalar(span_f[:, 3, :], span_f[:, 2, :], ROUND, None, ALU.add))
            link(nc.vector.tensor_scalar(bounds_f[:, tiles:2 * tiles], span_f[:, 3, :], -ROUND, 1.0, ALU.add, ALU.max))
            nc.vector.tensor_copy(bounds[:, :], bounds_f[:, :]).then_inc(bounds_ready, 1)
            dve.wait_ge(edge_cols, 2)
            dve.wait_ge(bounds_ready, 1)
            before = 0
            for b in range(tiles):
                start = dve.value_load(bounds[0:1, b:b + 1], min_val=0, max_val=groups - 1)
                rounds = dve.value_load(bounds[0:1, tiles + b:tiles + b + 1], min_val=1, max_val=groups // visits + 1)
                with dve.Fori(0, rounds) as k:
                    first = dve.snap(start + k * visits)
                    free = dve.snap((before + k) * visits)
                    for v in range(visits):
                        dve.wait_ge(hot_free, free + (v + 1))
                        for q in range(DUO):
                            nc.vector.tensor_scalar(src_hot[:, DUO * v + q, :], node_row[:, :], src_col[:, q, bass.ds(first + v, 1)],
                                                    None, ALU.is_equal)
                            last = nc.vector.tensor_scalar(dst_hot[:, DUO * v + q, :], node_row[:, b * R:(b + 1) * R],
                                                           dst_col[:, q, bass.ds(first + v, 1)], None, ALU.is_equal)
                        last.then_inc(hot_ready, 1)
                before = dve.snap(before + rounds)
                if b >= 1:
                    dve.wait_ge(root_ready, b)
                    nc.vector.reciprocal(dinv[:, b - 1:b], root[:, b - 1:b]).then_inc(dinv_ready, 1)
            dve.wait_ge(root_ready, tiles)
            nc.vector.reciprocal(dinv[:, tiles - 1:tiles], root[:, tiles - 1:tiles]).then_inc(dinv_ready, 1)

        @block.scalar
        def _(act):
            def scale_rows(b):
                act.wait_ge(loops_in, b + 1)
                act.wait_ge(dinv_ready, b + 1)
                nc.scalar.mul(rows[:, b % 3, :], rows[:, b % 3, :], dinv[:, b:b + 1]).then_inc(rows_scaled, 1)

            def blocks_out(b):
                for n, (t0, t1) in enumerate(turn_groups):
                    act.wait_ge(block_turned, 3 * b + n + 1)
                    nc.scalar.copy(adj[:, t0:t1, b * R:(b + 1) * R],
                                   ps[0:R, 6 + (b + n) % 2, 0:(t1 - t0) * R].rearrange("p (t n) -> p t n", n=R)).then_inc(block_out, 1)

            for b in range(tiles):
                if b >= 2:
                    blocks_out(b - 2)
                act.wait_ge(counted, b + 1)
                if b >= 3:
                    act.wait_ge(block_turned, 3 * (b - 2))
                nc.scalar.activation(rows[:, b % 3, :].rearrange("p (c n) -> p c n", n=part), count_rows(b),
                                     ACT.Identity, accum_out=degree[:, b:b + 1]).then_inc(counts_out, 1)
                act.wait_ge(counts_out, b + 1)
                nc.scalar.activation(root[:, b:b + 1], degree[:, b:b + 1], ACT.Sqrt, bias=1.0).then_inc(root_ready, 1)
                if b >= 1:
                    scale_rows(b - 1)
            scale_rows(tiles - 1)
            blocks_out(tiles - 2)
            blocks_out(tiles - 1)

        @block.tensor
        def _(pe):
            pe.wait_ge(edge_f, 2)
            for n, edges in enumerate((src_f, dst_f)):
                for q in range(2 * DUO):
                    last = nc.tensor.transpose(ps[0:R, 2 + n, q * rows_in:(q + 1) * rows_in], edges[:, q * R:(q + 1) * R],
                                               ident[0:rows_in, 0:rows_in])
                last.then_inc(edge_turned, 1)
            pe.wait_ge(cand_ready, 2)
            for g in range(2):
                last = nc.tensor.transpose(ps[0:2 * tiles, 0, g * rows_in:(g + 1) * rows_in], candidates[:, g, :],
                                           ident[0:rows_in, 0:rows_in])
            last.then_inc(cand_turned, 1)
            pe.wait_ge(extreme_ready, 1)
            nc.tensor.transpose(ps[0:1, 1, 0:2 * tiles], extreme[:, :], ident[0:2 * tiles, 0:2 * tiles]).then_inc(extreme_turned, 1)
            pe.wait_ge(bounds_ready, 1)
            pe.wait_ge(edge_cols, 2)
            pe.sem_inc(hot_free, visits)

            def turn(b):
                pe.wait_ge(rows_scaled, b + 1)
                for n, (t0, t1) in enumerate(turn_groups):
                    g = 3 * b + n
                    if g >= 2:
                        pe.wait_ge(block_out, g - 1)
                    for t in range(t0, t1):
                        last = nc.tensor.transpose(ps[0:R, 6 + (b + n) % 2, (t - t0) * R:(t - t0 + 1) * R],
                                                   rows[:, b % 3, t * R:(t + 1) * R], ident[0:R, 0:R])
                    last.then_inc(block_turned, 1)

            before = 0
            for b in range(tiles):
                if b >= 2:
                    pe.wait_ge(counts_out, b - 1)
                    turn(b - 2)
                rounds = pe.value_load(bounds[0:1, tiles + b:tiles + b + 1], min_val=1, max_val=groups // visits + 1)
                first = 3 * (b % 2)
                for c, width in enumerate((512, 512, 256)):
                    nc.tensor.matmul(ps[0:R, first + c, 0:width], zero_hot[:, 0:R], zero_hot[:, 0:width], start=True,
                                     stop=False, skip_group_check=True)
                with pe.Fori(0, rounds) as k:
                    ready = pe.snap((before + k) * visits)
                    for v in range(visits):
                        pe.wait_ge(hot_ready, ready + (v + 1))
                        for q in range(DUO * v, DUO * v + DUO):
                            for c in range(5):
                                last = nc.tensor.matmul(count_rows(b)[:, c, :], dst_hot[:, q, :],
                                                        src_hot[:, q, c * part:(c + 1) * part],
                                                        start=False, stop=False, skip_group_check=True)
                        last.then_inc(hot_free, 1)
                before = pe.snap(before + rounds)
                nc.tensor.matmul(ps[0:R, first, 0:256], zero_hot[:, 0:R], zero_hot[:, 0:256], start=False, stop=True,
                                 skip_group_check=True).then_inc(counted, 1)
            turn(tiles - 2)
            turn(tiles - 1)

def turn_normalised(nc, name, x_tiles, ident, turned_hi, turned_lo, eps, gain=None, offset=None, known=None,
                    rows_in=None):
    tiles = x_tiles.shape[1]
    width = x_tiles.shape[2]
    blocks = width // 128
    with ExitStack() as ctx:
        sb, banks, sem = tools(nc, ctx, name)
        stats = sb("stats", [R, 2, 6])
        moments = sb("moments", [R, tiles, 2]) if known is None else known
        root = sb("root", [R, tiles])
        scale = sb("scale", [R, tiles])
        eps_col = sb("eps_col", [R, 1])
        unit = sb("unit", [R, 2, width])
        affine = sb("affine", [128, 2, blocks * R])
        gains = sb("gains", [128, 2, blocks])
        ps = banks("ps", 2)
        eps_in = sem("eps_in")
        stats_ready = sem("stats_ready")
        moments_ready = sem("moments_ready")
        root_ready = sem("root_ready")
        scale_ready = sem("scale_ready")
        unit_ready = sem("unit_ready")
        turned = sem("turned")
        hi_ready = sem("hi_ready")
        lo_ready = sem("lo_ready")
        gains_in = sem("gains_in")
        affine_ready = sem("affine_ready")
        block = ctx.enter_context(nc.Block())

        def turned_view(n):
            return ps[:, n % 2, 0:blocks * R].rearrange("p (k n) -> p k n", n=R)

        @block.sync
        def _(sp):
            for n, row in enumerate((gain, offset)):
                if row is not None:
                    sp.dma_start(gains[:, n, :], row.rearrange("(k p) -> p k", p=128),
                                 allow_slow_non_contiguous=True).then_inc(gains_in, 16)

        @block.gpsimd
        def _(pool):
            nc.gpsimd.memset(eps_col[:, :], eps).then_inc(eps_in, 1)

        @block.vector
        def _(dve):
            if rows_in is not None:
                dve.wait_ge(rows_in, 16)
            for t in range(tiles if known is None else 0):
                if t >= 2:
                    dve.wait_ge(moments_ready, t - 1)
                nc.vector.bn_stats(stats[:, t % 2, :], x_tiles[:, t, :]).then_inc(stats_ready, 1)
                dve.wait_ge(stats_ready, t + 1)
                nc.vector.bn_aggr(moments[:, t, :], stats[:, t % 2, :]).then_inc(moments_ready, 1)
            dve.wait_ge(root_ready, 1)
            nc.vector.reciprocal(scale[:, :], root[:, :]).then_inc(scale_ready, 1)
            dve.wait_ge(scale_ready, 1)
            for t in range(tiles + 1):
                if t < tiles:
                    if t >= 2:
                        dve.wait_ge(turned, t - 1)
                    nc.vector.tensor_scalar(unit[:, t % 2, :], x_tiles[:, t, :], moments[:, t, 0:1], scale[:, t:t + 1],
                                            ALU.subtract, ALU.mult).then_inc(unit_ready, 1)
                if t >= 1:
                    n = t - 1
                    at = slice(n * R, (n + 1) * R)
                    if gain is not None:
                        dve.wait_ge(affine_ready, n + 1)
                        nc.vector.tensor_copy(turned_hi[:, :, at], affine[:, n % 2, :].rearrange("p (k n) -> p k n", n=R)).then_inc(hi_ready, 1)
                    dve.wait_ge(hi_ready, n + 1)
                    whole = turned_view(n) if gain is None else affine[:, n % 2, :].rearrange("p (k n) -> p k n", n=R)
                    nc.vector.tensor_tensor(turned_lo[:, :, at], whole, turned_hi[:, :, at].bitcast(F32),
                                            ALU.subtract).then_inc(lo_ready, 1)

        @block.scalar
        def _(act):
            if known is None:
                act.wait_ge(moments_ready, tiles)
            act.wait_ge(eps_in, 1)
            nc.scalar.activation(root[:, :], moments[:, :, 1], ACT.Sqrt, bias=eps_col[:, 0:1]).then_inc(root_ready, 1)
            for t in range(tiles):
                act.wait_ge(turned, t + 1)
                whole = turned_view(t)
                if gain is not None:
                    act.wait_ge(gains_in, 32)
                    if t >= 2:
                        act.wait_ge(lo_ready, t - 1)
                    whole = affine[:, t % 2, :].rearrange("p (k n) -> p k n", n=R)
                    for k in range(blocks):
                        last = nc.scalar.activation(whole[:, k, :], turned_view(t)[:, k, :], ACT.Identity,
                                                    scale=gains[:, 0, k:k + 1], bias=gains[:, 1, k:k + 1])
                    last.then_inc(affine_ready, 1)
                else:
                    nc.scalar.copy(turned_hi[:, :, t * R:(t + 1) * R], whole).then_inc(hi_ready, 1)

        @block.tensor
        def _(pe):
            for t in range(tiles):
                pe.wait_ge(unit_ready, t + 1)
                if t >= 2:
                    pe.wait_ge(lo_ready, t - 1)
                for k in range(blocks):
                    last = nc.tensor.transpose(turned_view(t)[:, k, :], unit[:, t % 2, k * 128:(k + 1) * 128],
                                               ident[0:R, 0:R])
                last.then_inc(turned, 1)


def spans(width, step):
    return [(a, min(a + step, width)) for a in range(0, width, step)]


def graph_layers(nc, turned_hi, turned_lo, adj, dinv, weights, biases, kept):
    n_nodes = adj.shape[2]
    tiles = n_nodes // R
    chunks = spans(n_nodes, 500)
    sizes = [tuple(w.shape) for w in weights]
    with ExitStack() as ctx:
        sb, banks, sem = tools(nc, ctx, "graph")
        w1 = sb("w1", [128, sizes[0][0] // 128, sizes[0][1]])
        w1_hi = sb("w1_hi", [128, sizes[0][0] // 128, sizes[0][1]], F32R)
        w1_lo = sb("w1_lo", [128, sizes[0][0] // 128, sizes[0][1]], F32R)
        w2 = sb("w2", [128, sizes[1][0] // 128, sizes[1][1]])
        w3 = sb("w3", [128, sizes[2][0] // 128, sizes[2][1]])
        bias = sb("bias", [128, 4])
        projected = sb("projected", [R, tiles, sizes[0][1]])
        ps = banks("ps", 8)
        w1_in = sem("w1_in")
        w_in = sem("w_in")
        w1_part = sem("w1_part")
        rows_done = sem("rows_done")
        rows_out = sem("rows_out")
        gathered = sem("gathered")
        kept_ready = sem("kept_ready")
        block = ctx.enter_context(nc.Block())
        layers = [(None, 4, None, 2, 0), (w2, 2, 0, 1, 2), (w3, 1, 2, 1, 3)]

        @block.sync
        def _(sp):
            sp.dma_start(w1[:, :, :], weights[0].rearrange("(k p) n -> p k n", p=128)).then_inc(w1_in, 16)
            sp.dma_start(w2[:, :, :], weights[1].rearrange("(k p) n -> p k n", p=128)).then_inc(w_in, 16)
            sp.dma_start(w3[:, :, :], weights[2].rearrange("(k p) n -> p k n", p=128)).then_inc(w_in, 16)
            at = 0
            for b in biases:
                m = b.shape[0] // 128
                sp.dma_start(bias[:, at:at + m], b.rearrange("(m p) -> p m", p=128),
                             allow_slow_non_contiguous=True).then_inc(w_in, 16)
                at += m

        @block.vector
        def _(dve):
            dve.wait_ge(w1_in, 16)
            nc.vector.tensor_copy(w1_hi[:, :, :], w1[:, :, :]).then_inc(w1_part, 1)
            dve.wait_ge(w1_part, 1)
            nc.vector.tensor_tensor(w1_lo[:, :, :], w1[:, :, :], w1_hi[:, :, :].bitcast(F32), ALU.subtract).then_inc(w1_part, 1)
            done = 0
            for n in range(3):
                wide = sizes[n][1]
                for t in range(tiles):
                    dve.wait_ge(rows_done, done + 1)
                    if n and t == 0:
                        dve.wait_ge(gathered, (2, 3)[n - 1])
                    nc.vector.tensor_scalar(projected[:, t, 0:wide], ps[0:R, 6 + t % 2, 0:wide], dinv[:, t:t + 1], None,
                                            ALU.mult).then_inc(rows_out, 1)
                    done += 1

        @block.scalar
        def _(act):
            act.wait_ge(w_in, 16 * 5)
            done = 0
            for n in range(3):
                _, _, _, out_blocks, first = layers[n]
                for m in range(out_blocks):
                    act.wait_ge(gathered, done + 1)
                    for c, (a, b) in enumerate(chunks):
                        nc.scalar.activation(kept[:, first + m, a:b], ps[:, 3 * (done % 2) + c, 0:b - a], ACT.Relu,
                                             bias=bias[:, first + m:first + m + 1]).then_inc(kept_ready, 1)
                    done += 1

        @block.tensor
        def _(pe):
            pe.wait_ge(w1_part, 2)
            pe.wait_ge(w_in, 16 * 5)
            rows = 0
            done = 0
            for n in range(3):
                w, depth, source, out_blocks, first = layers[n]
                wide = sizes[n][1]
                if n:
                    pe.wait_ge(kept_ready, len(chunks) * done)
                for t in range(tiles):
                    if rows >= 2:
                        pe.wait_ge(rows_out, rows - 1)
                    to = ps[0:R, 6 + t % 2, 0:wide]
                    at = slice(t * R, (t + 1) * R)
                    for k in range(depth):
                        if n:
                            last = nc.tensor.matmul(to, kept[:, source + k, at], w[:, k, :],
                                                    start=(k == 0), stop=(k == depth - 1))
                        else:
                            nc.tensor.matmul(to, turned_hi[:, k, at], w1_hi[:, k, :], start=(k == 0), stop=False)
                            nc.tensor.matmul(to, turned_hi[:, k, at], w1_lo[:, k, :], start=False, stop=False)
                            last = nc.tensor.matmul(to, turned_lo[:, k, at], w1_hi[:, k, :],
                                                    start=False, stop=(k == depth - 1))
                    last.then_inc(rows_done, 1)
                    rows += 1
                for m in range(out_blocks):
                    if done >= 2:
                        pe.wait_ge(kept_ready, len(chunks) * (done - 1))
                    for t in range(tiles):
                        if m == 0:
                            pe.wait_ge(rows_out, rows - tiles + t + 1)
                        for c, (a, b) in enumerate(chunks):
                            last = nc.tensor.matmul(ps[:, 3 * (done % 2) + c, 0:b - a], projected[:, t, m * 128:(m + 1) * 128],
                                                    adj[:, t, a:b], start=(t == 0), stop=(t == tiles - 1))
                    last.then_inc(gathered, 1)
                    done += 1

PAIR = 128
CODES = 64


def splat_constants(nc, a, ident, center_hi, center_lo, columns, part_mask, head_sum, inv_temp, x, x_tiles, x_in):
    heads, splats, depth = a["base_centers"].shape
    pairs = heads // 2
    with ExitStack() as ctx:
        sb, banks, sem = tools(nc, ctx, "splats")
        base = sb("base", [128, pairs, 128])
        delta = sb("delta", [128, pairs, 128])
        log_scale = sb("log_scale", [128, pairs])
        log_amp = sb("log_amp", [128, pairs])
        move = sb("move", [128, 1])
        move_exp = sb("move_exp", [128, 1])
        move_one = sb("move_one", [128, 1])
        move_rec = sb("move_rec", [128, 1])
        move_by = sb("move_by", [128, 1])
        temp = sb("temp", [R, 1])
        temp_max = sb("temp_max", [R, 1])
        centers = sb("centers", [128, pairs, 128])
        squares = sb("squares", [128, pairs, 128])
        center_sq = sb("center_sq", [128, pairs])
        scales = sb("scales", [128, pairs])
        clipped = sb("clipped", [128, pairs])
        scale_sq = sb("scale_sq", [128, pairs])
        var_eps = sb("var_eps", [128, pairs])
        inv_var = sb("inv_var", [128, pairs])
        amps = sb("amps", [128, pairs])
        kept_amp = sb("kept_amp", [128, pairs])
        mask_rows = sb("mask_rows", [1, 3, 128])
        keep_rows = sb("keep_rows", [128, 1])
        center_f = sb("center_f", [128, pairs, 128])
        ps = banks("ps", 2)
        cleared = sem("cleared")
        loaded = sem("loaded")
        exps = sem("exps")
        step = sem("step")
        centers_ready = sem("centers_ready")
        centers_turned = sem("centers_turned")
        masks_turned = sem("masks_turned")
        halved = sem("halved")
        block = ctx.enter_context(nc.Block())

        @block.gpsimd
        def _(pool):
            for tile in (base, delta):
                nc.gpsimd.memset(tile[:, :, :], 0.0)
            nc.gpsimd.memset(log_scale[:, :], 0.0)
            nc.gpsimd.memset(log_amp[:, :], 0.0)
            nc.gpsimd.memset(mask_rows[:, :, :], 0.0)
            nc.gpsimd.memset(head_sum[:, :].bitcast(F32), 0.0).then_inc(cleared, 1)
            pool.wait_ge(cleared, 1)
            for h in range(2):
                at = CODES * h
                nc.gpsimd.memset(mask_rows[:, 0, at + splats:at + 2 * splats], 1.0)
                nc.gpsimd.memset(mask_rows[:, 1, at + 2 * splats:at + 3 * splats], 1.0)
                nc.gpsimd.memset(mask_rows[:, 2, at:at + 3 * splats], 1.0)
                last = nc.gpsimd.memset(head_sum[depth * h:depth * (h + 1), at:at + 3 * splats].bitcast(F32), 1.0)
            last.then_inc(cleared, 1)

        @block.sync
        def _(sp):
            sp.wait_ge(cleared, 1)
            for h in range(2):
                for r in range(3):
                    rows = slice(CODES * h + splats * r, CODES * h + splats * (r + 1))
                    own = slice(depth * h, depth * (h + 1))
                    for to, name in ((base, "base_centers"), (delta, "center_deltas")):
                        sp.dma_start(to[rows, :, own], a[name].rearrange("(p h) s d -> h s p d", h=2)[h]).then_inc(loaded, 16)
                    for to, name in ((log_scale, "log_scales"), (log_amp, "log_amps")):
                        sp.dma_start(to[rows, :], a[name].rearrange("(p h) s -> h s p", h=2)[h],
                                     allow_slow_non_contiguous=True).then_inc(loaded, 16)
            sp.dma_start(move[:, :], a["movement_scale_param"].partition_broadcast(128)).then_inc(loaded, 16)
            sp.dma_start(temp[:, :], a["temperature"].partition_broadcast(R)).then_inc(loaded, 16)
            sp.dma_start(x_tiles[:, :, :], x.rearrange("(t p) n -> p t n", p=R)).then_inc(x_in, 16)

        @block.scalar
        def _(act):
            act.wait_ge(loaded, 16 * 26)
            nc.scalar.activation(move_exp[:, :], move[:, :], ACT.Exp, scale=-1.0).then_inc(exps, 1)
            nc.scalar.activation(scales[:, :], log_scale[:, :], ACT.Exp).then_inc(exps, 1)
            nc.scalar.activation(amps[:, :], log_amp[:, :], ACT.Exp).then_inc(exps, 1)
            act.wait_ge(centers_turned, 1)
            nc.scalar.mul(center_hi[:, :, :], ps[:, 0, :].rearrange("p (n m) -> p n m", n=pairs), -2.0)
            nc.scalar.mul(center_f[:, :, :], ps[:, 0, :].rearrange("p (n m) -> p n m", n=pairs), -2.0).then_inc(halved, 1)

        @block.vector
        def _(dve):
            count = [0]

            def link(instruction):
                count[0] += 1
                instruction.then_inc(step, 1)
                dve.wait_ge(step, count[0])

            dve.wait_ge(loaded, 16 * 26)
            dve.wait_ge(exps, 3)
            link(nc.vector.tensor_scalar(move_one[:, :], move_exp[:, :], 1.0, None, ALU.add))
            link(nc.vector.reciprocal(move_rec[:, :], move_one[:, :]))
            link(nc.vector.tensor_scalar(move_by[:, :], move_rec[:, :], 0.1, None, ALU.mult))
            link(nc.vector.scalar_tensor_tensor(out=centers[:, :, :], in0=delta[:, :, :], scalar=move_by[:, 0:1],
                                                in1=base[:, :, :], op0=ALU.mult, op1=ALU.add))
            nc.vector.tensor_copy(center_f[:, :, :], centers[:, :, :]).then_inc(centers_ready, 1)
            link(nc.vector.tensor_tensor(squares[:, :, :], centers[:, :, :], centers[:, :, :], ALU.mult))
            link(nc.vector.tensor_reduce(center_sq[:, :], squares[:, :, :], AX.X, ALU.add))
            link(nc.vector.tensor_scalar(clipped[:, :], scales[:, :], 0.0001, 2.0, ALU.max, ALU.min))
            link(nc.vector.tensor_tensor(scale_sq[:, :], clipped[:, :], clipped[:, :], ALU.mult))
            link(nc.vector.tensor_scalar(var_eps[:, :], scale_sq[:, :], 1e-8, None, ALU.add))
            link(nc.vector.reciprocal(inv_var[:, :], var_eps[:, :]))
            link(nc.vector.tensor_scalar(columns[:, 0, :], inv_var[:, :], -0.5, None, ALU.mult))
            link(nc.vector.tensor_tensor(columns[:, 1, :], columns[:, 0, :], center_sq[:, :], ALU.mult))
            link(nc.vector.tensor_scalar(kept_amp[:, :], amps[:, :], 0.02, None, ALU.is_gt))
            link(nc.vector.tensor_tensor(columns[:, 3, :], kept_amp[:, :], amps[:, :], ALU.mult))
            dve.wait_ge(masks_turned, 1)
            link(nc.vector.tensor_scalar(part_mask[:, :], ps[:, 1, 0:2], -1.0, None, ALU.mult))
            link(nc.vector.tensor_copy(keep_rows[:, :], ps[:, 1, 2:3]))
            link(nc.vector.tensor_scalar(columns[:, 2, :], columns[:, 3, :], keep_rows[:, 0:1], None, ALU.mult))
            link(nc.vector.tensor_scalar(temp_max[:, :], temp[:, :], 0.1, None, ALU.max))
            link(nc.vector.reciprocal(inv_temp[:, :], temp_max[:, :]))
            dve.wait_ge(halved, 1)
            nc.vector.tensor_tensor(center_lo[:, :, :], center_f[:, :, :], center_hi[:, :, :].bitcast(F32), ALU.subtract)

        @block.tensor
        def _(pe):
            pe.wait_ge(cleared, 2)
            for n in range(3):
                last = nc.tensor.matmul(ps[:, 1, n:n + 1], mask_rows[:, n, :], ident[0:1, 0:1], start=True, stop=True)
            last.then_inc(masks_turned, 1)
            pe.wait_ge(centers_ready, 1)
            for p in range(pairs):
                last = nc.tensor.transpose(ps[:, 0, p * 128:(p + 1) * 128], center_f[:, p, :], ident[:, :])
            last.then_inc(centers_turned, 1)


def attention(nc, a, center_hi, center_lo, columns, part_mask, head_sum, inv_temp, ident, x_hi, x_lo, attended):
    n_nodes = x_hi.shape[2]
    tiles = n_nodes // R
    pairs = a["base_centers"].shape[0] // 2
    splats = a["base_centers"].shape[1]
    depth = a["base_centers"].shape[2]
    features = x_hi.shape[1] * 128
    blocks = x_hi.shape[1]
    wide = attended.shape[2]
    quarter = wide // 4
    slots = 2 * tiles
    parts = spans(n_nodes, 418)
    v_groups = [(0, 3), (3, 6), (6, 8), (8, tiles)]

    prepare = ([("w", n) for n in range(3)] + [("q", c) for c in range(3)] + [("q_dist", c) for c in range(3)]
               + [("k", c) for c in range(3)] + [("k_dist", c) for c in range(3)]
               + [("v", c) for c in range(3)] + [("v_turn", g) for g in range(len(v_groups))])
    q_and_k = prepare.index(("v", 0))
    scalar_order = [step for step in prepare if step[0] != "v"]
    maxima = [("max", m) for m in range(3 * tiles)] + [("turn", 0)]
    opening = prepare[:q_and_k]
    for i, step in enumerate(maxima):
        opening += [step] + (prepare[q_and_k + i // 3:][:1] if i % 3 == 0 and i // 3 < len(prepare) - q_and_k else [])
    head_count = len(prepare) + len(maxima)
    pair_count = len(prepare) + 2 * len(maxima)

    def side_steps(more):
        number = 0
        plan = []
        for h in range(2):
            first = (3, 3 * tiles // 2 - 2)[h]
            left = (prepare[:q_and_k], prepare[q_and_k:])[h] if more else []
            for n in range(slots):
                steps = []
                if (h == 0 or more) and 1 <= n <= 3 * tiles // 2:
                    steps += maxima[2 * n - 2:2 * n]
                if (h == 0 or more) and n == 3 * tiles // 2 + 2:
                    steps += maxima[-1:]
                if 0 <= n - first < len(left):
                    steps.insert(1, left[n - first])
                plan.append([(number + i, kind, index) for i, (kind, index) in enumerate(steps)])
                number += len(steps)
        return plan[:slots], plan[slots:]

    def head_steps(h, more):
        return side_steps(more)[h]

    with ExitStack() as ctx:
        sb, banks, sem = tools(nc, ctx, "attention")
        own_hi = sb("own_hi", [128, 128], F32R)
        own_lo = sb("own_lo", [128, 128], F32R)
        own_cols = sb("own_cols", [128, 4])
        raw = sb("raw", [128, 3, features])
        w_hi = sb("w_hi", [128, 3, blocks, 128], F32R)
        w_lo = sb("w_lo", [128, 3, blocks, 128], F32R)
        side_hi = sb("side_hi", [128, n_nodes], F32R)
        side_lo = sb("side_lo", [128, n_nodes], F32R)
        square = sb("square", [128, 2, 418])
        square_hi = sb("square_hi", [128, n_nodes], F32R)
        square_lo = sb("square_lo", [128, n_nodes], F32R)
        weight = sb("weight", [128, 2, 418])
        weight_amp = sb("weight_amp", [128, 2, n_nodes])
        weight_hi = sb("weight_hi", [128, 2, n_nodes], F32R)
        q_stack = sb("q_stack", [128, 2, wide], F32R)
        k_stack = sb("k_stack", [128, wide], F32R)
        k_next = sb("k_next", [128, wide], F32R)
        v_rows = sb("v_rows", [128, n_nodes])
        v_hi = sb("v_hi", [R, tiles, 2, depth + 1], F32R)
        v_lo = sb("v_lo", [R, tiles, 2, depth + 1], F32R)
        v_next_hi = sb("v_next_hi", [R, tiles, 2, depth], F32R)
        v_next_lo = sb("v_next_lo", [R, tiles, 2, depth], F32R)
        part_max = sb("part_max", [R, tiles, 3])
        row_max = sb("row_max", [R, tiles])
        shift = sb("shift", [tiles, R])
        shift_hi = sb("shift_hi", [tiles, R], F32R)
        shift_lo = sb("shift_lo", [tiles, R], F32R)
        prob = sb("prob", [R, 2, 2 * quarter])
        prob_hi = sb("prob_hi", [R, 3, 2 * quarter], F32R)
        prob_lo = sb("prob_lo", [R, 3, 2 * quarter], F32R)
        mixed = sb("mixed", [depth + 1, 2, 2 * quarter])
        ps = banks("ps", 8)

        sem = cleared_semaphores(nc, ctx, "attention")
        names = ("ready raw_in raw_free own_in side_ready side_scaled side_free squares_parted squares_ready weights_parted "
                 "k_next_in k_in q_in v_in v_freed max_ready shift_parted shift_in logits_ready prob_ready prob_hi_ready prob_lo_ready "
                 "mixed_out mix_step")
        s = {name: sem(name) for name in names.split()}
        stored = [sem("stored_0"), sem("stored_1")]
        block = ctx.enter_context(nc.Block())

        def first_number(p):
            return p * pair_count + head_count

        def bank(number, in_loop):
            return (number + (head_count if in_loop else 0)) % 2

        def back(n):
            return 1 if n < 2 else 2

        def pair_of_banks(first, rows):
            return ps[0:rows, first:first + 2, 0:quarter]

        def turned_v(at_bank, g):
            t0, t1 = v_groups[g]
            return ps[0:R, at_bank, 0:(t1 - t0) * 128].rearrange("p (t h d) -> p t h d", h=2, d=depth)

        def turned_w(at_bank):
            return ps[:, at_bank, :].rearrange("p (k n) -> p k n", n=128)

        @block.sync
        def _(sp):
            def load(n):
                for m in range(3):
                    sp.dma_start(raw[:, m, :], a["qkv_w"][bass.ds(n * PAIR + m * features, PAIR), :]).then_inc(s["raw_in"], 16)

            def send_shift(head, h):
                row = CODES * h + 3 * splats
                sp.wait_ge(s["shift_parted"], head * 2 + 2)
                sp.dma_start(q_stack[row:row + 1, h, 0:n_nodes].bitcast(F32), shift_hi[:, :].bitcast(F32)).then_inc(s["shift_in"], 16)
                sp.dma_start(q_stack[row + 1:row + 2, h, 0:n_nodes].bitcast(F32), shift_lo[:, :].bitcast(F32)).then_inc(s["shift_in"], 16)

            def store(p, h, half):
                sp.wait_ge(s["mixed_out"], p * 4 + 2 * h + half + 2)
                sp.dma_start(attended[bass.ds(p * 2 + h, 1), :, 2 * quarter * half:2 * quarter * (half + 1)].rearrange("a d n -> (a d) n"),
                             mixed[:, half, :]).then_inc(stored[half], 16)

            def one_pair(p, more):
                if more:
                    sp.wait_ge(s["raw_free"], p + 1)
                    load(p + 1)
                for h in range(2):
                    store(p, h, 0)
                    if h == 0 or more:
                        send_shift(p * 2 + h + 1, 1 - h)
                    store(p, h, 1)

            load(0)
            send_shift(0, 0)
            with sp.Fori(0, pairs - 1) as p:
                one_pair(p, True)
            one_pair(pairs - 1, False)
            for half in range(2):
                sp.wait_ge(stored[half], 16 * (2 * pairs + 1))

        @block.gpsimd
        def _(pool):
            nc.gpsimd.memset(q_stack[:, :, :].bitcast(F32), 0.0).then_inc(s["ready"], 1)
            nc.gpsimd.memset(k_stack[:, :].bitcast(F32), 0.0).then_inc(s["ready"], 1)
            nc.gpsimd.memset(v_hi[:, :, :, :].bitcast(F32), 1.0).then_inc(s["ready"], 1)
            nc.gpsimd.memset(v_lo[:, :, :, :].bitcast(F32), 0.0).then_inc(s["ready"], 1)
            for half in range(2):
                pool.sem_inc(stored[half], 16)

            def own(n):
                nc.gpsimd.tensor_copy(own_hi[:, :], center_hi[:, bass.ds(n, 1), :].rearrange("p a n -> p (a n)").bitcast(F32))
                nc.gpsimd.tensor_copy(own_lo[:, :], center_lo[:, bass.ds(n, 1), :].rearrange("p a n -> p (a n)").bitcast(F32))
                nc.gpsimd.tensor_copy(own_cols[:, :], columns[:, :, bass.ds(n, 1)].rearrange("p c a -> p (c a)")).then_inc(s["own_in"], 1)

            def head_v(h):
                nc.gpsimd.tensor_copy(v_hi[:, :, h, 0:depth], v_next_hi[:, :, h, :].bitcast(F32))
                nc.gpsimd.tensor_copy(v_lo[:, :, h, 0:depth], v_next_lo[:, :, h, :].bitcast(F32)).then_inc(s["v_in"], 1)

            pool.wait_ge(s["ready"], 4)
            own(0)
            pool.wait_ge(s["side_free"], opening.index(prepare[-1]) + 1)
            head_v(0)
            head_v(1)
            last_turn = max(number for slot in head_steps(1, True) for number, kind, _ in slot if kind == "v_turn")
            with pool.Fori(0, pairs - 1) as p:
                pool.wait_ge(s["weights_parted"], p * 6 + 6)
                own(p + 1)
                pool.wait_ge(s["side_free"], first_number(p) + last_turn + 1)
                for h in range(2):
                    pool.wait_ge(s["mix_step"], (p * 2 + h + 1) * slots)
                    pool.sem_inc(s["v_freed"], 1)
                    head_v(h)

        @block.vector
        def _(dve):
            def write_q(n, h):
                rows = slice(CODES * h, CODES * (h + 1))
                dve.wait_ge(s["weights_parted"], n * 6 + 3)
                nc.vector.scalar_tensor_tensor(out=q_stack[rows, h, 0:n_nodes], in0=weight_hi[rows, 0, :].bitcast(F32),
                                               scalar=part_mask[rows, 0:1], in1=weight_amp[rows, 0, :],
                                               op0=ALU.mult, op1=ALU.add).then_inc(s["q_in"], 1)

            def copy_k(n):
                dve.wait_ge(s["k_next_in"], n * 3 + 3)
                nc.vector.tensor_copy(k_stack[:, 0:n_nodes], k_next[:, 0:n_nodes].bitcast(F32)).then_inc(s["k_in"], 1)

            def side(step, first, n, head, in_loop, started):
                number, kind, i = step
                held = bank(number, in_loop)
                a0, a1 = parts[i] if kind in ("q", "k", "v", "q_dist", "k_dist") else (0, 0)
                if (kind, i) in scalar_order:
                    dve.wait_ge(s["side_scaled"], n * len(scalar_order) + scalar_order.index((kind, i)) + 1)
                else:
                    dve.wait_ge(s["side_ready"], first + number + 1)
                if kind == "w":
                    nc.vector.tensor_tensor(w_lo[:, i, :, :], turned_w(held), w_hi[:, i, :, :].bitcast(F32), ALU.subtract).then_inc(s["side_free"], 1)
                elif kind in ("q", "k"):
                    at = n * 6 + (0 if kind == "q" else 3) + i
                    nc.vector.tensor_tensor(side_lo[:, a0:a1], ps[:, held, 0:a1 - a0], side_hi[:, a0:a1].bitcast(F32), ALU.subtract).then_inc(s["side_free"], 1)
                    nc.vector.tensor_copy(square_hi[:, a0:a1], square[:, i % 2, 0:a1 - a0]).then_inc(s["squares_parted"], 1)
                    dve.wait_ge(s["squares_parted"], at + 1)
                    nc.vector.tensor_tensor(square_lo[:, a0:a1], square[:, i % 2, 0:a1 - a0], square_hi[:, a0:a1].bitcast(F32),
                                            ALU.subtract).then_inc(s["squares_ready"], 1)
                elif kind in ("q_dist", "k_dist"):
                    m = 0 if kind == "q_dist" else 1
                    if started:
                        dve.wait_ge(*((s["q_in"], n * 2) if m == 0 else (s["k_next_in"], n * 3)))
                    nc.vector.tensor_scalar(weight_amp[:, m, a0:a1], weight[:, i % 2, 0:a1 - a0], own_cols[:, 2 + m:3 + m], None,
                                            ALU.mult).then_inc(s["side_free"], 1)
                    dve.wait_ge(s["side_free"], first + number + 1)
                    nc.vector.tensor_copy(weight_hi[:, m, a0:a1], weight_amp[:, m, a0:a1]).then_inc(s["weights_parted"], 1)
                    if m == 1:
                        dve.wait_ge(s["weights_parted"], n * 6 + 4 + i)
                        if started:
                            dve.wait_ge(s["k_in"], n)
                        nc.vector.scalar_tensor_tensor(out=k_next[:, a0:a1], in0=weight_hi[:, 1, a0:a1].bitcast(F32),
                                                       scalar=part_mask[:, 1:2], in1=weight_amp[:, 1, a0:a1],
                                                       op0=ALU.mult, op1=ALU.add).then_inc(s["k_next_in"], 1)
                elif kind == "v":
                    nc.vector.tensor_copy(v_rows[:, a0:a1], ps[:, held, 0:a1 - a0]).then_inc(s["side_free"], 1)
                elif kind == "v_turn":
                    t0, t1 = v_groups[i]
                    nc.vector.tensor_tensor(v_next_lo[:, t0:t1, :, :], turned_v(held, i), v_next_hi[:, t0:t1, :, :].bitcast(F32),
                                            ALU.subtract).then_inc(s["side_free"], 1)
                elif kind == "max":
                    t, c = divmod(i, 3)
                    if i == 0 and started:
                        dve.wait_ge(s["max_ready"], head)
                    nc.vector.tensor_reduce(part_max[:, t, c:c + 1], ps[0:R, held, 0:parts[c][1] - parts[c][0]], AX.X, ALU.max).then_inc(s["side_free"], 1)
                    if i == 3 * tiles - 1:
                        dve.wait_ge(s["side_free"], first + number + 1)
                        nc.vector.tensor_reduce(row_max[:, :], part_max[:, :, :], AX.X, ALU.max).then_inc(s["max_ready"], 1)
                elif kind == "turn":
                    if started:
                        dve.wait_ge(s["shift_parted"], head * 2)
                        dve.wait_ge(s["shift_in"], head * 32)
                    nc.vector.tensor_scalar(shift[:, :], ps[0:tiles, held, 0:R], -1.0, None, ALU.mult).then_inc(s["side_free"], 1)
                    dve.wait_ge(s["side_free"], first + number + 1)
                    nc.vector.tensor_copy(shift_hi[:, :], shift[:, :]).then_inc(s["shift_parted"], 1)
                    dve.wait_ge(s["shift_parted"], head * 2 + 1)
                    nc.vector.tensor_tensor(shift_lo[:, :], shift[:, :], shift_hi[:, :].bitcast(F32), ALU.subtract).then_inc(s["shift_parted"], 1)

            def one_pair(p, more):
                for h in range(2):
                    for n in range(slots):
                        at = (p * 2 + h) * slots + n
                        if h == 1 and more and n == slots - 1:
                            dve.wait_ge(s["logits_ready"], at + 1)
                            copy_k(p + 1)
                        dve.wait_ge(s["prob_hi_ready"], at + 1)
                        if n >= 3 or h == 1:
                            dve.wait_ge(s["mix_step"], at - back(n))
                        nc.vector.tensor_tensor(prob_lo[:, n % 3, :], prob[:, n % 2, :], prob_hi[:, n % 3, :].bitcast(F32),
                                                ALU.subtract).then_inc(s["prob_lo_ready"], 1)
                        if n == 0 and (h == 0 or more):
                            if h == 1:
                                dve.wait_ge(s["logits_ready"], at)
                            write_q(p + h, 1 - h)
                        for step in head_steps(h, more)[n]:
                            side(step, first_number(p), p + 1, p * 2 + h + 1, True, True)

            dve.wait_ge(s["ready"], 4)
            for number, (kind, i) in enumerate(opening):
                if kind == "max" and i == 0:
                    write_q(0, 0)
                    copy_k(0)
                side((number, kind, i), 0, 0, 0, False, False)
            with dve.Fori(0, pairs - 1) as p:
                one_pair(p, True)
            one_pair(pairs - 1, False)

        @block.scalar
        def _(act):
            def side(step, first, n, in_loop, started):
                number, kind, i = step
                if (kind, i) not in scalar_order:
                    return
                held = bank(number, in_loop)
                a0, a1 = parts[i] if kind in ("q", "k", "q_dist", "k_dist") else (0, 0)
                act.wait_ge(s["side_ready"], first + number + 1)
                if kind == "w":
                    nc.scalar.copy(w_hi[:, i, :, :], turned_w(held)).then_inc(s["side_scaled"], 1)
                elif kind in ("q", "k"):
                    at = n * 6 + (0 if kind == "q" else 3) + i
                    nc.scalar.copy(side_hi[:, a0:a1], ps[:, held, 0:a1 - a0])
                    if kind == "k" or i >= 2:
                        act.wait_ge(s["squares_ready"], at - (1 if i == 1 or i == 2 else 0))
                    nc.scalar.activation(square[:, i % 2, 0:a1 - a0], ps[:, held, 0:a1 - a0], ACT.Square).then_inc(s["side_scaled"], 1)
                elif kind in ("q_dist", "k_dist"):
                    act.wait_ge(s["own_in"], n + 1)
                    nc.scalar.activation(weight[:, i % 2, 0:a1 - a0], ps[:, held, 0:a1 - a0], ACT.Exp, scale=own_cols[:, 0:1],
                                         bias=own_cols[:, 1:2]).then_inc(s["side_scaled"], 1)
                elif kind == "v_turn":
                    t0, t1 = v_groups[i]
                    if started:
                        act.wait_ge(s["v_in"], n * 2)
                    nc.scalar.copy(v_next_hi[:, t0:t1, :, :], turned_v(held, i)).then_inc(s["side_scaled"], 1)

            def mix_out(p, h, half):
                act.wait_ge(s["mix_step"], (p * 2 + h) * slots + (half + 1) * tiles)
                act.wait_ge(stored[half], (p * 2 + h + 1) * 16)
                nc.scalar.copy(mixed[:, half, :].rearrange("p (a n) -> p a n", a=2), pair_of_banks(6, depth + 1)).then_inc(s["mixed_out"], 1)

            def one_pair(p, more):
                for h in range(2):
                    for n in range(slots):
                        at = (p * 2 + h) * slots + n
                        act.wait_ge(s["logits_ready"], at + 1)
                        if n >= 2 or h == 1:
                            act.wait_ge(s["prob_lo_ready"], at - 1)
                        nc.scalar.activation(prob[:, n % 2, :].rearrange("p (a n) -> p a n", a=2), pair_of_banks(2 + 2 * (n % 2), R),
                                             ACT.Exp, scale=inv_temp[:, 0:1]).then_inc(s["prob_ready"], 1)
                        act.wait_ge(s["prob_ready"], at + 1)
                        if n >= 3 or h == 1:
                            act.wait_ge(s["mix_step"], at - back(n))
                        nc.scalar.copy(prob_hi[:, n % 3, :], prob[:, n % 2, :]).then_inc(s["prob_hi_ready"], 1)
                        if n == 0 and h == 1:
                            mix_out(p, 0, 1)
                        if n == tiles:
                            mix_out(p, h, 0)
                        for step in head_steps(h, more)[n]:
                            side(step, first_number(p), p + 1, True, True)
                mix_out(p, 1, 1)

            act.sem_inc(s["mixed_out"], 1)
            act.wait_ge(s["ready"], 4)
            for number, (kind, i) in enumerate(opening):
                side((number, kind, i), 0, 0, False, False)
            with act.Fori(0, pairs - 1) as p:
                one_pair(p, True)
            one_pair(pairs - 1, False)

        @block.tensor
        def _(pe):
            def side(step, first, n, head, h, in_loop):
                number, kind, i = step
                held = bank(number, in_loop)
                a0, a1 = parts[i] if kind in ("q", "k", "v", "q_dist", "k_dist") else (0, 0)
                to = ps[:, held, 0:a1 - a0]
                if in_loop or number >= 2:
                    pe.wait_ge(s["side_free"], first + number - 1)
                if kind == "w":
                    pe.wait_ge(s["raw_in"], n * 48 + 48)
                    for k in range(blocks):
                        last = nc.tensor.transpose(turned_w(held)[:, k, :], raw[:, i, k * 128:(k + 1) * 128], ident[:, :])
                elif kind in ("q", "k", "v"):
                    m = "qkv".index(kind)
                    for k in range(blocks):
                        for x in (x_hi, x_lo):
                            nc.tensor.matmul(to, w_hi[:, m, k, :], x[:, k, a0:a1], start=(k == 0 and x is x_hi), stop=False)
                        last = nc.tensor.matmul(to, w_lo[:, m, k, :], x_hi[:, k, a0:a1], start=False, stop=(k == blocks - 1))
                elif kind in ("q_dist", "k_dist"):
                    pe.wait_ge(s["own_in"], n + 1)
                    pe.wait_ge(s["squares_ready"], n * 6 + (1 if kind == "q_dist" else 4) + i)
                    products = ((own_hi, side_hi), (own_lo, side_hi), (own_hi, side_lo), (head_sum, square_hi), (head_sum, square_lo))
                    for m, (w, x) in enumerate(products):
                        last = nc.tensor.matmul(to, w[:, :], x[:, a0:a1], start=(m == 0), stop=(m == 4))
                elif kind == "v_turn":
                    t0, t1 = v_groups[i]
                    for t in range(t0, t1):
                        last = nc.tensor.transpose(ps[0:R, held, (t - t0) * 128:(t - t0 + 1) * 128], v_rows[:, t * R:(t + 1) * R], ident[:, :])
                elif kind == "max":
                    t, c = divmod(i, 3)
                    b0, b1 = parts[c]
                    if i == 0:
                        pe.wait_ge(s["q_in"], head + 1)
                    keys = k_stack if h else k_next
                    if h == 0:
                        pe.wait_ge(s["k_next_in"], n * 3 + 3)
                    last = nc.tensor.matmul(ps[0:R, held, 0:b1 - b0], q_stack[:, h, t * R:(t + 1) * R], keys[:, b0:b1], start=True, stop=True)
                elif kind == "turn":
                    pe.wait_ge(s["max_ready"], head + 1)
                    last = nc.tensor.transpose(ps[0:tiles, held, 0:R], row_max[:, :], ident[0:R, 0:R])
                last.then_inc(s["side_ready"], 1)
                if kind == "w" and i == 2:
                    pe.sem_inc(s["raw_free"], 1)

            def one_pair(p, more):
                def mix(h, n):
                    half, t = divmod(n, tiles)
                    at = (p * 2 + h) * slots + n
                    if n == 0:
                        pe.wait_ge(s["v_in"], p * 2 + h + 1)
                    if t == 0:
                        pe.wait_ge(s["mixed_out"], p * 4 + 2 * h + half + 1)
                    pe.wait_ge(s["prob_hi_ready"], at + 1)
                    for m, (v, prb) in enumerate(((v_hi, prob_hi), (v_lo, prob_hi), (v_hi, prob_lo))):
                        if m == 2:
                            pe.wait_ge(s["prob_lo_ready"], at + 1)
                        for c in range(2):
                            last = nc.tensor.matmul(ps[0:depth + 1, 6 + c, 0:quarter], v[:, t, h, :],
                                                    prb[:, n % 3, c * quarter:(c + 1) * quarter],
                                                    start=(t == 0 and m == 0), stop=(t == tiles - 1 and m == 2),
                                                    skip_group_check=True)
                    last.then_inc(s["mix_step"], 1)

                for h in range(2):
                    head = p * 2 + h
                    pe.wait_ge(s["k_in"], p + 1)
                    pe.wait_ge(s["shift_in"], head * 32 + 32)

                    def logits(n):
                        half, t = divmod(n, tiles)
                        if n >= 2 or h == 1:
                            pe.wait_ge(s["prob_ready"], head * slots + n - 1)
                        for c in range(2):
                            at = (2 * half + c) * quarter
                            last = nc.tensor.matmul(ps[0:R, 2 + 2 * (n % 2) + c, 0:quarter], k_stack[:, t * R:(t + 1) * R],
                                                    q_stack[:, h, at:at + quarter], start=True, stop=True)
                        last.then_inc(s["logits_ready"], 1)

                    logits(0)
                    if h == 1:
                        mix(0, slots - 1)
                    for n in range(slots):
                        if n + 1 < slots:
                            logits(n + 1)
                        if n >= 1:
                            mix(h, n - 1)
                        for step in head_steps(h, more)[n]:
                            side(step, first_number(p), p + 1, head + 1, 1 - h, True)
                mix(1, slots - 1)

            pe.wait_ge(s["ready"], 4)
            for number, (kind, i) in enumerate(opening):
                side((number, kind, i), 0, 0, 0, 0, False)
            with pe.Fori(0, pairs - 1) as p:
                one_pair(p, True)
            one_pair(pairs - 1, False)

def combine(nc, x, attended, inverses, graph_w, graph_b, out_w, ident, kept, x_tiles, unit, unit_moments, eps):
    tiles, width = x_tiles.shape[1], x_tiles.shape[2]
    n_nodes = kept.shape[2]
    blocks = width // 128
    depth = attended.shape[1] - 1
    heads_n, cuts = attended.shape[0], 8
    early = 6
    with ExitStack() as ctx:
        sb, banks, sem = tools(nc, ctx, "combine")
        raw = sb("raw", [128, 2, width])
        w_hi = sb("w_hi", [128, 2, blocks, width], F32R)
        w_lo = sb("w_lo", [128, 2, blocks, width], F32R)
        offset = sb("offset", [R, width])
        heads = sb("heads", [128, 2, n_nodes])
        total = sb("total", [128, 2, n_nodes])
        part_hi = sb("part_hi", [128, 2 * blocks, n_nodes], F32R)
        part_lo = sb("part_lo", [128, 2 * blocks, n_nodes], F32R)
        sums = sb("sums", [heads_n * cuts, attended.shape[2] // cuts])
        inverse = sb("inverse", [heads_n * cuts, attended.shape[2] // cuts])
        ps = banks("ps", 8)
        stats = sb("stats", [R, 2, 6])
        moments = sb("moments", [R, tiles, 2])
        root = sb("root", [R, tiles])
        scale = sb("scale", [R, tiles])
        eps_col = sb("eps_col", [R, 1])
        names = "eps_in moments_ready root_ready step x_in offset_in sums_in inverse_ready inverse_stored raw_turned w_hi_ready w_lo_ready offset_added divided hi_ready lo_ready summed tile_out"
        s = {name: sem(name) for name in names.split()}
        raw_in = [sem("raw_in_0"), sem("raw_in_1")]
        heads_in = [sem("heads_in_0"), sem("heads_in_1")]
        block = ctx.enter_context(nc.Block())

        @block.sync
        def _(sp):
            for h in range(heads_n):
                sp.dma_start(sums[cuts * h:cuts * (h + 1), :], attended[h, depth, :].rearrange("(c n) -> c n", c=cuts)).then_inc(s["sums_in"], 16)
            for n in range(2 * blocks):
                w = (graph_w, out_w)[n // blocks]
                if n >= 2:
                    sp.wait_ge(s["raw_turned"], n - 1)
                sp.dma_start(raw[:, n % 2, :], w[n % blocks * 128:(n % blocks + 1) * 128, :]).then_inc(raw_in[n % 2], 16)
                if n == 0:
                    sp.dma_start(x_tiles[:, :, :], x.rearrange("(t p) n -> p t n", p=R)).then_inc(s["x_in"], 16)
                    sp.dma_start(offset[:, :], graph_b.partition_broadcast(R)).then_inc(s["offset_in"], 16)
                if n == blocks - 1:
                    sp.wait_ge(s["inverse_ready"], 1)
                    sp.dma_start(inverses.rearrange("h (c n) -> (h c) n", c=cuts), inverse[:, :]).then_inc(s["inverse_stored"], 16)

        @block.gpsimd
        def _(pool):
            def load_heads(k):
                for h in range(2):
                    rows = slice(depth * h, depth * (h + 1))
                    pool.dma_start(heads[rows, k % 2, :], attended[2 * k + h, 0:depth, 0:n_nodes]).then_inc(heads_in[k % 2], 16)
                pool.wait_ge(s["inverse_stored"], 16)
                for h in range(2):
                    rows = slice(depth * h, depth * (h + 1))
                    pool.dma_start(total[rows, k % 2, :],
                                   inverses[2 * k + h, 0:n_nodes].partition_broadcast(depth)).then_inc(heads_in[k % 2], 16)

            nc.gpsimd.memset(eps_col[:, :], eps).then_inc(s["eps_in"], 1)
            load_heads(0)
            load_heads(1)
            pool.wait_ge(s["x_in"], 16)
            pool.wait_ge(s["offset_in"], 16)
            for t in range(tiles):
                nc.gpsimd.tensor_tensor(x_tiles[:, t, :], x_tiles[:, t, :], offset[:, :], ALU.add).then_inc(s["offset_added"], 1)
            for k in range(2, blocks):
                pool.wait_ge(s["lo_ready"], blocks + k - 1)
                load_heads(k)

        @block.vector
        def _(dve):
            def w_low(n):
                dve.wait_ge(s["w_hi_ready"], n + 1)
                w, o = divmod(n, blocks)
                nc.vector.tensor_tensor(w_lo[:, w, :, o * 128:(o + 1) * 128], ps[:, n % 2, :].rearrange("p (k n) -> p k n", n=128),
                                        w_hi[:, w, :, o * 128:(o + 1) * 128].bitcast(F32), ALU.subtract).then_inc(s["w_lo_ready"], 1)

            for n in range(blocks):
                w_low(n)
            dve.wait_ge(s["sums_in"], 16 * heads_n)
            nc.vector.reciprocal(inverse[:, :], sums[:, :]).then_inc(s["inverse_ready"], 1)
            for k in range(blocks):
                dve.wait_ge(s["hi_ready"], k + 1)
                nc.vector.tensor_tensor(part_lo[:, k, :], kept[:, k, :], part_hi[:, k, :].bitcast(F32),
                                        ALU.subtract).then_inc(s["lo_ready"], 1)
            for n in range(blocks, 2 * blocks):
                w_low(n)
            for k in range(blocks):
                dve.wait_ge(heads_in[k % 2], 64 * (k // 2 + 1))
                nc.vector.tensor_tensor(heads[:, k % 2, :], heads[:, k % 2, :], total[:, k % 2, :], ALU.mult).then_inc(s["divided"], 1)
                dve.wait_ge(s["hi_ready"], blocks + k + 1)
                nc.vector.tensor_tensor(part_lo[:, blocks + k, :], heads[:, k % 2, :], part_hi[:, blocks + k, :].bitcast(F32),
                                        ALU.subtract).then_inc(s["lo_ready"], 1)
            dve.wait_ge(s["offset_added"], tiles)
            count = [0]

            def link(instruction):
                count[0] += 1
                instruction.then_inc(s["step"], 1)
                dve.wait_ge(s["step"], count[0])

            def finish_unit(t):
                dve.wait_ge(s["root_ready"], t + 1)
                link(nc.vector.reciprocal(scale[:, t:t + 1], root[:, t:t + 1]))
                link(nc.vector.tensor_scalar(unit[:, t, :], x_tiles[:, t, :], moments[:, t, 0:1], scale[:, t:t + 1],
                                             ALU.subtract, ALU.mult))
                link(nc.vector.bn_stats(stats[:, 1, :], unit[:, t, :]))
                link(nc.vector.bn_aggr(unit_moments[:, t, :], stats[:, 1, :]))

            for t in range(tiles):
                dve.wait_ge(s["summed"], t + 1)
                nc.vector.tensor_tensor(x_tiles[:, t, :], ps[0:R, 2 + t % early, :], x_tiles[:, t, :], ALU.add).then_inc(s["tile_out"], 1)
                dve.wait_ge(s["tile_out"], t + 1)
                link(nc.vector.bn_stats(stats[:, 0, :], x_tiles[:, t, :]))
                nc.vector.bn_aggr(moments[:, t, :], stats[:, 0, :]).then_inc(s["moments_ready"], 1)
                if t >= 1:
                    finish_unit(t - 1)
                dve.wait_ge(s["moments_ready"], t + 1)
            finish_unit(tiles - 1)

        @block.scalar
        def _(act):
            def w_high(n):
                act.wait_ge(s["raw_turned"], n + 1)
                w, o = divmod(n, blocks)
                nc.scalar.copy(w_hi[:, w, :, o * 128:(o + 1) * 128], ps[:, n % 2, :].rearrange("p (k n) -> p k n", n=128)).then_inc(s["w_hi_ready"], 1)

            for n in range(blocks):
                w_high(n)
            for k in range(blocks):
                nc.scalar.copy(part_hi[:, k, :], kept[:, k, :]).then_inc(s["hi_ready"], 1)
            for n in range(blocks, 2 * blocks):
                w_high(n)
            for k in range(blocks):
                act.wait_ge(s["divided"], k + 1)
                nc.scalar.copy(part_hi[:, blocks + k, :], heads[:, k % 2, :]).then_inc(s["hi_ready"], 1)
            act.wait_ge(s["eps_in"], 1)
            for t in range(tiles):
                act.wait_ge(s["moments_ready"], t + 1)
                nc.scalar.activation(root[:, t:t + 1], moments[:, t, 1:2], ACT.Sqrt, bias=eps_col[:, 0:1]).then_inc(s["root_ready"], 1)

        @block.tensor
        def _(pe):
            def turn(n):
                pe.wait_ge(raw_in[n % 2], 16 * (n // 2 + 1))
                if n >= 2:
                    pe.wait_ge(s["w_lo_ready"], n - 1)
                for k in range(blocks):
                    last = nc.tensor.transpose(ps[:, n % 2, k * 128:(k + 1) * 128], raw[:, n % 2, k * 128:(k + 1) * 128], ident[:, :])
                last.then_inc(s["raw_turned"], 1)

            def products(t, k):
                at = slice(t * R, (t + 1) * R)
                w, kk = divmod(k, blocks)
                for m, (left, right) in enumerate(((part_hi, w_hi), (part_hi, w_lo), (part_lo, w_hi))):
                    last = nc.tensor.matmul(ps[0:R, 2 + t % early, :], left[:, k, at], right[:, w, kk, :],
                                            start=(k == 0 and m == 0), stop=(k == 2 * blocks - 1 and m == 2))
                if k == 2 * blocks - 1:
                    last.then_inc(s["summed"], 1)

            for n in range(blocks):
                turn(n)
            pe.wait_ge(s["w_lo_ready"], blocks)
            for k in range(blocks):
                pe.wait_ge(s["lo_ready"], k + 1)
                for t in range(early):
                    products(t, k)
                if k == 1:
                    turn(blocks)
                    turn(blocks + 1)
                if k == blocks - 1:
                    for n in range(blocks + 2, 2 * blocks):
                        turn(n)
            pe.wait_ge(s["w_lo_ready"], 2 * blocks)
            for k in range(blocks, 2 * blocks):
                pe.wait_ge(s["lo_ready"], k + 1)
                for t in range(early):
                    products(t, k)
            for t in range(early, tiles):
                pe.wait_ge(s["tile_out"], t - early + 1)
                for k in range(2 * blocks):
                    products(t, k)


def normalise(nc, name, x_tiles, out_tiles, eps, gain=None, offset=None, residual=None, out=None):
    tiles, width = x_tiles.shape[1], x_tiles.shape[2]
    with ExitStack() as ctx:
        sb, banks, sem = tools(nc, ctx, name)
        stats = sb("stats", [R, 2, 6])
        moments = sb("moments", [R, tiles, 2])
        root = sb("root", [R, tiles])
        scale = sb("scale", [R, tiles])
        eps_col = sb("eps_col", [R, 1])
        rows = sb("rows", [R, 2, width])
        names = "eps_in rows_in stats_ready moments_ready root_ready scale_ready unit_ready gained shifted finished stored"
        s = {n: sem(n) for n in names.split()}
        block = ctx.enter_context(nc.Block())

        @block.sync
        def _(sp):
            if gain is not None:
                sp.dma_start(rows[:, 0, :], gain.partition_broadcast(R)).then_inc(s["rows_in"], 16)
                sp.dma_start(rows[:, 1, :], offset.partition_broadcast(R)).then_inc(s["rows_in"], 16)
                for t in range(tiles):
                    sp.wait_ge(s["finished"], t + 1)
                    sp.dma_start(out[t * R:(t + 1) * R, :], x_tiles[:, t, :]).then_inc(s["stored"], 16)
                sp.wait_ge(s["stored"], 16 * tiles)

        @block.gpsimd
        def _(pool):
            nc.gpsimd.memset(eps_col[:, :], eps).then_inc(s["eps_in"], 1)
            if gain is not None:
                pool.wait_ge(s["rows_in"], 32)
                for t in range(tiles):
                    pool.wait_ge(s["gained"], t + 1)
                    nc.gpsimd.tensor_tensor(x_tiles[:, t, :], out_tiles[:, t, :], rows[:, 1, :], ALU.add).then_inc(s["shifted"], 1)

        @block.vector
        def _(dve):
            for t in range(tiles):
                if t >= 2:
                    dve.wait_ge(s["moments_ready"], t - 1)
                nc.vector.bn_stats(stats[:, t % 2, :], x_tiles[:, t, :]).then_inc(s["stats_ready"], 1)
                dve.wait_ge(s["stats_ready"], t + 1)
                nc.vector.bn_aggr(moments[:, t, :], stats[:, t % 2, :]).then_inc(s["moments_ready"], 1)
            dve.wait_ge(s["root_ready"], 1)
            nc.vector.reciprocal(scale[:, :], root[:, :]).then_inc(s["scale_ready"], 1)
            dve.wait_ge(s["scale_ready"], 1)
            for t in range(tiles):
                nc.vector.tensor_scalar(out_tiles[:, t, :], x_tiles[:, t, :], moments[:, t, 0:1], scale[:, t:t + 1],
                                        ALU.subtract, ALU.mult).then_inc(s["unit_ready"], 1)
                if gain is not None:
                    dve.wait_ge(s["rows_in"], 32)
                    dve.wait_ge(s["unit_ready"], t + 1)
                    nc.vector.tensor_tensor(out_tiles[:, t, :], out_tiles[:, t, :], rows[:, 0, :], ALU.mult).then_inc(s["gained"], 1)
                    if t >= 1:
                        dve.wait_ge(s["shifted"], t)
                        nc.vector.tensor_tensor(x_tiles[:, t - 1, :], x_tiles[:, t - 1, :], residual[:, t - 1, :], ALU.add).then_inc(s["finished"], 1)
            if gain is not None:
                dve.wait_ge(s["shifted"], tiles)
                nc.vector.tensor_tensor(x_tiles[:, tiles - 1, :], x_tiles[:, tiles - 1, :], residual[:, tiles - 1, :], ALU.add).then_inc(s["finished"], 1)

        @block.scalar
        def _(act):
            act.wait_ge(s["moments_ready"], tiles)
            act.wait_ge(s["eps_in"], 1)
            nc.scalar.activation(root[:, :], moments[:, :, 1], ACT.Sqrt, bias=eps_col[:, 0:1]).then_inc(s["root_ready"], 1)


def gate(nc, x_hi, x_lo, w_gate, b2, ident, unit, share, mixed):
    tiles, experts = share.shape[1], share.shape[2]
    width = b2.shape[1]
    blocks = w_gate.shape[0] // 128
    with ExitStack() as ctx:
        sb, banks, sem = tools(nc, ctx, "gate")
        w = sb("w", [128, blocks, experts])
        w_hi = sb("w_hi", [128, blocks, experts], F32R)
        w_lo = sb("w_lo", [128, blocks, experts], F32R)
        bias = sb("bias", [experts, width])
        number = sb("number", [R, tiles, experts])
        logit = sb("logit", [R, tiles, experts])
        top_logit = sb("top_logit", [R, tiles])
        less = sb("less", [R, tiles, experts])
        exps = sb("exps", [R, tiles, experts])
        total = sb("total", [R, tiles])
        total_rec = sb("total_rec", [R, tiles])
        prob = sb("prob", [R, tiles, experts])
        best = sb("best", [R, tiles, 8])
        best_at = sb("best_at", [R, tiles, 8], mybir.dt.uint32)
        best_f = sb("best_f", [R, tiles, 8])
        pair_sum = sb("pair_sum", [R, tiles])
        pair_rec = sb("pair_rec", [R, tiles])
        conf = sb("conf", [R, tiles, 2])
        chosen = sb("chosen", [R, 2, tiles, experts])
        weighed = sb("weighed", [R, 2, tiles, experts])
        share_turn = sb("share_turn", [experts, tiles, R])
        ps = banks("ps", 5)
        names = "w_in bias_in numbers parted scored step less_ready exp_ready shared turned turn_out biased bias_out"
        s = {n: sem(n) for n in names.split()}
        block = ctx.enter_context(nc.Block())

        @block.sync
        def _(sp):
            sp.dma_start(w[:, :, :], w_gate.rearrange("(k p) e -> p k e", p=128)).then_inc(s["w_in"], 16)
            sp.dma_start(bias[:, :], b2).then_inc(s["bias_in"], 16)

        @block.gpsimd
        def _(pool):
            nc.gpsimd.iota(number[:, :, :], [[0, tiles], [1, experts]], base=0, channel_multiplier=0,
                           allow_small_or_imprecise_dtypes=True).then_inc(s["numbers"], 1)

        @block.scalar
        def _(act):
            act.wait_ge(s["less_ready"], 1)
            nc.scalar.activation(exps[:, :, :], less[:, :, :], ACT.Exp).then_inc(s["exp_ready"], 1)

        @block.vector
        def _(dve):
            count = [0]

            def link(instruction):
                count[0] += 1
                instruction.then_inc(s["step"], 1)
                dve.wait_ge(s["step"], count[0])

            def along(column):
                return column.unsqueeze(2).to_broadcast([R, tiles, experts])

            dve.wait_ge(s["w_in"], 16)
            link(nc.vector.tensor_copy(w_hi[:, :, :], w[:, :, :]))
            nc.vector.tensor_tensor(w_lo[:, :, :], w[:, :, :], w_hi[:, :, :].bitcast(F32), ALU.subtract).then_inc(s["parted"], 1)
            dve.wait_ge(s["scored"], 1)
            link(nc.vector.tensor_copy(logit[:, :, :], ps[0:R, 0, 0:tiles * experts].rearrange("p (t e) -> p t e", e=experts)))
            link(nc.vector.tensor_reduce(top_logit[:, :], logit[:, :, :], AX.X, ALU.max))
            nc.vector.tensor_tensor(less[:, :, :], logit[:, :, :], along(top_logit[:, :]), ALU.subtract).then_inc(s["less_ready"], 1)
            dve.wait_ge(s["exp_ready"], 1)
            link(nc.vector.tensor_reduce(total[:, :], exps[:, :, :], AX.X, ALU.add))
            link(nc.vector.reciprocal(total_rec[:, :], total[:, :]))
            link(nc.vector.tensor_tensor(prob[:, :, :], exps[:, :, :], along(total_rec[:, :]), ALU.mult))
            for t in range(tiles):
                last = nc.vector.max(best[:, t, :], prob[:, t, :])
            link(last)
            for t in range(tiles):
                last = nc.vector.max_index(best_at[:, t, :], best[:, t, :], prob[:, t, :])
            link(last)
            link(nc.vector.tensor_copy(best_f[:, :, :], best_at[:, :, :]))
            link(nc.vector.tensor_tensor(pair_sum[:, :], best[:, :, 0], best[:, :, 1], ALU.add))
            link(nc.vector.reciprocal(pair_rec[:, :], pair_sum[:, :]))
            dve.wait_ge(s["numbers"], 1)
            for n in range(2):
                link(nc.vector.tensor_tensor(conf[:, :, n], best[:, :, n], pair_rec[:, :], ALU.mult))
                link(nc.vector.tensor_tensor(chosen[:, n, :, :], number[:, :, :], along(best_f[:, :, n]), ALU.is_equal))
                link(nc.vector.tensor_tensor(weighed[:, n, :, :], chosen[:, n, :, :], along(conf[:, :, n]), ALU.mult))
            nc.vector.tensor_tensor(share[:, :, :], weighed[:, 0, :, :], weighed[:, 1, :, :], ALU.add).then_inc(s["shared"], 1)
            for t0 in range(0, tiles, 4):
                t1 = min(t0 + 4, tiles)
                dve.wait_ge(s["turned"], t0 // 4 + 1)
                nc.vector.tensor_copy(share_turn[:, t0:t1, :], ps[0:experts, 1 + t0 // 4 % 2, 0:(t1 - t0) * R].rearrange("p (t n) -> p t n", n=R)).then_inc(s["turn_out"], 1)
            for t in range(tiles):
                dve.wait_ge(s["biased"], t + 1)
                nc.vector.tensor_tensor(mixed[:, t, :], ps[0:R, 3 + t % 2, :], unit[:, t, :], ALU.add).then_inc(s["bias_out"], 1)

        @block.tensor
        def _(pe):
            pe.wait_ge(s["parted"], 1)
            for t in range(tiles):
                at = slice(t * R, (t + 1) * R)
                for k in range(blocks):
                    for m, (left, right) in enumerate(((x_hi, w_hi), (x_hi, w_lo), (x_lo, w_hi))):
                        last = nc.tensor.matmul(ps[0:R, 0, t * experts:(t + 1) * experts], left[:, k, at], right[:, k, :],
                                                start=(k == 0 and m == 0), stop=(k == blocks - 1 and m == 2))
            last.then_inc(s["scored"], 1)
            pe.wait_ge(s["shared"], 1)
            for t in range(tiles):
                if t == 8:
                    pe.wait_ge(s["turn_out"], 1)
                last = nc.tensor.transpose(ps[0:experts, 1 + t // 4 % 2, t % 4 * R:(t % 4 + 1) * R], share[:, t, :], ident[0:R, 0:R])
                if t % 4 == 3 or t == tiles - 1:
                    last.then_inc(s["turned"], 1)
            pe.wait_ge(s["turn_out"], (tiles + 3) // 4)
            pe.wait_ge(s["bias_in"], 16)
            for t in range(tiles):
                if t >= 2:
                    pe.wait_ge(s["bias_out"], t - 1)
                nc.tensor.matmul(ps[0:R, 3 + t % 2, :], share_turn[:, t, :], bias[:, :], start=True, stop=True).then_inc(s["biased"], 1)


def experts_mix(nc, x_hi, x_lo, w1, b1, w2, share, mixed):
    tiles = mixed.shape[1]
    n_nodes = x_hi.shape[2]
    experts, width, hidden = w1.shape
    k1, k2 = width // 128, hidden // 128
    chunks = spans(n_nodes, 500)
    with ExitStack() as ctx:
        sb, banks, sem = tools(nc, ctx, "experts")
        raw1 = sb("raw1", [128, k1, hidden])
        raw2 = sb("raw2", [128, k2, width])
        bias = sb("bias", [128, k2])
        w1_hi = sb("w1_hi", [128, k1, hidden], F32R)
        w1_lo = sb("w1_lo", [128, k1, hidden], F32R)
        w2_hi = sb("w2_hi", [128, k2, width], F32R)
        w2_lo = sb("w2_lo", [128, k2, width], F32R)
        act_f = sb("act_f", [128, k2, n_nodes])
        act_hi = sb("act_hi", [128, k2, n_nodes], F32R)
        act_lo = sb("act_lo", [128, k2, n_nodes], F32R)
        ps = banks("ps", 8)
        names = ("raw1_in raw2_in bias_in w1_hi_ready w1_lo_ready w2_hi_ready w2_lo_ready projected act_ready act_hi_ready "
                 "act_lo_ready output added")
        s = {n: sem(n) for n in names.split()}
        block = ctx.enter_context(nc.Block())
        parts = k2 * len(chunks)

        @block.sync
        def _(sp):
            for name, amount in (("w1_lo_ready", 1), ("w2_lo_ready", 1), ("act_ready", parts)):
                sp.sem_inc(s[name], amount)
            with sp.Fori(0, experts) as e:
                sp.wait_ge(s["w1_lo_ready"], e + 1)
                sp.dma_start(raw1[:, :, :], w1[bass.ds(e, 1), :, :].rearrange("a (k p) n -> p (a k) n", p=128)).then_inc(s["raw1_in"], 16)
                sp.wait_ge(s["w2_lo_ready"], e + 1)
                sp.dma_start(raw2[:, :, :], w2[bass.ds(e, 1), :, :].rearrange("a (k p) n -> p (a k) n", p=128)).then_inc(s["raw2_in"], 16)
                sp.wait_ge(s["act_ready"], e * parts + parts)
                sp.dma_start(bias[:, :], b1[bass.ds(e, 1), :].rearrange("a (k p) -> p (a k)", p=128),
                             allow_slow_non_contiguous=True).then_inc(s["bias_in"], 16)

        @block.vector
        def _(dve):
            def split_w1(e):
                dve.wait_ge(s["raw1_in"], e * 16 + 16)
                nc.vector.tensor_copy(w1_hi[:, :, :], raw1[:, :, :]).then_inc(s["w1_hi_ready"], 1)
                dve.wait_ge(s["w1_hi_ready"], e + 1)
                nc.vector.tensor_tensor(w1_lo[:, :, :], raw1[:, :, :], w1_hi[:, :, :].bitcast(F32), ALU.subtract).then_inc(s["w1_lo_ready"], 1)

            def expert(e, last):
                dve.wait_ge(s["raw2_in"], e * 16 + 16)
                nc.vector.tensor_copy(w2_hi[:, :, :], raw2[:, :, :]).then_inc(s["w2_hi_ready"], 1)
                dve.wait_ge(s["w2_hi_ready"], e + 1)
                nc.vector.tensor_tensor(w2_lo[:, :, :], raw2[:, :, :], w2_hi[:, :, :].bitcast(F32), ALU.subtract).then_inc(s["w2_lo_ready"], 1)
                for m in range(k2):
                    for c, (a, b) in enumerate(chunks):
                        n = m * len(chunks) + c
                        dve.wait_ge(s["act_ready"], e * parts + (parts + n + 1))
                        nc.vector.tensor_copy(act_hi[:, m, a:b], act_f[:, m, a:b]).then_inc(s["act_hi_ready"], 1)
                        dve.wait_ge(s["act_hi_ready"], e * parts + (n + 1))
                        nc.vector.tensor_tensor(act_lo[:, m, a:b], act_f[:, m, a:b], act_hi[:, m, a:b].bitcast(F32), ALU.subtract).then_inc(s["act_lo_ready"], 1)
                if not last:
                    split_w1(e + 1)
                for t in range(tiles):
                    dve.wait_ge(s["output"], e * tiles + (t + 1))
                    nc.vector.scalar_tensor_tensor(out=mixed[:, t, :], in0=ps[0:R, 6 + t % 2, :],
                                                   scalar=share[:, t, e:e + 1] if last else share[:, t, bass.ds(e, 1)],
                                                   in1=mixed[:, t, :], op0=ALU.mult, op1=ALU.add).then_inc(s["added"], 1)
                dve.wait_ge(s["added"], e * tiles + 2 * tiles)

            dve.sem_inc(s["added"], tiles)
            split_w1(0)
            with dve.Fori(0, experts - 1) as e:
                expert(e, last=False)
            expert(experts - 1, last=True)

        @block.scalar
        def _(act):
            act.sem_inc(s["act_lo_ready"], parts)
            with act.Fori(0, experts) as e:
                act.wait_ge(s["bias_in"], e * 16 + 16)
                for m in range(k2):
                    for c, (a, b) in enumerate(chunks):
                        n = m * len(chunks) + c
                        act.wait_ge(s["projected"], e * parts + (n + 1))
                        act.wait_ge(s["act_lo_ready"], e * parts + (n + 1))
                        nc.scalar.activation(act_f[:, m, a:b], ps[:, 3 * m + c, 0:b - a], ACT.Gelu_apprx_tanh,
                                             bias=bias[:, m:m + 1]).then_inc(s["act_ready"], 1)

        @block.tensor
        def _(pe):
            with pe.Fori(0, experts) as e:
                pe.wait_ge(s["w1_lo_ready"], e + 2)
                for m in range(k2):
                    for c, (a, b) in enumerate(chunks):
                        n = m * len(chunks) + c
                        pe.wait_ge(s["act_ready"], e * parts + (n + 1))
                        for k in range(k1):
                            for i, (w, x) in enumerate(((w1_hi, x_hi), (w1_hi, x_lo), (w1_lo, x_hi))):
                                last = nc.tensor.matmul(ps[:, n, 0:b - a], w[:, k, m * 128:(m + 1) * 128], x[:, k, a:b],
                                                        start=(k == 0 and i == 0), stop=(k == k1 - 1 and i == 2))
                        last.then_inc(s["projected"], 1)
                pe.wait_ge(s["w2_lo_ready"], e + 2)
                for t in range(tiles):
                    at = slice(t * R, (t + 1) * R)
                    chunk = [c for c, (a, b) in enumerate(chunks) if a <= t * R < b][0]
                    pe.wait_ge(s["act_lo_ready"], e * parts + (parts + (k2 - 1) * len(chunks) + chunk + 1))
                    pe.wait_ge(s["added"], e * tiles + (tiles + t - 1))
                    for k in range(k2):
                        for i, (h, w) in enumerate(((act_hi, w2_hi), (act_hi, w2_lo), (act_lo, w2_hi))):
                            last = nc.tensor.matmul(ps[0:R, 6 + t % 2, :], h[:, k, at], w[:, k, :],
                                                    start=(k == 0 and i == 0), stop=(k == k2 - 1 and i == 2))
                    last.then_inc(s["output"], 1)


def constants(nc, ident, zero_hot):
    with ExitStack() as ctx:
        sb, banks, sem = tools(nc, ctx, "constants")
        zeroed = sem("zeroed")
        block = ctx.enter_context(nc.Block())

        @block.gpsimd
        def _(pool):
            nc.gpsimd.memset(ident[:, :], 0.0).then_inc(zeroed, 1)
            nc.gpsimd.memset(zero_hot[:, :], 0.0)
            pool.wait_ge(zeroed, 1)
            nc.gpsimd.affine_select(out=ident[:, :], in_=ident[:, :], compare_op=ALU.not_equal, fill=1.0,
                                    base=0, pattern=[[-1, 128]], channel_multiplier=1)


def graph_transformer(nc, a, out):
    n_nodes, width = a["x"].shape
    tiles = n_nodes // R
    blocks = width // 128
    heads, _, depth = a["L0_mix_base_centers"].shape
    experts = a["L0_ffn_W1"].shape[0]
    padded = (n_nodes + 7) // 8 * 8
    eps = 1e-5
    attended = nc.dram_tensor("attended", (heads, depth + 1, padded), F32, kind="Internal").ap()
    inverses = nc.dram_tensor("inverses", (heads, padded), F32, kind="Internal").ap()
    mix = {k[len("L0_mix_"):]: v for k, v in a.items() if k.startswith("L0_mix_")}
    with ExitStack() as ctx:
        sb, banks, sem = tools(nc, ctx, "layer")
        ident = sb("ident", [128, 128])
        with ExitStack() as first:
            sb, banks, sem = tools(nc, first, "mixers")
            kept = sb("kept", [128, blocks, n_nodes])
            with ExitStack() as own:
                sb, banks, sem = tools(nc, own, "inputs")
                x_hi = sb("x_hi", [128, blocks, n_nodes], F32R)
                x_lo = sb("x_lo", [128, blocks, n_nodes], F32R)
                splat = [sb("center_hi", [128, heads // 2, 128], F32R), sb("center_lo", [128, heads // 2, 128], F32R),
                         sb("columns", [128, 4, heads // 2]), sb("part_mask", [128, 2]), sb("head_sum", [128, 128], F32R),
                         sb("inv_temp", [R, 1])]
                with ExitStack() as graph:
                    sb, banks, sem = tools(nc, graph, "edges")
                    zero_hot = sb("zero_hot", [R, 512], F16)
                    x_tiles = sb("x_tiles", [R, tiles, width])
                    adj = sb("adj", [R, tiles, n_nodes])
                    dinv = sb("dinv", [R, tiles])
                    x_in = sem("x_in")
                    constants(nc, ident, zero_hot)
                    splat_constants(nc, mix, ident, *splat, a["x"], x_tiles, x_in)
                    turn_normalised(nc, "norm1", x_tiles, ident, x_hi, x_lo, eps, rows_in=x_in)
                    adjacency(nc, a["src"], a["dst"], ident, zero_hot, adj, dinv)
                    graph_layers(nc, x_hi, x_lo, adj, dinv, [a[f"L0_gnn_W{n}"] for n in (1, 2, 3)],
                                 [a[f"L0_gnn_b{n}"] for n in (1, 2, 3)], kept)
                attention(nc, mix, *splat, ident, x_hi, x_lo, attended)
            second = ctx.enter_context(ExitStack())
            sb, banks, sem = tools(nc, first, "residual")
            x_new = sb("x_new", [R, tiles, width])
            unit = sb("unit", [R, tiles, width])
            unit_moments = sb("unit_moments", [R, tiles, 2])
            combine(nc, a["x"], attended, inverses, a["L0_gnn_W4"], a["L0_gnn_b4"], a["L0_mix_out_w"], ident, kept,
                    x_new, unit, unit_moments, eps)
            sb, banks, sem = tools(nc, first, "mixture")
            mixed = sb("mixed", [R, tiles, width])
            share = sb("share", [R, tiles, experts])
            f_hi = sb("f_hi", [128, blocks, n_nodes], F32R)
            f_lo = sb("f_lo", [128, blocks, n_nodes], F32R)
            turn_normalised(nc, "norm3", unit, ident, f_hi, f_lo, eps, a["L0_ffn_ln_g"], a["L0_ffn_ln_b"],
                            unit_moments)
            gate(nc, f_hi, f_lo, a["L0_ffn_Wg"], a["L0_ffn_b2"], ident, unit, share, mixed)
            experts_mix(nc, f_hi, f_lo, a["L0_ffn_W1"], a["L0_ffn_b1"], a["L0_ffn_W2"], share, mixed)
            normalise(nc, "norm4", mixed, unit, eps, a["L0_ffn_out_g"], a["L0_ffn_out_b"], x_new, out)


INPUTS = (["x", "src", "dst"] + [f"L0_gnn_{w}{n}" for n in (1, 2, 3, 4) for w in "Wb"]
          + ["L0_mix_" + n for n in ("base_centers", "center_deltas", "log_scales", "log_amps", "movement_scale_param",
                                     "temperature", "qkv_w", "out_w")]
          + ["L0_ffn_" + n for n in ("Wg", "W1", "b1", "W2", "b2", "ln_g", "ln_b", "out_g", "out_b")])


def kernel(**inputs):
    import numpy as np
    import concourse.bacc as bacc
    from concourse.bass_utils import run_bass_kernel_spmd as run

    nc = bacc.Bacc("TRN2", target_bir_lowering=False, num_devices=1)
    arrays = {f"in_{name}": np.ascontiguousarray(inputs[name]) for name in INPUTS}
    args = {name[3:]: nc.dram_tensor(name, v.shape, mybir.dt.from_np(v.dtype), kind="ExternalInput").ap()
            for name, v in arrays.items()}
    out = nc.dram_tensor("out_0", inputs["x"].shape, F32, kind="ExternalOutput").ap()
    graph_transformer(nc, args, out)
    return run(nc, [arrays], core_ids=[0]).results[0]["out_0"]
```
